# Optimizing a Trainium2 kernel written in Bass

```python
import numpy as np
import jax
import jax.numpy as jnp

def _softmax(x, axis=-1):
    return jax.nn.softmax(x, axis=axis)

def _gelu(x):
    return jax.nn.gelu(x, approximate=True)

def _silu(x):
    return jax.nn.silu(x)

def _sigmoid(x):
    return jax.nn.sigmoid(x)

def _layernorm(x, axis=-1, eps=1e-05):
    m = jnp.mean(x, axis=axis, keepdims=True)
    v = jnp.var(x, axis=axis, keepdims=True)
    return (x - m) / jnp.sqrt(v + eps)

def _scatter_add(tgt, idx, src, axis=0):
    return tgt.at[idx].add(src)

def _segment_sum(src, seg, n):
    return jax.ops.segment_sum(src, seg, n)
kernel_name = 'mk_sandwich_d2_jaxref_r8_40702d'

def setup_inputs(seed: int=0):
    np.random.seed(seed)
    _w = jnp.asarray

    def _L0_attn_setup():
        import jax, jax.numpy as jnp
        import numpy as np
        B, S, QD = (2, 512, 256)
        H, D = (32, 64)
        INNER = H * D
        key = jax.random.key(seed)
        ks = jax.random.split(key, 6)
        scale = 1.0 / np.sqrt(QD)
        return {'hidden_states': jax.random.normal(ks[0], (B, S, QD), dtype=jnp.float32), 'Wq': jax.random.normal(ks[1], (QD, INNER), dtype=jnp.float32) * scale, 'Wk': jax.random.normal(ks[2], (QD, INNER), dtype=jnp.float32) * scale, 'Wv': jax.random.normal(ks[3], (QD, INNER), dtype=jnp.float32) * scale, 'Wo': jax.random.normal(ks[4], (INNER, QD), dtype=jnp.float32) * (1.0 / np.sqrt(INNER)), 'bo': jax.random.normal(ks[5], (QD,), dtype=jnp.float32) * 0.01}
    _L0_attn_in = _L0_attn_setup()

    def _L0_ffn_setup():
        import jax, jax.numpy as jnp
        import numpy as np
        SEQ, BS, D, F, E = (128, 2, 256, 256, 8)
        key = jax.random.key(seed)
        ks = jax.random.split(key, 8)
        s = 0.02
        return {'hidden_states': jax.random.normal(ks[0], (SEQ, BS, D), jnp.float32), 'router_w': jax.random.normal(ks[1], (D, E), jnp.float32) * s, 'gate_w': jax.random.normal(ks[2], (E, D, F), jnp.float32) * s, 'up_w': jax.random.normal(ks[3], (E, D, F), jnp.float32) * s, 'down_w': jax.random.normal(ks[4], (E, F, D), jnp.float32) * s, 'shared_gate_w': jax.random.normal(ks[5], (D, F), jnp.float32) * s, 'shared_up_w': jax.random.normal(ks[6], (D, F), jnp.float32) * s, 'shared_down_w': jax.random.normal(ks[7], (F, D), jnp.float32) * s}
    _L0_ffn_in = _L0_ffn_setup()

    def _L1_attn_setup():
        import jax, jax.numpy as jnp
        import numpy as np
        D_MODEL = 256
        N_Q = 32
        N_KV = 8
        HEAD_DIM = D_MODEL // N_Q
        N_REP = N_Q // N_KV
        QKV_OUT = HEAD_DIM * (N_Q + 2 * N_KV)
        key = jax.random.key(seed)
        ks = jax.random.split(key, 6)
        s = 1.0 / np.sqrt(D_MODEL)
        x = jax.random.normal(ks[0], (2, 256, D_MODEL), dtype=jnp.float32)
        Wqkv = jax.random.normal(ks[1], (D_MODEL, QKV_OUT), dtype=jnp.float32) * s
        bqkv = jax.random.normal(ks[2], (QKV_OUT,), dtype=jnp.float32) * 0.02
        Wo = jax.random.normal(ks[3], (D_MODEL, D_MODEL), dtype=jnp.float32) * s
        bo = jax.random.normal(ks[4], (D_MODEL,), dtype=jnp.float32) * 0.02
        return {'x': x, 'Wqkv': Wqkv, 'bqkv': bqkv, 'Wo': Wo, 'bo': bo}
    _L1_attn_in = _L1_attn_setup()

    def _L1_ffn_setup():
        import jax, jax.numpy as jnp
        import numpy as np
        SEQ, BS, D, F, E = (128, 2, 256, 256, 8)
        key = jax.random.key(seed)
        ks = jax.random.split(key, 8)
        s = 0.02
        return {'hidden_states': jax.random.normal(ks[0], (SEQ, BS, D), jnp.float32), 'router_w': jax.random.normal(ks[1], (D, E), jnp.float32) * s, 'gate_w': jax.random.normal(ks[2], (E, D, F), jnp.float32) * s, 'up_w': jax.random.normal(ks[3], (E, D, F), jnp.float32) * s, 'down_w': jax.random.normal(ks[4], (E, F, D), jnp.float32) * s, 'shared_gate_w': jax.random.normal(ks[5], (D, F), jnp.float32) * s, 'shared_up_w': jax.random.normal(ks[6], (D, F), jnp.float32) * s, 'shared_down_w': jax.random.normal(ks[7], (F, D), jnp.float32) * s}
    _L1_ffn_in = _L1_ffn_setup()
    _d = {'L0_attn_hidden_states': _L0_attn_in['hidden_states'], 'L0_attn_Wq': _L0_attn_in['Wq'], 'L0_attn_Wk': _L0_attn_in['Wk'], 'L0_attn_Wv': _L0_attn_in['Wv'], 'L0_attn_Wo': _L0_attn_in['Wo'], 'L0_attn_bo': _L0_attn_in['bo'], 'L0_ffn_router_w': _L0_ffn_in['router_w'], 'L0_ffn_gate_w': _L0_ffn_in['gate_w'], 'L0_ffn_up_w': _L0_ffn_in['up_w'], 'L0_ffn_down_w': _L0_ffn_in['down_w'], 'L0_ffn_shared_gate_w': _L0_ffn_in['shared_gate_w'], 'L0_ffn_shared_up_w': _L0_ffn_in['shared_up_w'], 'L0_ffn_shared_down_w': _L0_ffn_in['shared_down_w'], 'L1_attn_Wqkv': _L1_attn_in['Wqkv'], 'L1_attn_bqkv': _L1_attn_in['bqkv'], 'L1_attn_Wo': _L1_attn_in['Wo'], 'L1_attn_bo': _L1_attn_in['bo'], 'L1_ffn_router_w': _L1_ffn_in['router_w'], 'L1_ffn_gate_w': _L1_ffn_in['gate_w'], 'L1_ffn_up_w': _L1_ffn_in['up_w'], 'L1_ffn_down_w': _L1_ffn_in['down_w'], 'L1_ffn_shared_gate_w': _L1_ffn_in['shared_gate_w'], 'L1_ffn_shared_up_w': _L1_ffn_in['shared_up_w'], 'L1_ffn_shared_down_w': _L1_ffn_in['shared_down_w']}
    _x0 = _d['L0_attn_hidden_states']
    _d['L0_attn_hidden_states'] = jax.random.normal(jax.random.fold_in(jax.random.key(seed), 1), (2, 512, 256), dtype=_x0.dtype)
    del _x0
    return _d

def reference(L0_attn_hidden_states, L0_attn_Wq, L0_attn_Wk, L0_attn_Wv, L0_attn_Wo, L0_attn_bo, L0_ffn_router_w, L0_ffn_gate_w, L0_ffn_up_w, L0_ffn_down_w, L0_ffn_shared_gate_w, L0_ffn_shared_up_w, L0_ffn_shared_down_w, L1_attn_Wqkv, L1_attn_bqkv, L1_attn_Wo, L1_attn_bo, L1_ffn_router_w, L1_ffn_gate_w, L1_ffn_up_w, L1_ffn_down_w, L1_ffn_shared_gate_w, L1_ffn_shared_up_w, L1_ffn_shared_down_w):

    def _L0_attn_ref(hidden_states, Wq, Wk, Wv, Wo, bo):
        import jax, jax.numpy as jnp
        import numpy as np
        B, S, QD = (2, 512, 256)
        H, D = (32, 64)
        INNER = H * D
        b, s, _ = hidden_states.shape

        def proj(W):
            return (hidden_states @ W).reshape(b, s, H, D).transpose(0, 2, 1, 3)
        q = jax.nn.relu(proj(Wq))
        k = jax.nn.relu(proj(Wk))
        v = proj(Wv)
        kv = jnp.einsum('bhsd,bhse->bhde', k, v)
        qkv = jnp.einsum('bhsd,bhde->bhse', q, kv)
        key_sum = k.sum(axis=2)
        normalizer = jnp.einsum('bhsd,bhd->bhs', q, key_sum)
        normalizer = jnp.clip(normalizer, 1e-06, None)[..., None]
        out = qkv / normalizer
        out = out.transpose(0, 2, 1, 3).reshape(b, s, INNER)
        return out @ Wo + bo

    def _L0_ffn_ref(hidden_states, router_w, gate_w, up_w, down_w, shared_gate_w, shared_up_w, shared_down_w):
        import jax, jax.numpy as jnp
        import numpy as np
        SEQ, BS, D, F, E = (128, 2, 256, 256, 8)
        S, B, Dm = hidden_states.shape
        x = hidden_states.reshape(-1, Dm)
        logits = x @ router_w
        expert_idx = jnp.argmax(logits, axis=-1)
        score = jax.nn.sigmoid(jnp.max(logits, axis=-1))
        xs = x * score[:, None]
        n_experts = router_w.shape[1]
        out = jnp.zeros_like(x)
        for e in range(n_experts):
            m = (expert_idx == e)[:, None]
            xe = jnp.where(m, xs, 0.0)
            h = jax.nn.silu(xe @ gate_w[e]) * (xe @ up_w[e])
            out = out + jnp.where(m, h @ down_w[e], 0.0)
        shared = jax.nn.silu(x @ shared_gate_w) * (x @ shared_up_w) @ shared_down_w
        return (out + shared).reshape(S, B, Dm)

    def _L1_attn_ref(x, Wqkv, bqkv, Wo, bo):
        import jax, jax.numpy as jnp
        import numpy as np
        D_MODEL = 256
        N_Q = 32
        N_KV = 8
        HEAD_DIM = D_MODEL // N_Q
        N_REP = N_Q // N_KV
        QKV_OUT = HEAD_DIM * (N_Q + 2 * N_KV)
        bsz, seqlen, _ = x.shape
        qkv = jnp.einsum('bsd,df->bsf', x, Wqkv) + bqkv
        q_end = HEAD_DIM * N_Q
        k_end = q_end + HEAD_DIM * N_KV
        q = qkv[..., :q_end].reshape(bsz, seqlen, N_Q, HEAD_DIM)
        k = qkv[..., q_end:k_end].reshape(bsz, seqlen, N_KV, HEAD_DIM)
        v = qkv[..., k_end:].reshape(bsz, seqlen, N_KV, HEAD_DIM)
        k = jnp.repeat(k, N_REP, axis=2)
        v = jnp.repeat(v, N_REP, axis=2)
        scores = jnp.einsum('bqhd,bkhd->bhqk', q, k) / np.sqrt(HEAD_DIM).astype(np.float32)
        attn = jax.nn.softmax(scores, axis=-1)
        out = jnp.einsum('bhqk,bkhd->bqhd', attn, v).reshape(bsz, seqlen, D_MODEL)
        return jnp.einsum('bsd,de->bse', out, Wo) + bo

    def _L1_ffn_ref(hidden_states, router_w, gate_w, up_w, down_w, shared_gate_w, shared_up_w, shared_down_w):
        import jax, jax.numpy as jnp
        import numpy as np
        SEQ, BS, D, F, E = (128, 2, 256, 256, 8)
        S, B, Dm = hidden_states.shape
        x = hidden_states.reshape(-1, Dm)
        logits = x @ router_w
        expert_idx = jnp.argmax(logits, axis=-1)
        score = jax.nn.sigmoid(jnp.max(logits, axis=-1))
        xs = x * score[:, None]
        n_experts = router_w.shape[1]
        out = jnp.zeros_like(x)
        for e in range(n_experts):
            m = (expert_idx == e)[:, None]
            xe = jnp.where(m, xs, 0.0)
            h = jax.nn.silu(xe @ gate_w[e]) * (xe @ up_w[e])
            out = out + jnp.where(m, h @ down_w[e], 0.0)
        shared = jax.nn.silu(x @ shared_gate_w) * (x @ shared_up_w) @ shared_down_w
        return (out + shared).reshape(S, B, Dm)
    x = L0_attn_hidden_states
    x = x + _layernorm(_L0_attn_ref(_layernorm(x, axis=-1), L0_attn_Wq, L0_attn_Wk, L0_attn_Wv, L0_attn_Wo, L0_attn_bo), axis=-1)
    x = x + _layernorm(_L0_ffn_ref(_layernorm(x, axis=-1), L0_ffn_router_w, L0_ffn_gate_w, L0_ffn_up_w, L0_ffn_down_w, L0_ffn_shared_gate_w, L0_ffn_shared_up_w, L0_ffn_shared_down_w), axis=-1)
    x = x + _layernorm(_L1_attn_ref(_layernorm(x, axis=-1), L1_attn_Wqkv, L1_attn_bqkv, L1_attn_Wo, L1_attn_bo), axis=-1)
    x = x + _layernorm(_L1_ffn_ref(_layernorm(x, axis=-1), L1_ffn_router_w, L1_ffn_gate_w, L1_ffn_up_w, L1_ffn_down_w, L1_ffn_shared_gate_w, L1_ffn_shared_up_w, L1_ffn_shared_down_w), axis=-1)
    return x

_drawn_inputs = setup_inputs


def setup_inputs(seed=0):
    import zlib

    import numpy as np

    out = dict(_drawn_inputs(seed))
    spreads = {}
    factors = {}
    for name, (base, spread) in spreads.items():
        noise = np.random.default_rng([zlib.crc32(name.encode()), seed]).standard_normal(out[name].shape)
        drawn = base * np.exp(spread * noise) if base else spread * noise
        out[name] = jnp.asarray(drawn.astype(out[name].dtype))
    for name, factor in factors.items():
        out[name] = (out[name] * factor).astype(out[name].dtype)
    return out
```

```python
from contextlib import ExitStack

import concourse.bass as bass
from concourse import mybir

F32 = mybir.dt.float32
F32R = mybir.dt.float32r
BF16 = mybir.dt.bfloat16
I32 = mybir.dt.int32
U32 = mybir.dt.uint32
ALU = mybir.AluOpType
ACT = mybir.ActivationFunctionType
AX = mybir.AxisListType

P = 128
B, S, D = 2, 512, 256
NT = B * S // P
TB = S // P
KC = D // P
EPS = 1e-5

INNER = 2048
SL = 512
NS = INNER // SL
CH = SL // P
HC = 64

E, F = 8, 256
FC = F // P
NR = NT + E - 1
NU = NT + NR

NQ, NKV, HD = 32, 8, 8
GH = NQ // NKV
QKV = HD * (NQ + 2 * NKV)
KEND = HD * (NQ + NKV)
HW = 64
MAXAT = 6 * HD
VW = 32
NG = B * NKV
SCALE = float(1.0 / HD ** 0.5)


def build(nc, a, out, phases=4):
    ctx = ExitStack()
    with ctx:
        def sem(name):
            return ctx.enter_context(nc.semaphore(name))

        arena_at = [0]
        names = {}

        def at(name, shape, dt, where):
            n = 1
            for d in shape[1:]:
                n *= d
            size = n * (2 if dt == BF16 else 4)
            t = nc.alloc_sbuf_tensor_at(name, shape, dt, offset=where[0])
            where[0] += (size + 31) // 32 * 32
            assert where[0] <= LIMIT, (name, where[0], LIMIT, here[0])
            return t

        base = nc.sbuf_base
        LIMIT = nc.sbuf_usable_end
        fence = ctx.enter_context(nc.sbuf_tensor("arena", [P, (LIMIT - base - 256) // 4], F32))
        here = [(base + 31) // 32 * 32]

        x = at("x", [P, NT, D], F32, here)
        in_xn = [here[0]]
        xn = at("xn", [P, NT, D], F32, here)
        in_xT = [here[0]]
        xT = at("xT", [P, KC, B * S], F32, here)
        in_y = [here[0]]
        y = at("y", [P, NT, D], F32, here)
        ident = at("ident", [P, P], F32, here)
        identb = at("identb", [P, P], BF16, here)
        ones = at("ones", [P, P], F32, here)
        onesb = at("onesb", [P, P], BF16, here)
        below = at("below", [P, P], BF16, here)
        same_head = at("same_head", [P, P], F32, here)
        pick_r = at("pick_r", [P, CH, P], F32R, here)
        up_to = at("up_to", [P, E, E], F32, here)
        rows_at = at("rows_at", [P, NT], F32, here)
        tile_no = at("tile_no", [P, 16], F32, here)
        rank_key = at("rank_key", [P, E], F32, here)
        mhalf = at("mhalf", [P, NT], F32, here)
        stat = at("stat", [P, NT, 6], F32, here)
        mv = at("mv", [P, NT, 2], F32, here)
        var = at("var", [P, NT], F32, here)
        rstd = at("rstd", [P, NT], F32, here)
        bo0 = at("bo0", [P, D], F32, here)
        bo1 = at("bo1", [P, D], F32, here)
        zeros = at("zeros", [P, D], F32, here)
        router = [at(f"router{l}", [P, KC, E], F32, here) for l in range(2)]
        shared_gu = at("shared_gu", [P, KC, 2 * F], F32, here)
        shared_d = at("shared_d", [P, FC, D], F32, here)

        l0 = [here[0]]
        xT_hi = at("xT_hi", [P, KC, B * S], F32R, in_xT)
        xT_lo = at("xT_lo", [P, KC, B * S], F32R, in_y)
        xn_hi = at("xn_hi", [P, NT, D], F32R, l0)
        xn_lo = at("xn_lo", [P, NT, D], F32R, l0)
        wk_f, wq_f, wv_f = (at(n, [P, KC, SL], F32, l0) for n in ("wk_f", "wq_f", "wv_f"))
        wo_f = at("wo_f", [P, CH, D], F32, l0)
        wk_hi, wk_lo, wq_hi, wq_lo = (at(n, [P, KC, SL], F32R, l0) for n in ("wk_hi", "wk_lo", "wq_hi", "wq_lo"))
        k_hi = [at(f"k_hi{b}", [P, TB, SL], F32R, l0) for b in range(B)]
        k_lo = [at(f"k_lo{b}", [P, TB, SL], F32R, l0) for b in range(B)]
        kx = at("kx", [P, KC, SL], F32, l0)
        q = [at(f"q{b}", [P, CH, SL], F32, l0) for b in range(B)]
        q_hi = [at(f"q_hi{b}", [P, CH, SL], F32R, l0) for b in range(B)]
        q_lo = [at(f"q_lo{b}", [P, CH, SL], F32R, l0) for b in range(B)]
        in_kv = [l0[0]]
        kv = [at(f"kv{b}", [P, CH, P], F32, l0) for b in range(B)]
        pick = at("pick", [P, CH, P], F32, in_kv)
        kvo_hi = [at(f"kvo_hi{b}", [P, CH, D], F32R, l0) for b in range(B)]
        kvo_lo = [at(f"kvo_lo{b}", [P, CH, D], F32R, l0) for b in range(B)]
        ksum = at("ksum", [P, SL], F32, in_xn)
        ksum_t = at("ksum_t", [P, 2, SL], F32, l0)
        nk = [at(f"nk{b}", [P, CH, 32], F32, l0) for b in range(B)]
        rec = at("rec", [P, SL], F32, in_xn)
        rec_hi = [at(f"rec_hi{b}", [P, SL], F32R, w) for b, w in enumerate((in_xn, l0))]
        rec_lo = [at(f"rec_lo{b}", [P, SL], F32R, w) for b, w in enumerate((in_xn, l0))]

        me = [here[0]]
        w_gu = at("w_gu", [P, E, KC, 2 * F], F32, me)
        w_d = at("w_d", [P, E, FC, D], F32, me)
        y_shared = at("y_shared", [P, NT, D], F32, me)
        xg = [at(f"xg{i}", [P, D], F32, me) for i in range(4)]
        xgT = [at(f"xgT{i}", [P, KC, P], F32, me) for i in range(2)]
        sg = [at(f"sg{i}", [P, F], F32, me) for i in range(2)]
        h = [at(f"h{i}", [P, F], F32, me) for i in range(2)]
        hT = [at(f"hT{i}", [P, FC, P], F32, me) for i in range(2)]
        yr = [at(f"yr{i}", [P, D], F32, me) for i in range(4)]
        lg = at("lg", [P, NT, E], F32, me)
        best = at("best", [P, NT], F32, me)
        score = at("score", [P, NT], F32, me)
        hot_f = at("hot_f", [P, NT, E], F32, me)
        hot = at("hot", [P, NT, E], BF16, me)
        last_max = at("last_max", [P, NT], F32, me)
        cnt = at("cnt", [P, E], F32, me)
        cmp = at("cmp", [P, E, E], F32, me)
        tiles_of = at("tiles_of", [P, E], F32, me)
        tiles_end = at("tiles_end", [P, E], F32, me)
        row0 = at("row0", [P, E], F32, me)
        place = at("place", [P, NT, E], F32, me)
        slot_f = at("slot_f", [P, NT], F32, me)
        slot = at("slot", [P, NT], U32, me)
        past = at("past", [P, 16, E], F32, me)
        expert_f = at("expert_f", [P, 16], F32, me)
        expert = at("expert", [P, 16], I32, me)

        l1 = [here[0]]
        bqkv = at("bqkv", [P, QKV], F32, l1)
        wqkv = at("wqkv", [P, KC, QKV], F32, l1)
        wo1 = at("wo1", [P, KC, D], F32, l1)
        qkv = at("qkv", [P, NT, QKV], F32, l1)
        part = [at(f"part{i}", [P, TB, KEND], BF16, l1) for i in range(3)]
        rest = [at(f"rest{i}", [P, TB, KEND], F32, l1) for i in range(2)]
        qs = [at(f"qs{b}", [P, TB, NQ, HW], BF16, l1) for b in range(B)]
        ks = at("ks", [P, TB, NKV, 2, P], BF16, l1)
        kT = [at(f"kT{b}", [P, NKV, 2, S], BF16, l1) for b in range(B)]
        vals = at("vals", [P, NT, NKV, VW], F32, l1)
        qT1 = at("qT1", [P, 2, S], BF16, l1)
        qT2 = at("qT2", [P, 2, S], BF16, l1)
        pr = [at(f"pr{i}", [P, GH, S], F32, l1) for i in range(2)]
        mx = at("mx", [P, TB, GH], F32, l1)
        mr = [at(f"mr{i}", [P, TB, GH], F32, l1) for i in range(2)]
        oT = at("oT", [P, S], F32, l1)
        dn = at("dn", [P, TB, GH], F32, l1)
        att = xn

        psum = ctx.enter_context(nc.psum_tensor("psum", [P, 8 * 512], F32))
        ps = [psum[:, i * 512:(i + 1) * 512] for i in range(8)]

        sorted_x = [nc.dram_tensor(f"sorted_x{l}", [NR * P, D], F32).ap() for l in range(2)]
        sorted_y = [nc.dram_tensor(f"sorted_y{l}", [NR * P, D], F32).ap() for l in range(2)]

        x_loaded = sem("x_loaded")
        small_loaded = sem("small_loaded")
        consts = sem("consts")
        const_casts = sem("const_casts")
        zeroed = sem("zeroed")
        var_ready, rstd_ready = sem("var_ready"), sem("rstd_ready")
        dve_chain = sem("dve_chain")
        xn_ready, xT_made, xT_ready = sem("xn_ready"), sem("xT_made"), sem("xT_ready")
        x_final = sem("x_final")
        stored = sem("stored")

        w_loaded = {n: sem(f"w_loaded_{n}") for n in ("k", "q", "v", "o")}
        w_hi_ready, w_lo_ready = ({n: sem(f"w_{p}_{n}") for n in "kq"} for p in ("hi", "lo"))
        split_hi, split_lo, xT_lo_ready = sem("split_hi"), sem("split_lo"), sem("xT_lo_ready")
        product = sem("product")
        act_done, dve_done = sem("act_done"), sem("dve_done")
        ksum_ready = sem("ksum_ready")
        rec_ready = sem("rec_ready")
        q_hi_ready, q_lo_ready = sem("q_hi_ready"), sem("q_lo_ready")
        out_done = sem("out_done")
        out_tiles = sem("out_tiles")
        y_ready = sem("y_ready")
        pool_chain = sem("pool_chain")
        act_chain = sem("act_chain")

        def trio(name):
            return [sem(f"{name}{l}") for l in range(2)]

        moe_w, shared_w = trio("moe_w"), trio("shared_w")
        logits_made, hot_ready, rank_made = trio("logits_made"), trio("hot_ready"), trio("rank_made")
        rank_read, logits_read = trio("rank_read"), trio("logits_read")
        slot_ready, expert_ready = trio("slot_ready"), trio("expert_ready")
        best_ready, score_ready, scaled = trio("best_ready"), trio("score_ready"), trio("scaled")
        scattered = trio("scattered")
        xg_loaded = [[sem(f"xg_loaded{l}_{i}") for i in range(4)] for l in range(2)]
        xgT_made, xgT_ready = trio("xgT_made"), trio("xgT_ready")
        gu_made, silu_ready, h_ready = trio("gu_made"), trio("silu_ready"), trio("h_ready")
        hT_made, hT_ready, d_made, yr_ready = trio("hT_made"), trio("hT_ready"), trio("d_made"), trio("yr_ready")
        yr_stored = [[sem(f"yr_stored{l}_{i}") for i in range(4)] for l in range(2)]
        gathered = trio("gathered")

        qkv_made, qkv_ready, stacks_ready, kT_made, kT_copied = (
            sem(n) for n in ("qkv_made", "qkv_ready", "stacks_ready", "kT_made", "kT_copied"))
        l1_consts, l1_loaded, part_ready = sem("l1_consts"), sem("l1_loaded"), sem("part_ready")
        turned, qT_ready = sem("turned"), sem("qT_ready")
        s1_made, max_read, max_ready = sem("s1_made"), sem("max_read"), sem("max_ready")
        s2_made, exp_ready = sem("s2_made"), sem("exp_ready")
        av_done, oT_ready, o_made, att_ready = sem("av_done"), sem("oT_ready"), sem("o_made"), sem("att_ready")
        attT_made, attT_ready, proj_made = sem("attT_made"), sem("attT_ready"), sem("proj_made")

        block = ctx.enter_context(nc.Block())

        def split_mm(o, lhs, rhs, start, stop, **kw):
            nc.tensor.matmul(o, lhs[0], rhs[0], start=start, stop=False, **kw)
            nc.tensor.matmul(o, lhs[0], rhs[1], start=False, stop=False, **kw)
            return nc.tensor.matmul(o, lhs[1], rhs[0], start=False, stop=stop, **kw)

        ORDER = [("K", b, t) for b in range(B) for t in range(TB)]
        ORDER += [("Q", 0, j) for j in range(CH)] + [("G", 0, c) for c in range(KC)] + [("S", 0, 0)]
        ORDER += [("KV", 0, 0)] + [("G", 1, c) for c in range(KC)] + [("N", 0, 0), ("S", 1, 0)]
        ORDER += [("Q", 1, j) for j in range(CH)] + [("N", 1, 0), ("KV", 1, 0)]
        ORDER += [("BC", 0, 0), ("KVO", 0, 0), ("BC", 0, 1), ("KVO", 0, 1), ("BC", 0, 2), ("KVO", 1, 0),
                  ("BC", 0, 3), ("KVO", 1, 1)]
        ORDER += [("BC", 1, j) for j in range(CH)]
        NP_ = len(ORDER)
        BY_ACT = [n for n in ORDER if n[0] in ("K", "G", "Q", "KVO")]
        BY_DVE = [n for n in ORDER if n[0] in ("K", "S", "KV", "N", "KVO", "BC")]
        BANKS = 4

        def made(s, n):
            return s * NP_ + ORDER.index(n) + 1

        def act_through(s, n):
            return s * len(BY_ACT) + BY_ACT.index(n) + 1

        def dve_through(s, n):
            return s * len(BY_DVE) + BY_DVE.index(n) + 1

        def bank(n):
            return ps[ORDER.index(n) % BANKS]

        acc = [[ps[4 + 2 * b + i] for i in range(2)] for b in range(B)]

        NORMS = 8

        def load(eng, dst, src, s):
            return eng.dma_start(dst, src).then_inc(s, 16)

        def sync_program(sp):
            xv = a["L0_attn_hidden_states"].rearrange("b (t p) d -> p (b t) d", p=P)
            for half in range(2):
                load(sp, x[:, half * TB:(half + 1) * TB, :], xv[:, half * TB:(half + 1) * TB, :], x_loaded)
            cols = {n: a[f"L0_attn_W{n}"].rearrange("(c p) n -> p c n", p=P) for n in "kqv"}
            rows = a["L0_attn_Wo"].rearrange("(j p) n -> p j n", p=P)
            stage = {"k": wk_f, "q": wq_f, "v": wv_f, "o": wo_f}
            for s in range(NS):
                if s:
                    sp.wait_ge(w_hi_ready["k"], s)
                    sp.wait_ge(w_lo_ready["k"], s)
                load(sp, stage["k"][:], cols["k"][:, :, s * SL:(s + 1) * SL], w_loaded["k"])
                if s:
                    sp.wait_ge(w_hi_ready["q"], s)
                    sp.wait_ge(w_lo_ready["q"], s)
                load(sp, stage["q"][:], cols["q"][:, :, s * SL:(s + 1) * SL], w_loaded["q"])
                if s:
                    sp.wait_ge(product, made(s - 1, ("KV", 1, 0)))
                load(sp, stage["v"][:], cols["v"][:, :, s * SL:(s + 1) * SL], w_loaded["v"])
                if s:
                    sp.wait_ge(product, made(s - 1, ("KVO", 1, 1)))
                load(sp, stage["o"][:], rows[:, s * CH:(s + 1) * CH, :], w_loaded["o"])
                if s == 0:
                    small_loads(sp)
            for p in range(1, phases):
                if p == 2:
                    sp.wait_ge(y_ready, 2 * NT)
                    load(sp, wqkv[:], a["L1_attn_Wqkv"].rearrange("(c p) n -> p c n", p=P), l1_loaded)
                    load(sp, bqkv[:], a["L1_attn_bqkv"].partition_broadcast(P), l1_loaded)
                    load(sp, wo1[:], a["L1_attn_Wo"].rearrange("(c p) n -> p c n", p=P), l1_loaded)
                else:
                    sp_moe(sp, p // 2)
            for t in range(NT):
                sp.wait_ge(x_final, t + 1)
                sp.dma_start(out.rearrange("b (t p) d -> p (b t) d", p=P)[:, t, :], x[:, t, :]).then_inc(stored, 16)
            sp.wait_ge(stored, 16 * NT)

        def small_loads(sp):
            for dst, name in ((bo0, "L0_attn_bo"), (bo1, "L1_attn_bo")):
                load(sp, dst[:], a[name].partition_broadcast(P), small_loaded)
            for l in range(2):
                load(sp, router[l][:], a[f"L{l}_ffn_router_w"].rearrange("(c p) n -> p c n", p=P), small_loaded)
            sp.wait_ge(consts, N_CONSTS)
            for l in range(2):
                for i in range(NR):
                    load(sp, sorted_x[l][i * P:(i + 1) * P, :], zeros[:], zeroed)

        SMALL = 16 * 4

        def shared_loads(sp, l):
            pre = f"L{l}_ffn_"
            if l:
                sp.wait_ge(gu_made[0], NT)
                sp.wait_ge(d_made[0], NT)
            for i, n in enumerate(("gate", "up")):
                load(sp, shared_gu[:, :, i * F:(i + 1) * F], a[f"{pre}shared_{n}_w"].rearrange("(c p) f -> p c f", p=P),
                     shared_w[l])
            load(sp, shared_d[:], a[f"{pre}shared_down_w"].rearrange("(c p) f -> p c f", p=P), shared_w[l])

        def sp_moe(sp, l):
            pre = f"L{l}_ffn_"
            shared_loads(sp, l)
            sp.wait_ge(y_ready, (2 * l + 1) * NT)
            for e in range(E):
                for i, n in enumerate(("gate", "up")):
                    load(sp, w_gu[:, e, :, i * F:(i + 1) * F], a[f"{pre}{n}_w"][e].rearrange("(c p) f -> p c f", p=P),
                         moe_w[l])
                load(sp, w_d[:, e], a[f"{pre}down_w"][e].rearrange("(c p) f -> p c f", p=P), moe_w[l])
            sp.wait_ge(scattered[l], 16 * NT)

            def fetch(r):
                if r >= 4:
                    sp.wait_ge(xgT_made[l], r - 3)
                load(sp, xg[r % 4][:], sorted_x[l][r * P:(r + 1) * P, :], xg_loaded[l][r % 4])

            for r in range(NR + 4):
                if r < NR:
                    fetch(r)
                if r >= 4:
                    sp.wait_ge(yr_ready[l], NT + r - 3)
                    load(sp, sorted_y[l][(r - 4) * P:(r - 3) * P, :], yr[r % 4][:], yr_stored[l][r % 4])

        N_CONSTS = 11

        def gpsimd_program(pool):
            g = nc.gpsimd
            count = [0]

            def link(ins):
                count[0] += 1
                ins.then_inc(pool_chain, 1)
                pool.wait_ge(pool_chain, count[0])

            g.memset(zeros[:], 0.0).then_inc(consts, 1)
            g.memset(ones[:], 1.0).then_inc(consts, 1)
            g.memset(mhalf[:], -0.5).then_inc(consts, 1)
            link(g.memset(ident[:], 0.0))
            g.affine_select(out=ident[:], in_=ident[:], compare_op=ALU.not_equal, fill=1.0, base=0,
                            pattern=[[-1, P]], channel_multiplier=1).then_inc(consts, 1)
            for n in range(2):
                pool_rstd(pool, n)
            link(g.memset(below[:], 1.0))
            g.affine_select(out=below[:], in_=below[:], compare_op=ALU.is_gt, fill=0.0, base=0,
                            pattern=[[1, P]], channel_multiplier=-1).then_inc(consts, 1)
            link(g.memset(pick[:], 0.0))
            g.affine_select(out=pick[:], in_=pick[:], compare_op=ALU.not_equal, fill=1.0, base=0,
                            pattern=[[-32, CH], [-1, 2], [0, P // 2]], channel_multiplier=1).then_inc(consts, 1)
            link(g.memset(up_to[:], 1.0))
            g.affine_select(out=up_to[:], in_=up_to[:], compare_op=ALU.is_ge, fill=0.0, base=0,
                            pattern=[[1, E], [-1, E]], channel_multiplier=0).then_inc(consts, 1)
            kw = dict(channel_multiplier=0, allow_small_or_imprecise_dtypes=True)
            g.iota(rows_at[:], pattern=[[P, NT]], base=0, **kw).then_inc(consts, 1)
            g.iota(tile_no[:], pattern=[[1, 16]], base=0, **kw).then_inc(consts, 1)
            g.iota(rank_key[:], pattern=[[-1, E]], base=E, **kw).then_inc(consts, 1)
            g.memset(onesb[:], 1.0).then_inc(consts, 1)
            pool_l0(pool, link)
            for p in range(1, phases):
                if p == 2:
                    pool_l1(pool, link)
                for n in range(4 * p - 2, 4 * p + 2):
                    pool_rstd(pool, n)
                if p != 2:
                    pool_moe(pool, p // 2)
            for n in range(4 * phases - 2, 4 * phases):
                pool_rstd(pool, n)

        def pool_rstd(pool, n):
            half = slice((n % 2) * TB, (n % 2 + 1) * TB)
            pool.wait_ge(consts, 3)
            pool.wait_ge(var_ready, n + 1)
            nc.gpsimd.tensor_tensor(rstd[:, half], var[:, half], mhalf[:, half], ALU.pow).then_inc(rstd_ready, 1)

        def pool_l1(pool, link):
            g = nc.gpsimd
            pool.wait_ge(y_ready, 2 * NT)
            g.memset(vals[:], 0.0).then_inc(l1_consts, 1)
            g.memset(ks[:].bitcast(F32), 0.0).then_inc(l1_consts, 1)
            for b in range(B):
                g.memset(qs[b][:, :, :, MAXAT:HW].bitcast(F32), 0.0).then_inc(l1_consts, 1)
            pool.wait_ge(l1_consts, 4)
            g.memset(vals[:, :, :, HD:HD + 1], 1.0).then_inc(l1_consts, 1)
            for ver in range(2):
                at_ = ver * HW + MAXAT
                g.memset(ks[:, :, :, ver, at_:at_ + 3], 1.0).then_inc(l1_consts, 1)

        def pool_l0(pool, link):
            g = nc.gpsimd
            stage = {"k": (wk_f, wk_hi, wk_lo), "q": (wq_f, wq_hi, wq_lo)}

            def weight_lo(n, s):
                full, hi, lo = stage[n]
                if s:
                    pool.wait_ge(product, made(s - 1, (n.upper(), 1, TB - 1)))
                pool.wait_ge(w_hi_ready[n], s + 1)
                g.tensor_tensor(lo[:], full[:], hi[:].bitcast(F32), ALU.subtract).then_inc(w_lo_ready[n], 1)

            weight_lo("k", 0)
            for half in range(2):
                sl = slice(half * TB, (half + 1) * TB)
                pool.wait_ge(split_hi, half + 1)
                g.tensor_tensor(xn_lo[:, sl], xn[:, sl], xn_hi[:, sl].bitcast(F32), ALU.subtract).then_inc(split_lo, 1)
            weight_lo("q", 0)
            for s in range(NS):
                for b in range(B):
                    pool.wait_ge(dve_done, dve_through(s, ("K", b, TB - 1)))
                    hi, lo = k_hi[b][:].bitcast(F32), k_lo[b][:].bitcast(F32)
                    if s or b:
                        pool.wait_ge(product, made(s, ("S", 0, 0)) if b else made(s - 1, ("S", 1, 0)))
                    link(g.tensor_tensor(ksum_t[:], hi[:, 0:2], hi[:, 2:4], ALU.add))
                    link(g.tensor_tensor(rest_of(lo)[0], lo[:, 0], lo[:, 1], ALU.add))
                    link(g.tensor_tensor(ksum_t[:, 1], ksum_t[:, 0], ksum_t[:, 1], ALU.add))
                    link(g.tensor_tensor(ksum_t[:, 0], lo[:, 2], lo[:, 3], ALU.add))
                    link(g.tensor_tensor(ksum_t[:, 0], ksum_t[:, 0], ksum[:], ALU.add))
                    g.tensor_tensor(ksum[:], ksum_t[:, 0], ksum_t[:, 1], ALU.add).then_inc(ksum_ready, 1)
                if s + 1 < NS:
                    weight_lo("k", s + 1)
                    weight_lo("q", s + 1)

        def rest_of(_):
            return [ksum[:]]

        def pool_moe(pool, l):
            g = nc.gpsimd
            pool.wait_ge(zeroed, 16 * 2 * NR)
            pool.wait_ge(slot_ready[l], 1)
            for t in range(NT):
                pool.wait_ge(scaled[l], t + 1)
                g.indirect_dma_start(sorted_x[l][:, :], bass.IndirectOffsetOnAxis(ap=slot[:, t:t + 1], axis=0),
                                     xn[:, t, :], None).then_inc(scattered[l], 16)
            for i in range(4):
                n = len([r for r in range(NR) if r % 4 == i])
                pool.wait_ge(yr_stored[l][i], 16 * n)
            for t in range(NT):
                g.indirect_dma_start(y[:, t, :], None, sorted_y[l][:, :],
                                     bass.IndirectOffsetOnAxis(ap=slot[:, t:t + 1], axis=0)).then_inc(gathered[l], 16)

        def vector_program(dve):
            v = nc.vector
            count = [0]

            def link(ins):
                count[0] += 1
                ins.then_inc(dve_chain, 1)
                dve.wait_ge(dve_chain, count[0])

            def mark(ins):
                count[0] += 1
                ins.then_inc(dve_chain, 1)

            def settle():
                dve.wait_ge(dve_chain, count[0])

            dve.wait_ge(consts, 4)
            v.tensor_copy(identb[:], ident[:]).then_inc(const_casts, 1)
            for i in range(2):
                for j in range(2):
                    v.memset(same_head[i * HC:(i + 1) * HC, j * HC:(j + 1) * HC], float(i == j)).then_inc(const_casts, 1)

            def variances(src, n, ready=None):
                for half in range(2):
                    if n > 0 or half > 0:
                        settle()
                    for t in range(half * TB, (half + 1) * TB):
                        if ready:
                            ready(t)
                        mark(v.bn_stats(stat[:, t, :], src[:, t, :]))
                    settle()
                    for t in range(half * TB, (half + 1) * TB):
                        mark(v.bn_aggr(mv[:, t, :], stat[:, t, :]))
                    settle()
                    sl = slice(half * TB, (half + 1) * TB)
                    v.tensor_scalar(var[:, sl], mv[:, sl, 1], EPS, None, ALU.add).then_inc(var_ready, 1)

            def normalise(p):
                for t in range(NT):
                    if t % TB == 0:
                        dve.wait_ge(rstd_ready, 4 * p + t // TB + 1)
                    v.tensor_scalar(xn[:, t, :], x[:, t, :], mv[:, t, 0:1], rstd[:, t:t + 1],
                                    ALU.subtract, ALU.mult).then_inc(xn_ready, 1)

            def residual(p):
                variances(y, 2 * p + 1)
                for t in range(NT):
                    if t % TB == 0:
                        dve.wait_ge(rstd_ready, 4 * p + 2 + t // TB + 1)
                    mark(v.tensor_scalar(y[:, t, :], y[:, t, :], mv[:, t, 0:1], rstd[:, t:t + 1],
                                         ALU.subtract, ALU.mult))
                settle()
                for t in range(NT):
                    ins = v.tensor_tensor(x[:, t, :], x[:, t, :], y[:, t, :], ALU.add)
                    if p == phases - 1:
                        ins.then_inc(x_final, 1)
                    else:
                        mark(ins)

            def turn_lo(i):
                dve.wait_ge(xT_ready, i + 1)
                cols = slice(i * 256, (i + 1) * 256)
                v.tensor_tensor(xT_lo[:, :, cols], ps[i][:].rearrange("p (c n) -> p c n", c=KC),
                                xT_hi[:, :, cols].bitcast(F32), ALU.subtract).then_inc(xT_lo_ready, 1)

            def load_wait(t):
                if t % TB == 0:
                    dve.wait_ge(x_loaded, 32)

            variances(x, 0, load_wait)
            normalise(0)
            for half in range(2):
                dve.wait_ge(xn_ready, (half + 1) * TB)
                sl = slice(half * TB, (half + 1) * TB)
                v.tensor_copy(xn_hi[:, sl], xn[:, sl]).then_inc(split_hi, 1)
            for i in range(4):
                turn_lo(i)
            dve.wait_ge(consts, N_CONSTS)
            v.tensor_copy(pick_r[:], pick[:]).then_inc(const_casts, 1)
            for b in range(B):
                v.memset(nk[b][:], 0.0).then_inc(const_casts, 1)
            dve.wait_ge(const_casts, 8)
            for s in range(NS):
                dve_slice(dve, link, s)
            dve.wait_ge(out_done, B)
            dve.wait_ge(small_loaded, SMALL)
            for t in range(NT):
                v.tensor_tensor(y[:, t, :], acc[t // TB][t % TB // 2][:, t % 2 * D:(t % 2 + 1) * D], bo0[:],
                                ALU.add).then_inc(y_ready, 1)
            dve.wait_ge(y_ready, NT)
            residual(0)
            for p in range(1, phases):
                settle()
                variances(x, 2 * p)
                normalise(p)
                if p == 2:
                    dve_l1(dve, link, mark, settle)
                else:
                    dve_moe(dve, link, p // 2)
                residual(p)

        def dve_slice(dve, link, s):
            v = nc.vector

            def q_low(b, j):
                dve.wait_ge(q_hi_ready, (s * B + b) * CH + j + 1)
                v.tensor_tensor(q_lo[b][:, j], q[b][:, j], q_hi[b][:, j].bitcast(F32), ALU.subtract).then_inc(q_lo_ready, 1)

            for n in ORDER:
                kind, b, i = n
                if n not in BY_DVE:
                    continue
                pt = bank(n)
                if kind in ("K", "KVO"):
                    dve.wait_ge(act_done, act_through(s, n))
                else:
                    dve.wait_ge(product, made(s, n))
                if kind == "K":
                    if s:
                        dve.wait_ge(ksum_ready, (s - 1) * B + b + 1)
                    ins = v.scalar_tensor_tensor(k_lo[b][:, i], pt[:], 0.0, k_hi[b][:, i].bitcast(F32),
                                                 ALU.max, ALU.subtract)
                elif kind == "S":
                    ins = v.tensor_tensor(nk[b][:, :, 0:2], pt[:].rearrange("p (j m) -> p j m", j=CH)[:, :, 0:2],
                                          same_head[:, 0:P:HC].unsqueeze(1).to_broadcast([P, CH, 2]), ALU.mult)
                elif kind == "KV":
                    ins = v.tensor_tensor(kv[b][:], pt[:].rearrange("p (j m) -> p j m", j=CH),
                                          same_head[:].unsqueeze(1).to_broadcast([P, CH, P]), ALU.mult)
                elif kind == "N":
                    v.tensor_scalar(rec[:], pt[:], 1e-6, None, ALU.max).then_inc(dve_done, 1)
                    dve.wait_ge(dve_done, dve_through(s, n))
                    link(v.reciprocal(rec[:], rec[:]))
                    link(v.tensor_copy(rec_hi[b][:], rec[:]))
                    v.tensor_tensor(rec_lo[b][:], rec[:], rec_hi[b][:].bitcast(F32),
                                    ALU.subtract).then_inc(rec_ready, 1)
                    continue
                elif kind == "KVO":
                    ins = v.tensor_tensor(kvo_lo[b][:, 2 * i:2 * i + 2], pt[:].rearrange("p (j m) -> p j m", j=2),
                                          kvo_hi[b][:, 2 * i:2 * i + 2].bitcast(F32), ALU.subtract)
                else:
                    ins = v.tensor_tensor(q[b][:, i], q[b][:, i], pt[:], ALU.mult)
                ins.then_inc(dve_done, 1)
                if kind == "BC":
                    if i:
                        q_low(b, i - 1)
                    if i == CH - 1:
                        q_low(b, i)

        def dve_moe(dve, link, l):
            v = nc.vector
            dve.wait_ge(logits_made[l], 1)
            v.tensor_copy(lg[:], ps[6][:, 0:NT * E].rearrange("p (t e) -> p t e", e=E)).then_inc(logits_read[l], 1)
            dve.wait_ge(logits_read[l], 1)
            v.tensor_reduce(best[:], lg[:], AX.X, ALU.max).then_inc(best_ready[l], 1)
            dve.wait_ge(best_ready[l], 1)
            link(v.tensor_tensor(hot_f[:], lg[:], best[:].unsqueeze(2).to_broadcast([P, NT, E]), ALU.is_ge))
            link(v.tensor_tensor(hot_f[:], hot_f[:], rank_key[:].unsqueeze(1).to_broadcast([P, NT, E]), ALU.mult))
            link(v.tensor_reduce(last_max[:], hot_f[:], AX.X, ALU.max))
            link(v.tensor_tensor(hot_f[:], hot_f[:], last_max[:].unsqueeze(2).to_broadcast([P, NT, E]), ALU.is_equal))
            v.tensor_copy(hot[:], hot_f[:]).then_inc(hot_ready[l], 1)
            dve.wait_ge(score_ready[l], 1)
            for t in range(NT):
                v.tensor_scalar(xn[:, t, :], xn[:, t, :], score[:, t:t + 1], None, ALU.mult).then_inc(scaled[l], 1)
            dve.wait_ge(rank_made[l], 1)
            counts = ps[7][:, NT * E:(NT + 1) * E]
            link(v.tensor_copy(place[:], ps[7][:, 0:NT * E].rearrange("p (t e) -> p t e", e=E)))
            v.tensor_copy(cnt[:], counts).then_inc(rank_read[l], 1)
            dve.wait_ge(rank_read[l], 1)
            link(v.tensor_tensor(cmp[:], cnt[:].unsqueeze(2).to_broadcast([P, E, NT]),
                                 rows_at[:].unsqueeze(1).to_broadcast([P, E, NT]), ALU.is_gt))
            link(v.tensor_reduce(tiles_of[:], cmp[:], AX.X, ALU.add))
            link(v.tensor_tensor(cmp[:], up_to[:], tiles_of[:].unsqueeze(1).to_broadcast([P, E, E]), ALU.mult))
            link(v.tensor_reduce(tiles_end[:], cmp[:], AX.X, ALU.add))
            link(v.tensor_tensor(row0[:], tiles_end[:], tiles_of[:], ALU.subtract))
            link(v.tensor_scalar(row0[:], row0[:], float(P), None, ALU.mult))
            link(v.tensor_tensor(place[:], place[:], row0[:].unsqueeze(1).to_broadcast([P, NT, E]), ALU.add))
            link(v.tensor_tensor(place[:], place[:], hot_f[:], ALU.mult))
            link(v.tensor_reduce(slot_f[:], place[:], AX.X, ALU.add))
            v.tensor_copy(slot[:], slot_f[:]).then_inc(slot_ready[l], 1)
            link(v.tensor_tensor(past[:], tile_no[:].unsqueeze(2).to_broadcast([P, 16, E]),
                                 tiles_end[:].unsqueeze(1).to_broadcast([P, 16, E]), ALU.is_ge))
            link(v.tensor_reduce(expert_f[:], past[:], AX.X, ALU.add))
            link(v.tensor_scalar(expert_f[:], expert_f[:], float(E - 1), None, ALU.min))
            v.tensor_copy(expert[:], expert_f[:]).then_inc(expert_ready[l], 1)
            for i in range(NU + 2):
                if i < NU:
                    dve.wait_ge(silu_ready[l], i + 1)
                    if i >= 2:
                        dve.wait_ge(hT_made[l], i - 1)
                    v.tensor_tensor(h[i % 2][:], sg[i % 2][:], ps[2 + i % 2][:, F:2 * F], ALU.mult).then_inc(h_ready[l], 1)
                if i >= 2:
                    u = i - 2
                    dve.wait_ge(d_made[l], u + 1)
                    r = u - NT
                    if r >= 4:
                        dve.wait_ge(yr_stored[l][r % 4], 16 * (r // 4))
                    dst = y_shared[:, u, :] if r < 0 else yr[r % 4][:]
                    v.tensor_copy(dst, ps[6 + u % 2][:, 0:D]).then_inc(yr_ready[l], 1)
            dve.wait_ge(yr_ready[l], NT)
            for t in range(NT):
                if t == 0:
                    dve.wait_ge(gathered[l], 16 * NT)
                v.tensor_tensor(y[:, t, :], y[:, t, :], y_shared[:, t, :], ALU.add).then_inc(y_ready, 1)
            dve.wait_ge(y_ready, (2 * l + 2) * NT)

        def scalar_program(act):
            def turn(p, i):
                act.wait_ge(xT_made, 4 * p + i + 1)
                cols = slice(i * 256, (i + 1) * 256)
                dst = xT_hi if p == 0 else xT
                nc.scalar.activation(dst[:, :, cols], ps[i][:].rearrange("p (c n) -> p c n", c=KC),
                                     ACT.Copy).then_inc(xT_ready, 1)

            def weight_hi(n, s):
                full, hi = {"k": (wk_f, wk_hi), "q": (wq_f, wq_hi)}[n]
                if s:
                    act.wait_ge(product, made(s - 1, (n.upper(), 1, TB - 1)))
                    act.wait_ge(w_lo_ready[n], s)
                act.wait_ge(w_loaded[n], 16 * (s + 1))
                nc.scalar.activation(hi[:], full[:], ACT.Copy).then_inc(w_hi_ready[n], 1)

            weight_hi("k", 0)
            weight_hi("q", 0)
            for i in range(4):
                turn(0, i)
            for s in range(NS):
                for n in ORDER:
                    kind, b, i = n
                    pt = bank(n)
                    if n in BY_ACT:
                        act.wait_ge(product, made(s, n))
                        if kind == "K":
                            if s:
                                act.wait_ge(ksum_ready, (s - 1) * B + b + 1)
                            nc.scalar.activation(k_hi[b][:, i], pt[:], ACT.Relu).then_inc(act_done, 1)
                        elif kind == "G":
                            nc.scalar.activation(kx[:, i], pt[:], ACT.Copy).then_inc(act_done, 1)
                        elif kind == "Q":
                            if s:
                                act.wait_ge(q_lo_ready, ((s - 1) * B + b) * CH + i + 1)
                            nc.scalar.activation(q[b][:, i], pt[:], ACT.Relu).then_inc(act_done, 1)
                        else:
                            nc.scalar.activation(kvo_hi[b][:, 2 * i:2 * i + 2],
                                                 pt[:].rearrange("p (j m) -> p j m", j=2), ACT.Copy).then_inc(act_done, 1)
                    elif kind == "BC":
                        act.wait_ge(dve_done, dve_through(s, n))
                        nc.scalar.activation(q_hi[b][:, i], q[b][:, i], ACT.Copy).then_inc(q_hi_ready, 1)
                    if s + 1 < NS and n == ("K", 1, TB - 1):
                        weight_hi("k", s + 1)
                    if s + 1 < NS and n == ("Q", 1, CH - 1):
                        weight_hi("q", s + 1)
            for p in range(1, phases):
                for i in range(4):
                    turn(p, i)
                if p == 2:
                    act_l1(act)
                else:
                    act_moe(act, p // 2)

        def act_moe(act, l):
            act.wait_ge(best_ready[l], 1)
            nc.scalar.activation(score[:], best[:], ACT.Sigmoid).then_inc(score_ready[l], 1)
            for i in range(-2, NU + 1):
                if 0 <= i < NU:
                    act.wait_ge(gu_made[l], i + 1)
                    if i >= 2:
                        act.wait_ge(h_ready[l], i - 1)
                    nc.scalar.activation(sg[i % 2][:], ps[2 + i % 2][:, 0:F], ACT.Silu).then_inc(silu_ready[l], 1)
                if 1 <= i:
                    u = i - 1
                    act.wait_ge(hT_made[l], u + 1)
                    if u >= 2:
                        act.wait_ge(d_made[l], u - 1)
                    nc.scalar.activation(hT[u % 2][:], ps[4 + u % 2][:, 0:F].rearrange("p (c n) -> p c n", c=FC),
                                         ACT.Copy).then_inc(hT_ready[l], 1)
                r = i + 2 - NT
                if 0 <= r < NR:
                    act.wait_ge(xgT_made[l], r + 1)
                    if r >= 2:
                        act.wait_ge(gu_made[l], i + 1)
                    nc.scalar.activation(xgT[r % 2][:], ps[r % 2][:, 0:D].rearrange("p (c n) -> p c n", c=KC),
                                         ACT.Copy).then_inc(xgT_ready[l], 1)

        def tensor_program(pe):
            mm = nc.tensor.matmul

            def turn_x(p):
                if p == 0:
                    pe.wait_ge(consts, 4)
                for i in range(4):
                    for t in (2 * i, 2 * i + 1):
                        pe.wait_ge(xn_ready, NT * p + t + 1)
                        for c in range(KC):
                            last = nc.tensor.transpose(ps[i][:, c * 256 + t % 2 * P:c * 256 + (t % 2 + 1) * P],
                                                       xn[:, t, c * P:(c + 1) * P], ident[:])
                    last.then_inc(xT_made, 1)

            turn_x(0)
            pe.wait_ge(xT_lo_ready, 4)
            for s in range(NS):
                pe_slice(pe, s)
            for p in range(1, phases):
                turn_x(p)
                pe.wait_ge(xT_ready, 4 * p + 4)
                if p == 2:
                    pe_l1(pe)
                else:
                    pe_moe(pe, p // 2)

        def pe_slice(pe, s):
            mm = nc.tensor.matmul

            def out_mm(b, t, j, passes):
                o = acc[b][t // 2][:, t % 2 * D:(t % 2 + 1) * D]
                tok = slice(t * P, (t + 1) * P)
                return split_mm(o, (q_hi[b][:, j, tok], q_lo[b][:, j, tok]), (kvo_hi[b][:, j], kvo_lo[b][:, j]),
                                start=(s == 0 and j == 0 and t % 2 == 0), stop=(s == NS - 1 and j == CH - 1),
                                skip_group_check=True)

            for pos, n in enumerate(ORDER):
                kind, b, i = n
                prev = pos - BANKS if pos >= BANKS else max(q_ for q_ in range(NP_) if q_ % BANKS == pos)
                ps_ = s if pos >= BANKS else s - 1
                if ps_ >= 0:
                    pn = ORDER[prev]
                    if pn in BY_DVE:
                        pe.wait_ge(dve_done, dve_through(ps_, pn))
                    else:
                        pe.wait_ge(act_done, act_through(ps_, pn))
                pt = bank(n)
                if kind == "K":
                    if (b, i) == (0, 0):
                        pe.wait_ge(w_lo_ready["k"], s + 1)
                    tok = slice((b * TB + i) * P, (b * TB + i + 1) * P)
                    for c in range(KC):
                        last = split_mm(pt[:], (xT_hi[:, c, tok], xT_lo[:, c, tok]), (wk_hi[:, c], wk_lo[:, c]),
                                        c == 0, c == KC - 1)
                elif kind == "Q":
                    if (b, i) == (0, 0):
                        pe.wait_ge(w_lo_ready["q"], s + 1)
                    ch, tok = slice(i * P, (i + 1) * P), slice(b * S, (b + 1) * S)
                    for c in range(KC):
                        last = split_mm(pt[:], (wq_hi[:, c, ch], wq_lo[:, c, ch]), (xT_hi[:, c, tok], xT_lo[:, c, tok]),
                                        c == 0, c == KC - 1)
                elif kind == "G":
                    if s == 0:
                        pe.wait_ge(split_lo, b + 1)
                    ch = slice(i * P, (i + 1) * P)
                    for t in range(TB):
                        pe.wait_ge(dve_done, dve_through(s, ("K", b, t)))
                        last = split_mm(pt[:], (xn_hi[:, b * TB + t, ch], xn_lo[:, b * TB + t, ch]),
                                        (k_hi[b][:, t], k_lo[b][:, t]), t == 0, t == TB - 1)
                elif kind == "S":
                    pe.wait_ge(ksum_ready, s * B + b + 1)
                    for j in range(CH):
                        last = mm(pt[:, j * P:(j + 1) * P], ksum[:, j * P:(j + 1) * P], ones[:], start=True, stop=True)
                elif kind == "KV":
                    pe.wait_ge(w_loaded["v"], 16 * (s + 1))
                    pe.wait_ge(act_done, act_through(s, ("G", b, KC - 1)))
                    for j in range(CH):
                        ch = slice(j * P, (j + 1) * P)
                        for c in range(KC):
                            last = mm(pt[:, ch], wv_f[:, c, ch], kx[:, c, ch], start=(c == 0), stop=(c == KC - 1))
                elif kind == "N":
                    pe.wait_ge(dve_done, dve_through(s, ("S", b, 0)))
                    pe.wait_ge(act_done, act_through(s, ("Q", b, CH - 1)))
                    for j in range(CH):
                        last = mm(pt[j * 32:(j + 1) * 32, :], nk[b][:, j], q[b][:, j], start=True, stop=True)
                elif kind == "KVO":
                    pe.wait_ge(w_loaded["o"], 16 * (s + 1))
                    pe.wait_ge(dve_done, dve_through(s, ("KV", b, 0)))
                    for j in (2 * i, 2 * i + 1):
                        last = mm(pt[:, j % 2 * D:(j % 2 + 1) * D], kv[b][:, j], wo_f[:, j], start=True, stop=True)
                else:
                    if b:
                        if i == 0:
                            pe.wait_ge(q_lo_ready, (s * B) * CH + CH)
                            pe.wait_ge(dve_done, dve_through(s, ("KVO", 0, 1)))
                        for j in range(CH):
                            last = out_mm(0, i, j, 3)
                        last.then_inc(out_tiles, 1)
                    pe.wait_ge(rec_ready, s * B + b + 1)
                    mm(pt[:], pick_r[:, i], rec_hi[b][:], start=True, stop=False)
                    last = mm(pt[:], pick_r[:, i], rec_lo[b][:], start=False, stop=True)
                last.then_inc(product, 1)
            pe.wait_ge(dve_done, dve_through(s, ("KVO", 1, 1)))
            for j in range(CH):
                pe.wait_ge(q_lo_ready, (s * B + 1) * CH + j + 1)
                for t in range(TB):
                    last = out_mm(1, t, j, 3)
            if s == NS - 1:
                last.then_inc(out_done, B)
            else:
                last.then_inc(out_tiles, TB)

        def pe_moe(pe, l):
            mm = nc.tensor.matmul
            if l == 0:
                pe.wait_ge(small_loaded, SMALL)
            pe.wait_ge(y_ready, (2 * l + 1) * NT)
            for t in range(NT):
                for c in range(KC):
                    last = mm(ps[6][:, t * E:(t + 1) * E], xT[:, c, t * P:(t + 1) * P], router[l][:, c],
                              start=(c == 0), stop=(c == KC - 1))
            last.then_inc(logits_made[l], 1)

            def ranks():
                pe.wait_ge(hot_ready[l], 1)
                for t in range(NT):
                    o = ps[7][:, t * E:(t + 1) * E]
                    for j in range(t):
                        mm(o, onesb[:], hot[:, j], start=(j == 0), stop=False)
                    mm(o, below[:], hot[:, t], start=(t == 0), stop=True)
                for j in range(NT):
                    last = mm(ps[7][:, NT * E:(NT + 1) * E], onesb[:], hot[:, j], start=(j == 0), stop=(j == NT - 1))
                last.then_inc(rank_made[l], 1)

            def gate_up(u):
                r = u - NT
                if u >= 2:
                    pe.wait_ge(h_ready[l], u - 1)
                if r < 0:
                    if u == 0:
                        pe.wait_ge(shared_w[l], 48)
                    for c in range(KC):
                        last = mm(ps[2 + u % 2][:], xT[:, c, u * P:(u + 1) * P], shared_gu[:, c],
                                  start=(c == 0), stop=(c == KC - 1))
                else:
                    if r == 0:
                        pe.wait_ge(moe_w[l], 16 * 3 * E)
                    pe.wait_ge(xgT_ready[l], r + 1)
                    for c in range(KC):
                        last = mm(ps[2 + u % 2][:], xgT[r % 2][:, c], w_gu[:, bass.ds(experts[r], 1), c, :],
                                  start=(c == 0), stop=(c == KC - 1))
                last.then_inc(gu_made[l], 1)

            def turn_h(u):
                pe.wait_ge(h_ready[l], u + 1)
                if u >= 2:
                    pe.wait_ge(hT_ready[l], u - 1)
                for c in range(FC):
                    last = nc.tensor.transpose(ps[4 + u % 2][:, c * P:(c + 1) * P], h[u % 2][:, c * P:(c + 1) * P], ident[:])
                last.then_inc(hT_made[l], 1)

            def turn_rows(r):
                pe.wait_ge(xg_loaded[l][r % 4], 16 * (r // 4 + 1))
                if r >= 2:
                    pe.wait_ge(xgT_ready[l], r - 1)
                for c in range(KC):
                    last = nc.tensor.transpose(ps[r % 2][:, c * P:(c + 1) * P], xg[r % 4][:, c * P:(c + 1) * P], ident[:])
                last.then_inc(xgT_made[l], 1)

            def down(u):
                r = u - NT
                pe.wait_ge(hT_ready[l], u + 1)
                if u == 0:
                    pe.wait_ge(logits_read[l], 1)
                elif u == 1:
                    pe.wait_ge(rank_read[l], 1)
                else:
                    pe.wait_ge(yr_ready[l], u - 1)
                for c in range(FC):
                    w = shared_d[:, c] if r < 0 else w_d[:, bass.ds(experts[r], 1), c, :]
                    last = mm(ps[6 + u % 2][:, 0:D], hT[u % 2][:, c], w, start=(c == 0), stop=(c == FC - 1))
                last.then_inc(d_made[l], 1)

            experts = {}
            for i in range(NU + 2):
                if i < NU:
                    gate_up(i)
                if i == 0:
                    ranks()
                if 1 <= i <= NU:
                    turn_h(i - 1)
                r = i + 2 - NT
                if 0 <= r < NR:
                    if r == 0:
                        pe.wait_ge(expert_ready[l], 1)
                    experts[r] = pe.value_load(expert[0:1, r:r + 1], min_val=0, max_val=E - 1)
                    turn_rows(r)
                if i >= 2:
                    down(i - 2)

        TURNS = [("q1", 0)]
        for n_ in range(NG + 1):
            TURNS += [("q2", n_ - 1)] * (n_ >= 1) + [("o", n_ - 2)] * (n_ >= 2) + [("q1", n_ + 1)] * (n_ + 1 < NG)
        TURNS += [("o", NG - 1)]
        Q_TURNS = [x_ for x_ in TURNS if x_[0] != "o"]

        def turn_no(what):
            return TURNS.index(what) + 1

        def q_turn_no(what):
            return Q_TURNS.index(what) + 1

        def act_l1(act):
            for i in range(B * TB * 2):
                b, t, half = i // (2 * TB), i // 2 % TB, i % 2
                act.wait_ge(kT_made, i + 1)
                nc.scalar.activation(kT[b][:, half * 4:half * 4 + 4, :, t * P:(t + 1) * P],
                                     ps[i % 4].bitcast(BF16).rearrange("p (g w n) -> p g w n", g=4, w=2),
                                     ACT.Copy).then_inc(kT_copied, 1)

            def queries(what, dst):
                act.wait_ge(turned, turn_no(what))
                nc.scalar.activation(dst[:], ps[7].bitcast(BF16).rearrange("p (i n) -> p i n", i=2),
                                     ACT.Copy).then_inc(qT_ready, 1)

            queries(("q1", 0), qT1)
            for n in range(NG + 1):
                if n >= 1:
                    queries(("q2", n - 1), qT2)
                for kc in range(TB):
                    if kc == TB - 1 and n + 1 < NG:
                        queries(("q1", n + 1), qT1)
                    if n >= 1:
                        c = (n - 1) * TB + kc
                        if c >= 2:
                            act.wait_ge(av_done, c - 1)
                        for j in range(GH):
                            act.wait_ge(s2_made, c * GH + j + 1)
                            nc.scalar.activation(pr[c % 2][:, j], ps[4 + j % 2], ACT.Exp,
                                                 scale=SCALE).then_inc(exp_ready, 1)
            for t in range(NT):
                act.wait_ge(attT_made, t + 1)
                nc.scalar.activation(xT[:, :, t * P:(t + 1) * P],
                                     ps[t % 4][:, 0:D].rearrange("p (c n) -> p c n", c=KC), ACT.Copy).then_inc(attT_ready, 1)

        def pe_l1(pe):
            mm = nc.tensor.matmul
            pe.wait_ge(l1_loaded, 48)
            for t in range(NT):
                if t >= 4:
                    pe.wait_ge(qkv_ready, t - 3)
                for c in range(KC):
                    last = mm(ps[4 + t % 4][:, 0:QKV], xT[:, c, t * P:(t + 1) * P], wqkv[:, c],
                              start=(c == 0), stop=(c == KC - 1))
                last.then_inc(qkv_made, 1)
            for i in range(B * TB * 2):
                b, t, half = i // (2 * TB), i // 2 % TB, i % 2
                pe.wait_ge(stacks_ready, b + 1)
                if i >= 4:
                    pe.wait_ge(kT_copied, i - 3)
                for k in range(8):
                    last = nc.tensor.transpose(ps[i % 4].bitcast(BF16)[:, k * P:(k + 1) * P],
                                               ks[:, t, half * 4 + k // 2, k % 2, :], identb[:])
                last.then_inc(kT_made, 1)

            def turn(what):
                n = TURNS.index(what)
                if n:
                    if TURNS[n - 1][0] == "o":
                        pe.wait_ge(att_ready, TURNS[n - 1][1] + 1)
                    else:
                        pe.wait_ge(qT_ready, q_turn_no(TURNS[n - 1]))
                kind, g_ = what
                b, g = g_ // NKV, g_ % NKV
                if kind == "o":
                    pe.wait_ge(oT_ready, g_ + 1)
                    for t in range(TB):
                        last = nc.tensor.transpose(ps[7][:, t * P:(t + 1) * P], oT[:, t * P:(t + 1) * P], ident[:])
                else:
                    if kind == "q2":
                        pe.wait_ge(max_ready, g_ + 1)
                    for i in range(2):
                        for t in range(TB):
                            last = nc.tensor.transpose(
                                ps[7].bitcast(BF16)[:, (i * TB + t) * P:(i * TB + t + 1) * P],
                                qs[b][:, t, GH * g + 2 * i:GH * g + 2 * i + 2, :].rearrange("p h w -> p (h w)"), identb[:])
                last.then_inc(turned, 1)

            def scores1(n, t, i):
                b, g = n // NKV, n % NKV
                c = (n * TB + t) * 2 + i
                if c >= 2:
                    pe.wait_ge(max_read, c - 1)
                if t == 0 and i == 0:
                    pe.wait_ge(qT_ready, q_turn_no(("q1", n)))
                for ver in range(2):
                    last = mm(ps[c % 2 * 2 + ver], qT1[:, i, t * P:(t + 1) * P], kT[b][:, g, ver, :], start=True, stop=True)
                last.then_inc(s1_made, 1)

            def scores2(n, kc, i):
                b, g = n // NKV, n % NKV
                if kc == 0 and i == 0:
                    pe.wait_ge(qT_ready, q_turn_no(("q2", n)))
                for ver in range(2):
                    c = (n * TB + kc) * GH + 2 * i + ver
                    if c >= 2:
                        pe.wait_ge(exp_ready, c - 1)
                    mm(ps[4 + ver], kT[b][:, g, ver, kc * P:(kc + 1) * P], qT2[:, i, :], start=True,
                       stop=True).then_inc(s2_made, 1)

            def weigh(n, kc):
                b, g = n // NKV, n % NKV
                c = n * TB + kc
                pe.wait_ge(exp_ready, (c + 1) * GH)
                if kc == 0 and n:
                    pe.wait_ge(oT_ready, n)
                for j in range(GH):
                    last = mm(ps[6][j * VW:(j + 1) * VW, :], vals[:, b * TB + kc, g, :], pr[c % 2][:, j],
                              start=(kc == 0), stop=(kc == TB - 1), skip_group_check=True)
                last.then_inc(av_done, 1)

            pe.wait_ge(kT_copied, B * TB * 2)
            turn(("q1", 0))
            for n in range(NG + 1):
                m = n - 1
                one, two = n < NG, n >= 1
                if one:
                    scores1(n, 0, 0)
                    scores1(n, 0, 1)
                if two:
                    turn(("q2", m))
                for kc in range(TB):
                    if one and kc + 1 < TB:
                        scores1(n, kc + 1, 0)
                    if two:
                        scores2(m, kc, 0)
                        if kc:
                            weigh(m, kc - 1)
                    if one and kc + 1 < TB:
                        scores1(n, kc + 1, 1)
                    if two:
                        scores2(m, kc, 1)
                    if kc == 0 and n >= 2:
                        turn(("o", n - 2))
                    if kc == TB - 2 and n + 1 < NG:
                        turn(("q1", n + 1))
                if two:
                    weigh(m, TB - 1)
            turn(("o", NG - 1))
            for t in range(NT + 1):
                if t < NT:
                    pe.wait_ge(att_ready, NG)
                    if t >= 4:
                        pe.wait_ge(attT_ready, t - 3)
                    for c in range(KC):
                        last = nc.tensor.transpose(ps[t % 4][:, c * P:(c + 1) * P], xn[:, t, c * P:(c + 1) * P], ident[:])
                    last.then_inc(attT_made, 1)
                if t:
                    u = t - 1
                    pe.wait_ge(attT_ready, u + 1)
                    if u >= 4:
                        pe.wait_ge(y_ready, 2 * NT + u - 3)
                    for c in range(KC):
                        last = mm(ps[4 + u % 4][:, 0:D], xT[:, c, u * P:(u + 1) * P], wo1[:, c],
                                  start=(c == 0), stop=(c == KC - 1))
                    last.then_inc(proj_made, 1)

        def dve_l1(dve, link, mark, settle):
            v = nc.vector
            dve.wait_ge(l1_loaded, 48)
            dve.wait_ge(l1_consts, 7)
            for t in range(NT):
                dve.wait_ge(qkv_made, t + 1)
                v.tensor_tensor(qkv[:, t, :], ps[4 + t % 4][:, 0:QKV], bqkv[:], ALU.add).then_inc(qkv_ready, 1)
            dve.wait_ge(qkv_ready, NT)
            v.tensor_copy(vals[:, :, :, 0:HD], qkv[:, :, KEND:QKV].rearrange("p t (g d) -> p t g d", d=HD)).then_inc(part_ready, 1)
            for b in range(B):
                src = qkv[:, b * TB:(b + 1) * TB, 0:KEND]
                link(v.tensor_copy(part[0][:], src))
                link(v.tensor_tensor(rest[0][:], src, part[0][:], ALU.subtract))
                link(v.tensor_copy(part[1][:], rest[0][:]))
                link(v.tensor_tensor(rest[1][:], rest[0][:], part[1][:], ALU.subtract))
                link(v.tensor_copy(part[2][:], rest[1][:]))
                for t in range(TB):
                    for i, (at_, n) in enumerate(((0, 3), (3, 2), (5, 1))):
                        v.tensor_copy(qs[b][:, t, :, at_ * HD:(at_ + n) * HD].rearrange("p h (n d) -> p h n d", d=HD),
                                      part[i][:, t, 0:NQ * HD].rearrange("p (h d) -> p h d", d=HD).unsqueeze(2)
                                      .to_broadcast([P, NQ, n, HD])).then_inc(part_ready, 1)
                if b:
                    dve.wait_ge(kT_made, 2 * TB)
                for ver in range(2):
                    for at_, i in enumerate((0, 1, 2, 0, 1, 0)):
                        mark(v.tensor_copy(ks[:, :, :, ver, ver * HW + at_ * HD:ver * HW + (at_ + 1) * HD],
                                           part[i][:, :, NQ * HD:].rearrange("p t (g d) -> p t g d", d=HD)))
                settle()
                dve.wait_ge(part_ready, 1 + (b + 1) * 3 * TB)
                v.tensor_copy(dn[:, 0, 0:1], ones[:, 0:1]).then_inc(stacks_ready, 1)

            def maximum(n, t, i):
                c = (n * TB + t) * 2 + i
                dve.wait_ge(s1_made, c + 1)
                v.tensor_reduce(mx[:, t, 2 * i:2 * i + 2], psum[:, c % 2 * 1024:(c % 2 + 1) * 1024].rearrange(
                    "p (h n) -> p h n", h=2), AX.X, ALU.max).then_inc(max_read, 1)

            def outputs(n):
                b, g = n // NKV, n % NKV
                dve.wait_ge(turned, turn_no(("o", n)))
                o = ps[7].rearrange("p (t h w) -> p t h w", t=TB, h=GH)
                link(v.reciprocal(dn[:], o[:, :, :, HD]))
                for t in range(TB):
                    ins = v.tensor_tensor(
                        xn[:, b * TB + t, g * GH * HD:(g + 1) * GH * HD].rearrange("p (h d) -> p h d", d=HD),
                        o[:, t, :, 0:HD], dn[:, t, :].unsqueeze(2).to_broadcast([P, GH, HD]), ALU.mult)
                    if t < TB - 1:
                        mark(ins)
                    else:
                        ins.then_inc(att_ready, 1)

            for n in range(NG + 1):
                b, g = n // NKV, n % NKV
                for t in range(TB):
                    for i in range(2):
                        if n < NG:
                            maximum(n, t, i)
                        if n >= 2 and t == 2 and i == 0:
                            outputs(n - 2)
                if n < NG:
                    dve.wait_ge(max_read, (n + 1) * TB * 2)
                    to = [qs[b][:, :, g * GH:(g + 1) * GH, MAXAT + i] for i in range(3)]
                    link(v.tensor_scalar(to[0], mx[:], -1.0, None, ALU.mult))
                    link(v.scalar_tensor_tensor(mr[0][:], mx[:], -1.0, to[0], ALU.mult, ALU.subtract))
                    link(v.tensor_copy(to[1], mr[0][:]))
                    link(v.tensor_tensor(mr[1][:], mr[0][:], to[1], ALU.subtract))
                    v.tensor_copy(to[2], mr[1][:]).then_inc(max_ready, 1)
                if n >= 1:
                    dve.wait_ge(av_done, n * TB)
                    v.tensor_copy(oT[:], ps[6]).then_inc(oT_ready, 1)
            outputs(NG - 1)
            for t in range(NT):
                dve.wait_ge(proj_made, t + 1)
                v.tensor_tensor(y[:, t, :], ps[4 + t % 4][:, 0:D], bo1[:], ALU.add).then_inc(y_ready, 1)
            dve.wait_ge(y_ready, 3 * NT)

        @block.sync
        def _(eng):
            sync_program(eng)


        @block.gpsimd
        def _(eng):
            gpsimd_program(eng)


        @block.vector
        def _(eng):
            vector_program(eng)


        @block.scalar
        def _(eng):
            scalar_program(eng)


        @block.tensor
        def _(eng):
            tensor_program(eng)


_INS = ['L0_attn_hidden_states', 'L0_attn_Wq', 'L0_attn_Wk', 'L0_attn_Wv', 'L0_attn_Wo', 'L0_attn_bo',
        'L0_ffn_router_w', 'L0_ffn_gate_w', 'L0_ffn_up_w', 'L0_ffn_down_w', 'L0_ffn_shared_gate_w',
        'L0_ffn_shared_up_w', 'L0_ffn_shared_down_w', 'L1_attn_Wqkv', 'L1_attn_bqkv', 'L1_attn_Wo', 'L1_attn_bo',
        'L1_ffn_router_w', 'L1_ffn_gate_w', 'L1_ffn_up_w', 'L1_ffn_down_w', 'L1_ffn_shared_gate_w',
        'L1_ffn_shared_up_w', 'L1_ffn_shared_down_w']


def kernel(**inputs):
    import numpy as np
    import concourse.bacc as bacc
    from concourse.bass_utils import run_bass_kernel_spmd

    nc = bacc.Bacc("TRN2", target_bir_lowering=False, num_devices=1)
    arrays, args = {}, {}
    for name in _INS:
        arr = np.ascontiguousarray(inputs[name])
        arrays[f"in_{name}"] = arr
        args[name] = nc.dram_tensor(f"in_{name}", arr.shape, mybir.dt.from_np(arr.dtype), kind="ExternalInput").ap()
    out = nc.dram_tensor("out_x", (B, S, D), F32, kind="ExternalOutput").ap()
    build(nc, args, out)
    r = run_bass_kernel_spmd(nc, [arrays], core_ids=[0])
    return r.results[0]["out_x"]
```

```python
from contextlib import ExitStack

import concourse.bass as bass
from concourse import mybir

F32 = mybir.dt.float32
F32R = mybir.dt.float32r
BF16 = mybir.dt.bfloat16
I32 = mybir.dt.int32
U32 = mybir.dt.uint32
ALU = mybir.AluOpType
ACT = mybir.ActivationFunctionType
AX = mybir.AxisListType

P = 128
B, S, D = 2, 512, 256
NT = B * S // P
TB = S // P
KC = D // P
EPS = 1e-5

INNER = 2048
SL = 512
NS = INNER // SL
CH = SL // P
HC = 64

E, F = 8, 256
FC = F // P
NR = NT + E - 1
NSF = 4
NU = NT + NR


def routed(u):
    return u - NSF if NSF <= u < NSF + NR else None


def shared_tile(u):
    return u if u < NSF else u - NR


NQ, NKV, HD = 32, 8, 8
GH = NQ // NKV
QKV = HD * (NQ + 2 * NKV)
KEND = HD * (NQ + NKV)
HW = 64
MAXAT = 6 * HD
VW = 32
NG = B * NKV
SCALE = float(1.0 / HD ** 0.5)


def build(nc, a, out, phases=4):
    ctx = ExitStack()
    with ctx:
        def sem(name):
            return ctx.enter_context(nc.semaphore(name))

        arena_at = [0]
        names = {}

        def at(name, shape, dt, where):
            n = 1
            for d in shape[1:]:
                n *= d
            size = n * (2 if dt == BF16 else 4)
            t = nc.alloc_sbuf_tensor_at(name, shape, dt, offset=where[0])
            where[0] += (size + 31) // 32 * 32
            assert where[0] <= LIMIT, (name, where[0], LIMIT, here[0])
            return t

        base = nc.sbuf_base
        LIMIT = nc.sbuf_usable_end
        fence = ctx.enter_context(nc.sbuf_tensor("arena", [P, (LIMIT - base - 256) // 4], F32))
        here = [(base + 31) // 32 * 32]

        x = at("x", [P, NT, D], F32, here)
        in_xn = [here[0]]
        xn = at("xn", [P, NT, D], F32, here)
        in_xT = [here[0]]
        xT = at("xT", [P, KC, B * S], F32, here)
        in_y, l1_in_y = [here[0]], [here[0]]
        y = at("y", [P, NT, D], F32, here)
        ident = at("ident", [P, P], F32, here)
        identb = at("identb", [P, P], BF16, here)
        ones = at("ones", [P, P], F32, here)
        onesb = at("onesb", [P, P], BF16, here)
        below = at("below", [P, P], BF16, here)
        same_head = at("same_head", [P, P], F32, here)
        pick_r = at("pick_r", [P, CH, P], F32R, here)
        up_to = at("up_to", [P, E, E], F32, here)
        rows_at = at("rows_at", [P, NT], F32, here)
        tile_no = at("tile_no", [P, 16], F32, here)
        rank_key = at("rank_key", [P, E], F32, here)
        mhalf = at("mhalf", [P, NT], F32, here)
        stat = at("stat", [P, NT, 6], F32, here)
        mv = at("mv", [P, NT, 2], F32, here)
        var = at("var", [P, NT], F32, here)
        nmean = [at(f"nmean{i}", [P, NT], F32, here) for i in range(2)]
        rstd = at("rstd", [P, NT], F32, here)
        shift = [at(f"shift{i}", [P, NT], F32, here) for i in range(2)]
        bo0 = at("bo0", [P, D], F32, here)
        bo1 = at("bo1", [P, D], F32, here)
        zeros = at("zeros", [P, D], F32, here)
        router = [at(f"router{l}", [P, KC, 32], F32, here) for l in range(2)]
        shared_gu = at("shared_gu", [P, KC, 2 * F], F32, here)
        shared_d = at("shared_d", [P, FC, D], F32, here)

        l0 = [here[0]]
        xT_hi = at("xT_hi", [P, KC, B * S], F32R, in_xT)
        xT_lo = at("xT_lo", [P, KC, B * S], F32R, in_y)
        xn_hi = at("xn_hi", [P, NT, D], F32R, l0)
        xn_lo = at("xn_lo", [P, NT, D], F32R, l0)
        wk_f, wq_f, wv_f = (at(n, [P, KC, SL], F32, l0) for n in ("wk_f", "wq_f", "wv_f"))
        wo_f = at("wo_f", [P, CH, D], F32, l0)
        wk_hi, wk_lo, wq_hi, wq_lo = (at(n, [P, KC, SL], F32R, l0) for n in ("wk_hi", "wk_lo", "wq_hi", "wq_lo"))
        k_hi = [at(f"k_hi{b}", [P, TB, SL], F32R, l0) for b in range(B)]
        k_lo = [at(f"k_lo{b}", [P, TB, SL], F32R, l0) for b in range(B)]
        kx = at("kx", [P, KC, SL], F32, l0)
        q = [at(f"q{b}", [P, CH, SL], F32, l0) for b in range(B)]
        q_hi = [at(f"q_hi{b}", [P, CH, SL], F32R, l0) for b in range(B)]
        q_lo = [at(f"q_lo{b}", [P, CH, SL], F32R, l0) for b in range(B)]
        in_kv = [l0[0]]
        kv = [at(f"kv{b}", [P, CH, P], F32, l0) for b in range(B)]
        pick = at("pick", [P, CH, P], F32, in_kv)
        kvo_hi = [at(f"kvo_hi{b}", [P, CH, D], F32R, l0) for b in range(B)]
        kvo_lo = [at(f"kvo_lo{b}", [P, CH, D], F32R, l0) for b in range(B)]
        ksum = at("ksum", [P, SL], F32, in_xn)
        ksum_t = at("ksum_t", [P, 2, SL], F32, l0)
        nk = [at(f"nk{b}", [P, CH, 32], F32, l0) for b in range(B)]
        rec = at("rec", [P, SL], F32, in_xn)
        rec_hi = [at(f"rec_hi{b}", [P, SL], F32R, w) for b, w in enumerate((in_xn, l0))]
        rec_lo = [at(f"rec_lo{b}", [P, SL], F32R, w) for b, w in enumerate((in_xn, l0))]

        me = [here[0]]
        w_gu = at("w_gu", [P, E, KC, 2 * F], F32, me)
        in_wd = me[0]
        w_d = at("w_d", [P, E, FC, D], F32, me)
        y_shared = at("y_shared", [P, NT, D], F32, me)
        xg = [at(f"xg{i}", [P, D], F32, me) for i in range(4)]
        xgT = [at(f"xgT{i}", [P, KC, P], F32, me) for i in range(2)]
        sg = [at(f"sg{i}", [P, F], F32, me) for i in range(2)]
        h = [at(f"h{i}", [P, F], F32, me) for i in range(2)]
        hT = [at(f"hT{i}", [P, FC, P], F32, me) for i in range(2)]
        yr = [at(f"yr{i}", [P, D], F32, me) for i in range(4)]
        lgT = at("lgT", [P, 2 * P], F32, me)
        lg = at("lg", [P, NT, E], F32, me)
        best = at("best", [P, NT], F32, me)
        score = at("score", [P, NT], F32, me)
        hot_f = at("hot_f", [P, NT, E], F32, me)
        hot = at("hot", [P, NT, E], BF16, me)
        last_max = at("last_max", [P, NT], F32, me)
        cnt = at("cnt", [P, E], F32, me)
        cmp = at("cmp", [P, E, E], F32, me)
        tiles_of = at("tiles_of", [P, E], F32, me)
        tiles_end = at("tiles_end", [P, E], F32, me)
        row0 = at("row0", [P, E], F32, me)
        place = at("place", [P, NT, E], F32, me)
        slot_f = at("slot_f", [P, NT], F32, me)
        slot = at("slot", [P, NT], U32, me)
        past = at("past", [P, 16, E], F32, me)
        expert_f = at("expert_f", [P, 16], F32, me)
        expert = at("expert", [P, 16], I32, me)

        l1 = [here[0]]
        l1_first = [l1[0]]
        rest0 = [at(f"rest0_{i}", [P, TB, KEND], F32, l1) for i in range(2)]
        ks0 = at("ks0", [P, TB, NKV, 2, P], BF16, l1)
        assert l1[0] <= in_wd
        pr = [at(f"pr{i}", [P, GH, S], F32, l1_first) for i in range(3)]
        l1[0] = max(l1[0], l1_first[0])
        qkv = at("qkv", [P, NT, QKV], F32, l1)
        part = [[at(f"part{b}_{i}", [P, TB, KEND], BF16, l1) for i in range(3)] for b in range(B)]
        oT = at("oT", [P, S], F32, l1)
        kT = [at(f"kT{b}", [P, NKV, 2, S], BF16, l1) for b in range(B)]
        assert l1[0] >= me[0]
        qs = [at(f"qs{b}", [P, TB, NQ, HW], BF16, l1) for b in range(B)]
        ks1 = at("ks1", [P, TB, NKV, 2, P], BF16, l1)
        vals = at("vals", [P, NT, NKV, VW], F32, l1)
        bqkv = at("bqkv", [P, QKV], F32, l1)
        wqkv = at("wqkv", [P, KC, QKV], F32, l1)
        wo1 = at("wo1", [P, KC, D], F32, l1)
        rest1 = [at(f"rest1_{i}", [P, TB, KEND], F32, l1) for i in range(2)]
        mx = [at(f"mx{i}", [P, TB, GH], F32, l1) for i in range(2)]
        mr = [at(f"mr{i}", [P, TB, GH], F32, l1) for i in range(2)]
        dn = at("dn", [P, TB, GH], F32, l1)
        rest, ks = [rest0, rest1], [ks0, ks1]
        qT1 = [at(f"qT1_{i}", [P, 2, S], BF16, l1_in_y) for i in range(2)]
        qT2 = [at(f"qT2_{i}", [P, 2, S], BF16, l1_in_y) for i in range(2)]
        att = xn

        psum = ctx.enter_context(nc.psum_tensor("psum", [P, 8 * 512], F32))
        ps = [psum[:, i * 512:(i + 1) * 512] for i in range(8)]

        sorted_x = [nc.dram_tensor(f"sorted_x{l}", [NR * P, D], F32).ap() for l in range(2)]
        sorted_y = [nc.dram_tensor(f"sorted_y{l}", [NR * P, D], F32).ap() for l in range(2)]

        x_loaded = sem("x_loaded")
        small_loaded = sem("small_loaded")
        consts = sem("consts")
        const_casts = sem("const_casts")
        zeroed = sem("zeroed")
        var_ready, rstd_ready = sem("var_ready"), sem("rstd_ready")
        dve_chain = sem("dve_chain")
        xn_ready, xT_made, xT_ready = sem("xn_ready"), sem("xT_made"), sem("xT_ready")
        x_summed = sem("x_summed")
        last_summed = sem("last_summed")
        stored = sem("stored")

        w_loaded = {n: sem(f"w_loaded_{n}") for n in ("k", "q", "v", "o")}
        w_hi_ready, w_lo_ready = ({n: sem(f"w_{p}_{n}") for n in "kq"} for p in ("hi", "lo"))
        split_hi, split_lo, xT_lo_ready = sem("split_hi"), sem("split_lo"), sem("xT_lo_ready")
        product = sem("product")
        act_done, dve_done = sem("act_done"), sem("dve_done")
        ksum_ready = sem("ksum_ready")
        rec_ready = sem("rec_ready")
        q_hi_ready, q_lo_ready = sem("q_hi_ready"), sem("q_lo_ready")
        out_done = sem("out_done")
        y_ready = sem("y_ready")
        pool_chain = sem("pool_chain")
        act_chain = sem("act_chain")

        def trio(name):
            return [sem(f"{name}{l}") for l in range(2)]

        moe_w, shared_w = trio("moe_w"), trio("shared_w")
        lgT_ready, logits_made, hot_ready, rank_made = trio("lgT_ready"), trio("logits_made"), trio("hot_ready"), trio("rank_made")
        rank_read, logits_read = trio("rank_read"), trio("logits_read")
        slot_ready, expert_ready = trio("slot_ready"), trio("expert_ready")
        best_ready, score_ready, scaled = trio("best_ready"), trio("score_ready"), trio("scaled")
        scattered = trio("scattered")
        xg_loaded = [[sem(f"xg_loaded{l}_{i}") for i in range(4)] for l in range(2)]
        xgT_made, xgT_ready = trio("xgT_made"), trio("xgT_ready")
        gu_made, silu_ready, h_ready = trio("gu_made"), trio("silu_ready"), trio("h_ready")
        hT_made, hT_ready, d_made, yr_ready = trio("hT_made"), trio("hT_ready"), trio("d_made"), trio("yr_ready")
        yr_stored = [[sem(f"yr_stored{l}_{i}") for i in range(4)] for l in range(2)]
        gathered = [[sem(f"gathered{l}_{half}") for half in range(2)] for l in range(2)]

        qkv_made, qkv_ready, turn_copied = (sem(n) for n in ("qkv_made", "qkv_ready", "turn_copied"))
        q_stacked, k_stacked = trio("q_stacked"), trio("k_stacked")
        ks0_consts, l1_consts, l1_loaded, part_ready = sem("ks0_consts"), sem("l1_consts"), sem("l1_loaded"), sem("part_ready")
        turned = sem("turned")
        s1_made, max_read, max_ready = sem("s1_made"), sem("max_read"), sem("max_ready")
        s2_made, exp_ready = sem("s2_made"), sem("exp_ready")
        av_done, oT_ready, o_made, att_ready = sem("av_done"), sem("oT_ready"), sem("o_made"), sem("att_ready")
        attT_made, attT_ready, proj_made = sem("attT_made"), sem("attT_ready"), sem("proj_made")

        block = ctx.enter_context(nc.Block())

        def split_mm(o, lhs, rhs, start, stop, **kw):
            nc.tensor.matmul(o, lhs[0], rhs[0], start=start, stop=False, **kw)
            nc.tensor.matmul(o, lhs[0], rhs[1], start=False, stop=False, **kw)
            return nc.tensor.matmul(o, lhs[1], rhs[0], start=False, stop=stop, **kw)

        ORDER = [("K", b, t) for b in range(B) for t in range(TB)]
        ORDER += [("Q", 0, j) for j in range(CH)] + [("G", 0, c) for c in range(KC)] + [("S", 0, 0)]
        ORDER += [("KV", 0, 0)] + [("G", 1, c) for c in range(KC)] + [("N", 0, 0), ("S", 1, 0)]
        ORDER += [("Q", 1, j) for j in range(CH)] + [("N", 1, 0), ("KV", 1, 0)]
        ORDER += [("BC", 0, 0), ("KVO", 0, 0), ("BC", 0, 1), ("KVO", 0, 1), ("BC", 0, 2), ("KVO", 1, 0),
                  ("BC", 0, 3), ("KVO", 1, 1)]
        ORDER += [("BC", 1, j) for j in range(CH)]
        NP_ = len(ORDER)
        BY_ACT = [n for n in ORDER if n[0] in ("K", "G", "Q", "KVO")]
        BY_DVE = [n for n in ORDER if n[0] in ("K", "S", "KV", "N", "KVO", "BC")]
        BANKS = 4

        def made(s, n):
            return s * NP_ + ORDER.index(n) + 1

        def act_through(s, n):
            return s * len(BY_ACT) + BY_ACT.index(n) + 1

        def dve_through(s, n):
            return s * len(BY_DVE) + BY_DVE.index(n) + 1

        def bank(n):
            return ps[ORDER.index(n) % BANKS]

        acc = [[ps[4 + 2 * b + i] for i in range(2)] for b in range(B)]

        NORMS = 8

        def load(eng, dst, src, s):
            return eng.dma_start(dst, src).then_inc(s, 16)

        def sync_program(sp):
            xv = a["L0_attn_hidden_states"].rearrange("b (t p) d -> p (b t) d", p=P)
            for half in range(2):
                load(sp, x[:, half * TB:(half + 1) * TB, :], xv[:, half * TB:(half + 1) * TB, :], x_loaded)
            cols = {n: a[f"L0_attn_W{n}"].rearrange("(c p) n -> p c n", p=P) for n in "kqv"}
            rows = a["L0_attn_Wo"].rearrange("(j p) n -> p j n", p=P)
            stage = {"k": wk_f, "q": wq_f, "v": wv_f, "o": wo_f}
            for s in range(NS):
                if s:
                    sp.wait_ge(w_hi_ready["k"], s)
                    sp.wait_ge(w_lo_ready["k"], s)
                load(sp, stage["k"][:], cols["k"][:, :, s * SL:(s + 1) * SL], w_loaded["k"])
                if s:
                    sp.wait_ge(w_hi_ready["q"], s)
                    sp.wait_ge(w_lo_ready["q"], s)
                load(sp, stage["q"][:], cols["q"][:, :, s * SL:(s + 1) * SL], w_loaded["q"])
                if s:
                    sp.wait_ge(product, made(s - 1, ("KV", 1, 0)))
                load(sp, stage["v"][:], cols["v"][:, :, s * SL:(s + 1) * SL], w_loaded["v"])
                if s:
                    sp.wait_ge(product, made(s - 1, ("KVO", 1, 1)))
                load(sp, stage["o"][:], rows[:, s * CH:(s + 1) * CH, :], w_loaded["o"])
                if s == 0:
                    small_loads(sp)
            for p in range(1, phases):
                if p == 2:
                    load(sp, wqkv[:], a["L1_attn_Wqkv"].rearrange("(c p) n -> p c n", p=P), l1_loaded)
                    load(sp, bqkv[:], a["L1_attn_bqkv"].partition_broadcast(P), l1_loaded)
                    load(sp, wo1[:], a["L1_attn_Wo"].rearrange("(c p) n -> p c n", p=P), l1_loaded)
                else:
                    sp_moe(sp, p // 2)
            for t in range(NT):
                sp.wait_ge(x_summed, (phases - 1) * NT + t + 1)
                sp.dma_start(out.rearrange("b (t p) d -> p (b t) d", p=P)[:, t, :], x[:, t, :]).then_inc(stored, 16)
            sp.wait_ge(stored, 16 * NT)

        def small_loads(sp):
            for dst, name in ((bo0, "L0_attn_bo"), (bo1, "L1_attn_bo")):
                load(sp, dst[:], a[name].partition_broadcast(P), small_loaded)
            sp.wait_ge(consts, N_CONSTS)
            for l in range(2):
                load(sp, router[l][:, :, 0:E], a[f"L{l}_ffn_router_w"].rearrange("(c p) n -> p c n", p=P), small_loaded)
            for l in range(2):
                for i in range(NR):
                    load(sp, sorted_x[l][i * P:(i + 1) * P, :], zeros[:], zeroed)

        SMALL = 16 * 4

        def shared_loads(sp, l):
            pre = f"L{l}_ffn_"
            if l:
                sp.wait_ge(gu_made[0], NU)
                sp.wait_ge(d_made[0], NU)
            for i, n in enumerate(("gate", "up")):
                load(sp, shared_gu[:, :, i * F:(i + 1) * F], a[f"{pre}shared_{n}_w"].rearrange("(c p) f -> p c f", p=P),
                     shared_w[l])
            load(sp, shared_d[:], a[f"{pre}shared_down_w"].rearrange("(c p) f -> p c f", p=P), shared_w[l])

        def sp_moe(sp, l):
            pre = f"L{l}_ffn_"
            shared_loads(sp, l)
            sp.wait_ge(y_ready, (2 * l + 1) * NT)
            for e in range(E):
                for i, n in enumerate(("gate", "up")):
                    load(sp, w_gu[:, e, :, i * F:(i + 1) * F], a[f"{pre}{n}_w"][e].rearrange("(c p) f -> p c f", p=P),
                         moe_w[l])
                load(sp, w_d[:, e], a[f"{pre}down_w"][e].rearrange("(c p) f -> p c f", p=P), moe_w[l])
            sp.wait_ge(scattered[l], 16 * NT)

            def fetch(r):
                if r >= 4:
                    sp.wait_ge(xgT_made[l], r - 3)
                load(sp, xg[r % 4][:], sorted_x[l][r * P:(r + 1) * P, :], xg_loaded[l][r % 4])

            for r in range(NR + 5):
                if r < NR:
                    fetch(r)
                if r >= 5:
                    o = r - 5
                    sp.wait_ge(yr_ready[l], NSF + o + 1)
                    load(sp, sorted_y[l][o * P:(o + 1) * P, :], yr[o % 4][:], yr_stored[l][o % 4])

        N_CONSTS = 13

        def gpsimd_program(pool):
            g = nc.gpsimd
            count = [0]

            def link(ins):
                count[0] += 1
                ins.then_inc(pool_chain, 1)
                pool.wait_ge(pool_chain, count[0])

            g.memset(zeros[:], 0.0).then_inc(consts, 1)
            g.memset(ones[:], 1.0).then_inc(consts, 1)
            g.memset(mhalf[:], -0.5).then_inc(consts, 1)
            link(g.memset(ident[:], 0.0))
            g.affine_select(out=ident[:], in_=ident[:], compare_op=ALU.not_equal, fill=1.0, base=0,
                            pattern=[[-1, P]], channel_multiplier=1).then_inc(consts, 1)
            for n in range(2):
                pool_rstd(pool, n)
            link(g.memset(below[:], 1.0))
            g.affine_select(out=below[:], in_=below[:], compare_op=ALU.is_gt, fill=0.0, base=0,
                            pattern=[[1, P]], channel_multiplier=-1).then_inc(consts, 1)
            link(g.memset(pick[:], 0.0))
            g.affine_select(out=pick[:], in_=pick[:], compare_op=ALU.not_equal, fill=1.0, base=0,
                            pattern=[[-32, CH], [-1, 2], [0, P // 2]], channel_multiplier=1).then_inc(consts, 1)
            link(g.memset(up_to[:], 1.0))
            g.affine_select(out=up_to[:], in_=up_to[:], compare_op=ALU.is_ge, fill=0.0, base=0,
                            pattern=[[1, E], [-1, E]], channel_multiplier=0).then_inc(consts, 1)
            kw = dict(channel_multiplier=0, allow_small_or_imprecise_dtypes=True)
            g.iota(rows_at[:], pattern=[[P, NT]], base=0, **kw).then_inc(consts, 1)
            g.iota(tile_no[:], pattern=[[1, 16]], base=0, **kw).then_inc(consts, 1)
            g.iota(rank_key[:], pattern=[[-1, E]], base=E, **kw).then_inc(consts, 1)
            g.memset(onesb[:], 1.0).then_inc(consts, 1)
            for l in range(2):
                g.memset(router[l][:], 0.0).then_inc(consts, 1)
            pool_l0(pool, link)
            for p in range(1, phases):
                for n in range(4 * p - 2, 4 * p + 2):
                    pool_rstd(pool, n)
                if p == 2:
                    pool_l1_loop(pool, link)
                if p != 2:
                    pool_moe(pool, p // 2)
            for n in range(4 * phases - 2, 4 * phases):
                pool_rstd(pool, n)

        def pool_rstd(pool, n):
            half = slice((n % 2) * TB, (n % 2 + 1) * TB)
            pool.wait_ge(consts, 3)
            pool.wait_ge(var_ready, 2 * (n + 1))
            nc.gpsimd.tensor_tensor(rstd[:, half], var[:, half], mhalf[:, half], ALU.pow).then_inc(rstd_ready, 1)
            pool.wait_ge(rstd_ready, 2 * n + 1)
            nc.gpsimd.tensor_tensor(shift[n // 2 % 2][:, half], nmean[n // 2 % 2][:, half], rstd[:, half],
                                    ALU.mult).then_inc(rstd_ready, 1)

        def pool_l1(pool):
            g = nc.gpsimd
            g.memset(vals[:], 0.0).then_inc(l1_consts, 1)
            g.memset(ks[1][:].bitcast(F32), 0.0).then_inc(l1_consts, 1)
            for b in range(B):
                g.memset(qs[b][:, :, :, MAXAT:HW].bitcast(F32), 0.0).then_inc(l1_consts, 1)
            pool.wait_ge(l1_consts, 4)
            for ver in range(2):
                at_ = ver * HW + MAXAT
                g.memset(ks[1][:, :, :, ver, at_:at_ + 3], 1.0).then_inc(l1_consts, 1)
            g.memset(vals[:, :, :, HD:HD + 1], 1.0).then_inc(l1_consts, 1)

        def pool_l0(pool, link):
            g = nc.gpsimd
            stage = {"k": (wk_f, wk_hi, wk_lo), "q": (wq_f, wq_hi, wq_lo)}

            def weight_lo(n, s):
                full, hi, lo = stage[n]
                if s:
                    pool.wait_ge(product, made(s - 1, (n.upper(), 1, TB - 1)))
                pool.wait_ge(w_hi_ready[n], s + 1)
                g.tensor_tensor(lo[:], full[:], hi[:].bitcast(F32), ALU.subtract).then_inc(w_lo_ready[n], 1)

            weight_lo("k", 0)
            for half in range(2):
                sl = slice(half * TB, (half + 1) * TB)
                pool.wait_ge(split_hi, half + 1)
                g.tensor_tensor(xn_lo[:, sl], xn[:, sl], xn_hi[:, sl].bitcast(F32), ALU.subtract).then_inc(split_lo, 1)
            weight_lo("q", 0)
            for s in range(NS):
                for b in range(B):
                    pool.wait_ge(dve_done, dve_through(s, ("K", b, TB - 1)))
                    hi, lo = k_hi[b][:].bitcast(F32), k_lo[b][:].bitcast(F32)
                    if s or b:
                        pool.wait_ge(product, made(s, ("S", 0, 0)) if b else made(s - 1, ("S", 1, 0)))
                    link(g.tensor_tensor(ksum_t[:], hi[:, 0:2], hi[:, 2:4], ALU.add))
                    link(g.tensor_tensor(rest_of(lo)[0], lo[:, 0], lo[:, 1], ALU.add))
                    link(g.tensor_tensor(ksum_t[:, 1], ksum_t[:, 0], ksum_t[:, 1], ALU.add))
                    link(g.tensor_tensor(ksum_t[:, 0], lo[:, 2], lo[:, 3], ALU.add))
                    link(g.tensor_tensor(ksum_t[:, 0], ksum_t[:, 0], ksum[:], ALU.add))
                    g.tensor_tensor(ksum[:], ksum_t[:, 0], ksum_t[:, 1], ALU.add).then_inc(ksum_ready, 1)
                if s + 1 < NS:
                    weight_lo("k", s + 1)
                    weight_lo("q", s + 1)

        def rest_of(_):
            return [ksum[:]]

        def pool_moe(pool, l):
            g = nc.gpsimd
            pool.wait_ge(zeroed, 16 * 2 * NR)
            pool.wait_ge(slot_ready[l], 1)
            for t in range(NT):
                pool.wait_ge(scaled[l], t + 1)
                g.indirect_dma_start(sorted_x[l][:, :], bass.IndirectOffsetOnAxis(ap=slot[:, t:t + 1], axis=0),
                                     xn[:, t, :], None).then_inc(scattered[l], 16)
            if l == 0 and phases > 2:
                pool_l1(pool)
            for i in range(4):
                n = len([r for r in range(NR) if r % 4 == i])
                pool.wait_ge(yr_stored[l][i], 16 * n)
            for t in range(NT):
                g.indirect_dma_start(y[:, t, :], None, sorted_y[l][:, :],
                                     bass.IndirectOffsetOnAxis(ap=slot[:, t:t + 1], axis=0)).then_inc(gathered[l][t // TB], 16)

        def vector_program(dve):
            v = nc.vector
            count = [0]

            def link(ins):
                count[0] += 1
                ins.then_inc(dve_chain, 1)
                dve.wait_ge(dve_chain, count[0])

            def mark(ins):
                count[0] += 1
                ins.then_inc(dve_chain, 1)

            def settle():
                dve.wait_ge(dve_chain, count[0])

            dve.wait_ge(consts, 4)
            v.tensor_copy(identb[:], ident[:]).then_inc(const_casts, 1)
            for i in range(2):
                for j in range(2):
                    v.memset(same_head[i * HC:(i + 1) * HC, j * HC:(j + 1) * HC], float(i == j)).then_inc(const_casts, 1)

            def stats(src, half):
                tiles = range(half * TB, (half + 1) * TB)
                for t in tiles:
                    mark(v.bn_stats(stat[:, t, :], src[:, t, :]))
                settle()
                for t in tiles:
                    mark(v.bn_aggr(mv[:, t, :], stat[:, t, :]))
                settle()
                sl = slice(half * TB, (half + 1) * TB)
                v.tensor_scalar(var[:, sl], mv[:, sl, 1], EPS, None, ALU.add).then_inc(var_ready, 1)
                v.tensor_scalar(nmean[src is y][:, sl], mv[:, sl, 0], -1.0, None, ALU.mult).then_inc(var_ready, 1)

            def residual(p, make_y):
                for half in range(2):
                    make_y(half)
                    dve.wait_ge(y_ready, p * NT + (half + 1) * TB)
                    stats(y, half)
                for half in range(2):
                    dve.wait_ge(rstd_ready, 2 * (4 * p + 2 + half) + 1)
                    if p:
                        dve.wait_ge(x_summed, (p - 1) * NT + (half + 1) * TB)
                    for t in range(half * TB, (half + 1) * TB):
                        ins = v.scalar_tensor_tensor(x[:, t, :], y[:, t, :], rstd[:, t:t + 1], x[:, t, :],
                                                     ALU.mult, ALU.add)
                        if p == phases - 1:
                            ins.then_inc(last_summed, 1)
                        else:
                            mark(ins)
                    if p < phases - 1:
                        settle()
                        stats(x, half)

            def turn_lo(i):
                dve.wait_ge(xT_ready, i + 1)
                cols = slice(i * 256, (i + 1) * 256)
                v.tensor_tensor(xT_lo[:, :, cols], ps[i][:].rearrange("p (c n) -> p c n", c=KC),
                                xT_hi[:, :, cols].bitcast(F32), ALU.subtract).then_inc(xT_lo_ready, 1)

            for half in range(2):
                dve.wait_ge(x_loaded, 32)
                stats(x, half)
            for half in range(2):
                dve.wait_ge(xn_ready, (half + 1) * TB)
                sl = slice(half * TB, (half + 1) * TB)
                v.tensor_copy(xn_hi[:, sl], xn[:, sl]).then_inc(split_hi, 1)
            for i in range(4):
                turn_lo(i)
            dve.wait_ge(consts, N_CONSTS)
            v.tensor_copy(pick_r[:], pick[:]).then_inc(const_casts, 1)
            for b in range(B):
                v.memset(nk[b][:], 0.0).then_inc(const_casts, 1)
            dve.wait_ge(const_casts, 8)
            for s in range(NS):
                dve_slice(dve, link, s)
            dve.wait_ge(small_loaded, SMALL)

            def l0_y(b):
                dve.wait_ge(out_done, b + 1)
                for t in range(b * TB, (b + 1) * TB):
                    v.tensor_tensor(y[:, t, :], acc[b][t % TB // 2][:, t % 2 * D:(t % 2 + 1) * D], bo0[:],
                                    ALU.add).then_inc(y_ready, 1)

            residual(0, l0_y)
            for p in range(1, phases):
                make_y = dve_l1(dve, link, mark, settle) if p == 2 else dve_moe(dve, link, p // 2)
                residual(p, make_y)

        def dve_slice(dve, link, s):
            v = nc.vector

            def q_low(b, j):
                dve.wait_ge(q_hi_ready, (s * B + b) * CH + j + 1)
                v.tensor_tensor(q_lo[b][:, j], q[b][:, j], q_hi[b][:, j].bitcast(F32), ALU.subtract).then_inc(q_lo_ready, 1)

            for n in ORDER:
                kind, b, i = n
                if n not in BY_DVE:
                    continue
                pt = bank(n)
                if kind in ("K", "KVO"):
                    dve.wait_ge(act_done, act_through(s, n))
                else:
                    dve.wait_ge(product, made(s, n))
                if kind == "K":
                    if s:
                        dve.wait_ge(ksum_ready, (s - 1) * B + b + 1)
                    ins = v.scalar_tensor_tensor(k_lo[b][:, i], pt[:], 0.0, k_hi[b][:, i].bitcast(F32),
                                                 ALU.max, ALU.subtract)
                elif kind == "S":
                    ins = v.tensor_tensor(nk[b][:, :, 0:2], pt[:].rearrange("p (j m) -> p j m", j=CH)[:, :, 0:2],
                                          same_head[:, 0:P:HC].unsqueeze(1).to_broadcast([P, CH, 2]), ALU.mult)
                elif kind == "KV":
                    ins = v.tensor_tensor(kv[b][:], pt[:].rearrange("p (j m) -> p j m", j=CH),
                                          same_head[:].unsqueeze(1).to_broadcast([P, CH, P]), ALU.mult)
                elif kind == "N":
                    v.tensor_scalar(rec[:], pt[:], 1e-6, None, ALU.max).then_inc(dve_done, 1)
                    dve.wait_ge(dve_done, dve_through(s, n))
                    link(v.reciprocal(rec[:], rec[:]))
                    link(v.tensor_copy(rec_hi[b][:], rec[:]))
                    v.tensor_tensor(rec_lo[b][:], rec[:], rec_hi[b][:].bitcast(F32),
                                    ALU.subtract).then_inc(rec_ready, 1)
                    continue
                elif kind == "KVO":
                    ins = v.tensor_tensor(kvo_lo[b][:, 2 * i:2 * i + 2], pt[:].rearrange("p (j m) -> p j m", j=2),
                                          kvo_hi[b][:, 2 * i:2 * i + 2].bitcast(F32), ALU.subtract)
                else:
                    ins = v.tensor_tensor(q[b][:, i], q[b][:, i], pt[:], ALU.mult)
                ins.then_inc(dve_done, 1)
                if kind == "BC":
                    if i:
                        q_low(b, i - 1)
                    if i == CH - 1:
                        q_low(b, i)

        def dve_moe(dve, link, l):
            v = nc.vector
            dve.wait_ge(logits_made[l], 1)
            v.tensor_copy(lgT[:], ps[6][:, 0:2 * P]).then_inc(lgT_ready[l], 1)
            dve.wait_ge(logits_made[l], 2)
            v.tensor_copy(lg[:].rearrange("p (j i) e -> p i j e", i=2),
                          ps[6][:, 2 * P:4 * P].rearrange("p (i j m) -> p i j m", i=2, j=4)[:, :, :, 0:E]
                          ).then_inc(logits_read[l], 1)
            dve.wait_ge(logits_read[l], 1)
            v.tensor_reduce(best[:], lg[:], AX.X, ALU.max).then_inc(best_ready[l], 1)
            dve.wait_ge(best_ready[l], 1)
            link(v.tensor_tensor(hot_f[:], lg[:], best[:].unsqueeze(2).to_broadcast([P, NT, E]), ALU.is_ge))
            link(v.tensor_tensor(hot_f[:], hot_f[:], rank_key[:].unsqueeze(1).to_broadcast([P, NT, E]), ALU.mult))
            link(v.tensor_reduce(last_max[:], hot_f[:], AX.X, ALU.max))
            link(v.tensor_tensor(hot_f[:], hot_f[:], last_max[:].unsqueeze(2).to_broadcast([P, NT, E]), ALU.is_equal))
            v.tensor_copy(hot[:], hot_f[:]).then_inc(hot_ready[l], 1)
            dve.wait_ge(rank_made[l], 1)
            counts = ps[7][:, NT * E:(NT + 1) * E]
            link(v.tensor_copy(place[:], ps[7][:, 0:NT * E].rearrange("p (t e) -> p t e", e=E)))
            v.tensor_copy(cnt[:], counts).then_inc(rank_read[l], 1)
            dve.wait_ge(rank_read[l], 1)
            link(v.tensor_tensor(cmp[:], cnt[:].unsqueeze(2).to_broadcast([P, E, NT]),
                                 rows_at[:].unsqueeze(1).to_broadcast([P, E, NT]), ALU.is_gt))
            link(v.tensor_reduce(tiles_of[:], cmp[:], AX.X, ALU.add))
            link(v.tensor_tensor(cmp[:], up_to[:], tiles_of[:].unsqueeze(1).to_broadcast([P, E, E]), ALU.mult))
            link(v.tensor_reduce(tiles_end[:], cmp[:], AX.X, ALU.add))
            link(v.tensor_tensor(row0[:], tiles_end[:], tiles_of[:], ALU.subtract))
            link(v.tensor_scalar(row0[:], row0[:], float(P), None, ALU.mult))
            link(v.tensor_tensor(place[:], place[:], row0[:].unsqueeze(1).to_broadcast([P, NT, E]), ALU.add))
            link(v.tensor_tensor(place[:], place[:], hot_f[:], ALU.mult))
            link(v.tensor_reduce(slot_f[:], place[:], AX.X, ALU.add))
            v.tensor_copy(slot[:], slot_f[:]).then_inc(slot_ready[l], 1)
            dve.wait_ge(score_ready[l], 1)
            for t in range(NT):
                v.tensor_scalar(xn[:, t, :], xn[:, t, :], score[:, t:t + 1], None, ALU.mult).then_inc(scaled[l], 1)
            link(v.tensor_tensor(past[:], tile_no[:].unsqueeze(2).to_broadcast([P, 16, E]),
                                 tiles_end[:].unsqueeze(1).to_broadcast([P, 16, E]), ALU.is_ge))
            link(v.tensor_reduce(expert_f[:], past[:], AX.X, ALU.add))
            link(v.tensor_scalar(expert_f[:], expert_f[:], float(E - 1), None, ALU.min))
            v.tensor_copy(expert[:], expert_f[:]).then_inc(expert_ready[l], 1)
            for i in range(NU + 2):
                if i < NU:
                    dve.wait_ge(silu_ready[l], i + 1)
                    if i >= 2:
                        dve.wait_ge(hT_made[l], i - 1)
                    v.tensor_tensor(h[i % 2][:], sg[i % 2][:], ps[2 + i % 2][:, F:2 * F], ALU.mult).then_inc(h_ready[l], 1)
                if i >= 2:
                    u = i - 2
                    dve.wait_ge(d_made[l], u + 1)
                    r = routed(u)
                    if r is not None and r >= 4:
                        dve.wait_ge(yr_stored[l][r % 4], 16 * (r // 4))
                    dst = y_shared[:, shared_tile(u), :] if r is None else yr[r % 4][:]
                    v.tensor_copy(dst, ps[6 + u % 2][:, 0:D]).then_inc(yr_ready[l], 1)
            dve.wait_ge(yr_ready[l], NU)

            def moe_y(half):
                dve.wait_ge(gathered[l][half], 16 * TB)
                for t in range(half * TB, (half + 1) * TB):
                    v.tensor_tensor(y[:, t, :], y[:, t, :], y_shared[:, t, :], ALU.add).then_inc(y_ready, 1)

            return moe_y

        def scalar_program(act):
            def turn(p, i):
                act.wait_ge(xT_made, 4 * p + i + 1)
                cols = slice(i * 256, (i + 1) * 256)
                dst = xT_hi if p == 0 else xT
                nc.scalar.activation(dst[:, :, cols], ps[i][:].rearrange("p (c n) -> p c n", c=KC),
                                     ACT.Copy).then_inc(xT_ready, 1)

            def weight_hi(n, s):
                full, hi = {"k": (wk_f, wk_hi), "q": (wq_f, wq_hi)}[n]
                if s:
                    act.wait_ge(product, made(s - 1, (n.upper(), 1, TB - 1)))
                    act.wait_ge(w_lo_ready[n], s)
                act.wait_ge(w_loaded[n], 16 * (s + 1))
                nc.scalar.activation(hi[:], full[:], ACT.Copy).then_inc(w_hi_ready[n], 1)

            def normalise(p):
                for half in range(2):
                    act.wait_ge(rstd_ready, 2 * (4 * p + half + 1))
                    for t in range(half * TB, (half + 1) * TB):
                        nc.scalar.activation(xn[:, t, :], x[:, t, :], ACT.Identity, bias=shift[0][:, t:t + 1],
                                             scale=rstd[:, t:t + 1]).then_inc(xn_ready, 1)
                    if p:
                        turn(p, 2 * half)
                        turn(p, 2 * half + 1)

            def complete(p):
                for t in range(NT):
                    if p == phases - 1:
                        act.wait_ge(last_summed, t + 1)
                        act.wait_ge(rstd_ready, 2 * (4 * p + 2 + t // TB + 1))
                    nc.scalar.activation(x[:, t, :], x[:, t, :], ACT.Identity,
                                         bias=shift[1][:, t:t + 1]).then_inc(x_summed, 1)

            normalise(0)
            weight_hi("k", 0)
            weight_hi("q", 0)
            for i in range(4):
                turn(0, i)
            for s in range(NS):
                for n in ORDER:
                    kind, b, i = n
                    pt = bank(n)
                    if n in BY_ACT:
                        act.wait_ge(product, made(s, n))
                        if kind == "K":
                            if s:
                                act.wait_ge(ksum_ready, (s - 1) * B + b + 1)
                            nc.scalar.activation(k_hi[b][:, i], pt[:], ACT.Relu).then_inc(act_done, 1)
                        elif kind == "G":
                            nc.scalar.activation(kx[:, i], pt[:], ACT.Copy).then_inc(act_done, 1)
                        elif kind == "Q":
                            if s:
                                act.wait_ge(q_lo_ready, ((s - 1) * B + b) * CH + i + 1)
                            nc.scalar.activation(q[b][:, i], pt[:], ACT.Relu).then_inc(act_done, 1)
                        else:
                            nc.scalar.activation(kvo_hi[b][:, 2 * i:2 * i + 2],
                                                 pt[:].rearrange("p (j m) -> p j m", j=2), ACT.Copy).then_inc(act_done, 1)
                    elif kind == "BC":
                        act.wait_ge(dve_done, dve_through(s, n))
                        nc.scalar.activation(q_hi[b][:, i], q[b][:, i], ACT.Copy).then_inc(q_hi_ready, 1)
                    if s + 1 < NS and n == ("K", 1, TB - 1):
                        weight_hi("k", s + 1)
                    if s + 1 < NS and n == ("Q", 1, CH - 1):
                        weight_hi("q", s + 1)
            for p in range(1, phases):
                normalise(p)
                complete(p - 1)
                if p == 2:
                    act_l1(act)
                else:
                    act_moe(act, p // 2)
                if p == 1 and phases > 2:
                    act.wait_ge(gu_made[0], NU)
                    nc.scalar.activation(ks0[:].bitcast(F32).rearrange("p t g v n -> p (t g v n)").rearrange(
                        "p (r d) -> p r d", d=D), zeros[:].unsqueeze(1).to_broadcast([P, TB * NKV * P // D, D]),
                        ACT.Copy).then_inc(ks0_consts, 1)
                    act.wait_ge(ks0_consts, 1)
                    for ver in range(2):
                        at_ = ver * HW + MAXAT
                        nc.scalar.activation(ks0[:, :, :, ver, at_:at_ + 3], ones[:, 0:TB * NKV * 3].rearrange(
                            "p (t g i) -> p t g i", t=TB, g=NKV), ACT.Copy).then_inc(ks0_consts, 1)
            complete(phases - 1)

        def act_moe(act, l):
            act.wait_ge(best_ready[l], 1)
            nc.scalar.activation(score[:], best[:], ACT.Sigmoid).then_inc(score_ready[l], 1)
            for i in range(-2, NU + 1):
                if 0 <= i < NU:
                    act.wait_ge(gu_made[l], i + 1)
                    if i >= 2:
                        act.wait_ge(h_ready[l], i - 1)
                    nc.scalar.activation(sg[i % 2][:], ps[2 + i % 2][:, 0:F], ACT.Silu).then_inc(silu_ready[l], 1)
                if 1 <= i:
                    u = i - 1
                    act.wait_ge(hT_made[l], u + 1)
                    if u >= 2:
                        act.wait_ge(d_made[l], u - 1)
                    nc.scalar.activation(hT[u % 2][:], ps[4 + u % 2][:, 0:F].rearrange("p (c n) -> p c n", c=FC),
                                         ACT.Copy).then_inc(hT_ready[l], 1)
                r = i + 2 - NSF
                if 0 <= r < NR:
                    act.wait_ge(xgT_made[l], r + 1)
                    if r >= 2:
                        act.wait_ge(gu_made[l], i + 1)
                    nc.scalar.activation(xgT[r % 2][:], ps[r % 2][:, 0:D].rearrange("p (c n) -> p c n", c=KC),
                                         ACT.Copy).then_inc(xgT_ready[l], 1)

        def tensor_program(pe):
            mm = nc.tensor.matmul

            def turn_x(p):
                if p == 0:
                    pe.wait_ge(consts, 4)
                for i in range(4):
                    for t in (2 * i, 2 * i + 1):
                        pe.wait_ge(xn_ready, NT * p + t + 1)
                        for c in range(KC):
                            last = nc.tensor.transpose(ps[i][:, c * 256 + t % 2 * P:c * 256 + (t % 2 + 1) * P],
                                                       xn[:, t, c * P:(c + 1) * P], ident[:])
                    last.then_inc(xT_made, 1)

            turn_x(0)
            pe.wait_ge(xT_lo_ready, 4)
            for s in range(NS):
                pe_slice(pe, s)
            for p in range(1, phases):
                turn_x(p)
                if p == 2:
                    pe_l1(pe)
                else:
                    pe_moe(pe, p // 2)

        def pe_slice(pe, s):
            mm = nc.tensor.matmul

            def out_mm(b, t, j, passes):
                o = acc[b][t // 2][:, t % 2 * D:(t % 2 + 1) * D]
                tok = slice(t * P, (t + 1) * P)
                return split_mm(o, (q_hi[b][:, j, tok], q_lo[b][:, j, tok]), (kvo_hi[b][:, j], kvo_lo[b][:, j]),
                                start=(s == 0 and j == 0 and t % 2 == 0), stop=(s == NS - 1 and j == CH - 1),
                                skip_group_check=True)

            for pos, n in enumerate(ORDER):
                kind, b, i = n
                prev = pos - BANKS if pos >= BANKS else max(q_ for q_ in range(NP_) if q_ % BANKS == pos)
                ps_ = s if pos >= BANKS else s - 1
                if ps_ >= 0:
                    pn = ORDER[prev]
                    if pn in BY_DVE:
                        pe.wait_ge(dve_done, dve_through(ps_, pn))
                    else:
                        pe.wait_ge(act_done, act_through(ps_, pn))
                pt = bank(n)
                if kind == "K":
                    if (b, i) == (0, 0):
                        pe.wait_ge(w_lo_ready["k"], s + 1)
                    tok = slice((b * TB + i) * P, (b * TB + i + 1) * P)
                    for c in range(KC):
                        last = split_mm(pt[:], (xT_hi[:, c, tok], xT_lo[:, c, tok]), (wk_hi[:, c], wk_lo[:, c]),
                                        c == 0, c == KC - 1)
                elif kind == "Q":
                    if (b, i) == (0, 0):
                        pe.wait_ge(w_lo_ready["q"], s + 1)
                    ch, tok = slice(i * P, (i + 1) * P), slice(b * S, (b + 1) * S)
                    for c in range(KC):
                        last = split_mm(pt[:], (wq_hi[:, c, ch], wq_lo[:, c, ch]), (xT_hi[:, c, tok], xT_lo[:, c, tok]),
                                        c == 0, c == KC - 1)
                elif kind == "G":
                    if s == 0:
                        pe.wait_ge(split_lo, b + 1)
                    ch = slice(i * P, (i + 1) * P)
                    for t in range(TB):
                        pe.wait_ge(dve_done, dve_through(s, ("K", b, t)))
                        last = split_mm(pt[:], (xn_hi[:, b * TB + t, ch], xn_lo[:, b * TB + t, ch]),
                                        (k_hi[b][:, t], k_lo[b][:, t]), t == 0, t == TB - 1)
                elif kind == "S":
                    pe.wait_ge(ksum_ready, s * B + b + 1)
                    for j in range(CH):
                        last = mm(pt[:, j * P:(j + 1) * P], ksum[:, j * P:(j + 1) * P], ones[:], start=True, stop=True)
                elif kind == "KV":
                    pe.wait_ge(w_loaded["v"], 16 * (s + 1))
                    pe.wait_ge(act_done, act_through(s, ("G", b, KC - 1)))
                    for j in range(CH):
                        ch = slice(j * P, (j + 1) * P)
                        for c in range(KC):
                            last = mm(pt[:, ch], wv_f[:, c, ch], kx[:, c, ch], start=(c == 0), stop=(c == KC - 1))
                elif kind == "N":
                    pe.wait_ge(dve_done, dve_through(s, ("S", b, 0)))
                    pe.wait_ge(act_done, act_through(s, ("Q", b, CH - 1)))
                    for j in range(CH):
                        last = mm(pt[j * 32:(j + 1) * 32, :], nk[b][:, j], q[b][:, j], start=True, stop=True)
                elif kind == "KVO":
                    pe.wait_ge(w_loaded["o"], 16 * (s + 1))
                    pe.wait_ge(dve_done, dve_through(s, ("KV", b, 0)))
                    for j in (2 * i, 2 * i + 1):
                        last = mm(pt[:, j % 2 * D:(j % 2 + 1) * D], kv[b][:, j], wo_f[:, j], start=True, stop=True)
                else:
                    if b:
                        if i == 0:
                            pe.wait_ge(q_lo_ready, (s * B) * CH + CH)
                            pe.wait_ge(dve_done, dve_through(s, ("KVO", 0, 1)))
                        for j in range(CH):
                            last = out_mm(0, i, j, 3)
                        if s == NS - 1 and i == TB - 1:
                            last.then_inc(out_done, 1)
                    pe.wait_ge(rec_ready, s * B + b + 1)
                    mm(pt[:], pick_r[:, i], rec_hi[b][:], start=True, stop=False)
                    last = mm(pt[:], pick_r[:, i], rec_lo[b][:], start=False, stop=True)
                last.then_inc(product, 1)
            pe.wait_ge(dve_done, dve_through(s, ("KVO", 1, 1)))
            for j in range(CH):
                pe.wait_ge(q_lo_ready, (s * B + 1) * CH + j + 1)
                for t in range(TB):
                    last = out_mm(1, t, j, 3)
            if s == NS - 1:
                last.then_inc(out_done, 1)

        def pe_moe(pe, l):
            mm = nc.tensor.matmul
            if l == 0:
                pe.wait_ge(small_loaded, SMALL)
            pe.wait_ge(y_ready, (2 * l + 1) * NT)
            for c in range(KC):
                for j in range(4):
                    pe.wait_ge(xT_ready, 4 * (2 * l + 1) + j + 1)
                    last = mm(ps[6][j * 32:(j + 1) * 32, 0:2 * P], router[l][:, c], xT[:, c, j * 2 * P:(j + 1) * 2 * P],
                              start=(c == 0), stop=(c == KC - 1), skip_group_check=True)
            last.then_inc(logits_made[l], 1)
            pe.wait_ge(lgT_ready[l], 1)
            for i in range(2):
                last = nc.tensor.transpose(ps[6][:, (2 + i) * P:(3 + i) * P], lgT[:, i * P:(i + 1) * P], ident[:])
            last.then_inc(logits_made[l], 1)

            def ranks():
                pe.wait_ge(hot_ready[l], 1)
                for t in range(NT):
                    o = ps[7][:, t * E:(t + 1) * E]
                    for j in range(t):
                        mm(o, onesb[:], hot[:, j], start=(j == 0), stop=False)
                    mm(o, below[:], hot[:, t], start=(t == 0), stop=True)
                for j in range(NT):
                    last = mm(ps[7][:, NT * E:(NT + 1) * E], onesb[:], hot[:, j], start=(j == 0), stop=(j == NT - 1))
                last.then_inc(rank_made[l], 1)

            def gate_up(u):
                r = routed(u)
                if u >= 2:
                    pe.wait_ge(h_ready[l], u - 1)
                if r is None:
                    if u == 0:
                        pe.wait_ge(shared_w[l], 48)
                    t = shared_tile(u)
                    for c in range(KC):
                        last = mm(ps[2 + u % 2][:], xT[:, c, t * P:(t + 1) * P], shared_gu[:, c],
                                  start=(c == 0), stop=(c == KC - 1))
                else:
                    if r == 0:
                        pe.wait_ge(moe_w[l], 16 * 3 * E)
                    pe.wait_ge(xgT_ready[l], r + 1)
                    for c in range(KC):
                        last = mm(ps[2 + u % 2][:], xgT[r % 2][:, c], w_gu[:, bass.ds(experts[r], 1), c, :],
                                  start=(c == 0), stop=(c == KC - 1))
                last.then_inc(gu_made[l], 1)

            def turn_h(u):
                pe.wait_ge(h_ready[l], u + 1)
                if u >= 2:
                    pe.wait_ge(hT_ready[l], u - 1)
                for c in range(FC):
                    last = nc.tensor.transpose(ps[4 + u % 2][:, c * P:(c + 1) * P], h[u % 2][:, c * P:(c + 1) * P], ident[:])
                last.then_inc(hT_made[l], 1)

            def turn_rows(r):
                pe.wait_ge(xg_loaded[l][r % 4], 16 * (r // 4 + 1))
                if r >= 2:
                    pe.wait_ge(xgT_ready[l], r - 1)
                for c in range(KC):
                    last = nc.tensor.transpose(ps[r % 2][:, c * P:(c + 1) * P], xg[r % 4][:, c * P:(c + 1) * P], ident[:])
                last.then_inc(xgT_made[l], 1)

            def down(u):
                r = routed(u)
                pe.wait_ge(hT_ready[l], u + 1)
                if u == 0:
                    pe.wait_ge(logits_read[l], 1)
                elif u == 1:
                    pe.wait_ge(rank_read[l], 1)
                else:
                    pe.wait_ge(yr_ready[l], u - 1)
                for c in range(FC):
                    w = shared_d[:, c] if r is None else w_d[:, bass.ds(experts[r], 1), c, :]
                    last = mm(ps[6 + u % 2][:, 0:D], hT[u % 2][:, c], w, start=(c == 0), stop=(c == FC - 1))
                last.then_inc(d_made[l], 1)

            experts = {}
            for i in range(NU + 2):
                if i == 0:
                    ranks()
                if i < NU:
                    gate_up(i)
                if 1 <= i <= NU:
                    turn_h(i - 1)
                r = i + 2 - NSF
                if 0 <= r < NR:
                    if r == 0:
                        pe.wait_ge(expert_ready[l], 1)
                        for k in range(NR):
                            experts[k] = pe.value_load(expert[0:1, k:k + 1], min_val=0, max_val=E - 1)
                    turn_rows(r)
                if i >= 2:
                    down(i - 2)

        STEPS = NG * TB
        LAG = 7
        K1_AT = (15, 16, 19, 20, 23, 24, 27, 28)

        def turns_at(c):
            items = []
            if c < TB:
                items.append(("k", 0, TB + c))
            if c in K1_AT:
                items.append(("k", 1, K1_AT.index(c)))
            if c % TB == 0 and c // TB + 1 < NG:
                items.append(("q1", 0, c // TB + 1))
            if c % TB == 1 and 0 <= (c - 5) // TB < NG:
                items.append(("q2", 0, (c - 5) // TB))
            if c % TB == 2 and 0 <= (c - 14) // TB < NG:
                items.append(("o", 0, (c - 14) // TB))
            return items

        END = STEPS + 12
        FIRST = [("k", 0, t) for t in range(TB)] + [("q1", 0, 0)]
        TURNS = FIRST + [x_ for c_ in range(END) for x_ in turns_at(c_)]
        BY_READER = {"act": [x_ for x_ in TURNS if x_[0] != "o"], "dve": [x_ for x_ in TURNS if x_[0] == "o"]}

        def turn_no(what):
            return TURNS.index(what) + 1

        def wait_read(eng, what):
            if what[0] == "o":
                eng.wait_ge(att_ready, BY_READER["dve"].index(what) + 1)
            else:
                eng.wait_ge(turn_copied, BY_READER["act"].index(what) + 1)

        def act_l1(act):
            def copy_turn(what):
                kind, b, i = what
                act.wait_ge(turned, turn_no(what))
                bank7 = ps[7].bitcast(BF16)
                if kind == "k":
                    half, t = i // TB, i % TB
                    dst, src = kT[b][:, half * 4:half * 4 + 4, :, t * P:(t + 1) * P], bank7.rearrange(
                        "p (g w n) -> p g w n", g=4, w=2)
                else:
                    dst, src = (qT1 if kind == "q1" else qT2)[i % 2][:], bank7.rearrange("p (i n) -> p i n", i=2)
                nc.scalar.activation(dst, src, ACT.Copy).then_inc(turn_copied, 1)

            for i, (at_, n) in enumerate(((0, 3), (3, 2), (5, 1))):
                act.wait_ge(part_ready, i + 1)
                for t in range(TB):
                    stack_queries(nc.scalar, 0, t, i, at_, n).then_inc(q_stacked[0], 1)
            for what in FIRST:
                copy_turn(what)
            for c in range(END):
                d = c - LAG
                if 0 <= d < STEPS:
                    if d >= 3:
                        act.wait_ge(av_done, d - 2)
                for j in range(GH):
                    if j == 2:
                        for what in turns_at(c):
                            if what[0] != "o":
                                copy_turn(what)
                    if 0 <= d < STEPS:
                        act.wait_ge(s2_made, d * GH + j + 1)
                        nc.scalar.activation(pr[d % 3][:, j], ps[4 + j % 2], ACT.Exp, scale=SCALE).then_inc(exp_ready, 1)
            for t in range(NT):
                act.wait_ge(attT_made, t + 1)
                nc.scalar.activation(xT[:, :, t * P:(t + 1) * P],
                                     ps[t % 4][:, 0:D].rearrange("p (c n) -> p c n", c=KC), ACT.Copy).then_inc(attT_ready, 1)

        def stack_queries(eng, b, t, i, at_, n):
            dst = qs[b][:, t, :, at_ * HD:(at_ + n) * HD].rearrange("p h (n d) -> p h n d", d=HD)
            src = part[b][i][:, t, 0:NQ * HD].rearrange("p (h d) -> p h d", d=HD).unsqueeze(2).to_broadcast([P, NQ, n, HD])
            if eng is nc.scalar:
                return eng.activation(dst, src, ACT.Copy)
            return eng.tensor_copy(dst, src)

        def stack_keys(eng, b, ver, at_, i):
            return eng.tensor_copy(ks[b][:, :, :, ver, ver * HW + at_ * HD:ver * HW + (at_ + 1) * HD],
                                   part[b][i][:, :, NQ * HD:].rearrange("p t (g d) -> p t g d", d=HD))

        KEY_PARTS = (0, 1, 2, 0, 1, 0)

        def pool_l1_loop(pool, link):
            g = nc.gpsimd
            b = 1

            def split(i, t):
                src = qkv[:, b * TB + t, 0:KEND] if i == 0 else rest[b][i - 1][:, t]
                link(g.tensor_copy(part[b][i][:, t], src))
                if i < 2:
                    link(g.tensor_tensor(rest[b][i][:, t], src, part[b][i][:, t], ALU.subtract))

            work = [lambda i=i, t=t: split(i, t) for i in range(3) for t in range(TB)]
            work += [lambda ver=ver, at_=at_, i=i: stack_keys(g, b, ver, at_, i).then_inc(k_stacked[b], 1)
                     for ver in range(2) for at_, i in enumerate(KEY_PARTS)]
            work += [lambda t=t, i=i, at_=at_, n=n: stack_queries(g, b, t, i, at_, n).then_inc(q_stacked[b], 1)
                     for i, (at_, n) in enumerate(((0, 3), (3, 2), (5, 1))) for t in range(TB)]
            pool.wait_ge(qkv_ready, NT)
            for n in range(NG):
                for _ in range(12 if n == 0 else 6):
                    if work:
                        work.pop(0)()
                bb, gg = n // NKV, n % NKV
                pool.wait_ge(max_read, (n + 1) * TB * 2)
                to = [qs[bb][:, :, gg * GH:(gg + 1) * GH, MAXAT + i] for i in range(3)]
                m = mx[n % 2]
                link(g.tensor_copy(to[0], m[:]))
                link(g.tensor_tensor(mr[0][:], m[:], to[0], ALU.subtract))
                link(g.tensor_copy(to[1], mr[0][:]))
                link(g.tensor_tensor(mr[1][:], mr[0][:], to[1], ALU.subtract))
                g.tensor_copy(to[2], mr[1][:]).then_inc(max_ready, 1)

        def pe_l1(pe):
            mm = nc.tensor.matmul
            pe.wait_ge(l1_loaded, 48)
            for t in range(NT):
                pe.wait_ge(xT_ready, 4 * 2 + t // 2 + 1)
                if t >= 3:
                    pe.wait_ge(qkv_ready, t - 2)
                for c in range(KC):
                    last = mm(ps[4 + t % 3][:, 0:QKV], xT[:, c, t * P:(t + 1) * P], wqkv[:, c],
                              start=(c == 0), stop=(c == KC - 1))
                last.then_inc(qkv_made, 1)

            def turn(what):
                n = TURNS.index(what)
                if n:
                    wait_read(pe, TURNS[n - 1])
                kind, b, i = what
                if kind == "o":
                    pe.wait_ge(oT_ready, i + 1)
                    for t in range(TB):
                        last = nc.tensor.transpose(ps[7][:, t * P:(t + 1) * P], oT[:, t * P:(t + 1) * P], ident[:])
                elif kind == "k":
                    pe.wait_ge(k_stacked[b], 2 * len(KEY_PARTS))
                    half, t = i // TB, i % TB
                    for k in range(8):
                        last = nc.tensor.transpose(ps[7].bitcast(BF16)[:, k * P:(k + 1) * P],
                                                   ks[b][:, t, half * 4 + k // 2, k % 2, :], identb[:])
                else:
                    b, g = i // NKV, i % NKV
                    pe.wait_ge(q_stacked[b], 3 * TB)
                    if kind == "q2":
                        pe.wait_ge(max_ready, i + 1)
                    for k in range(2):
                        for t in range(TB):
                            last = nc.tensor.transpose(
                                ps[7].bitcast(BF16)[:, (k * TB + t) * P:(k * TB + t + 1) * P],
                                qs[b][:, t, GH * g + 2 * k:GH * g + 2 * k + 2, :].rearrange("p h w -> p (h w)"), identb[:])
                last.then_inc(turned, 1)

            def scores1(c, i):
                n, t = c // TB, c % TB
                b, g = n // NKV, n % NKV
                if 2 * c + i >= 2:
                    pe.wait_ge(max_read, 2 * c + i - 1)
                if t == 0 and i == 0:
                    wait_read(pe, ("q1", 0, n))
                    if g in (0, NKV // 2):
                        wait_read(pe, ("k", b, TB - 1 if g == 0 else 2 * TB - 1))
                for ver in range(2):
                    last = mm(ps[2 * i + ver], qT1[n % 2][:, i, t * P:(t + 1) * P], kT[b][:, g, ver, :],
                              start=True, stop=True)
                last.then_inc(s1_made, 1)

            def scores2(d, i):
                n, kc = d // TB, d % TB
                b, g = n // NKV, n % NKV
                if kc == 0 and i == 0:
                    wait_read(pe, ("q2", 0, n))
                for ver in range(2):
                    k = d * GH + 2 * i + ver
                    if k >= 2:
                        pe.wait_ge(exp_ready, k - 1)
                    mm(ps[4 + ver], kT[b][:, g, ver, kc * P:(kc + 1) * P], qT2[n % 2][:, i, :], start=True,
                       stop=True).then_inc(s2_made, 1)

            def weigh(d):
                n, kc = d // TB, d % TB
                b, g = n // NKV, n % NKV
                pe.wait_ge(exp_ready, (d + 1) * GH)
                if kc == 0 and n:
                    pe.wait_ge(oT_ready, n)
                for j in range(GH):
                    last = mm(ps[6][j * VW:(j + 1) * VW, :], vals[:, b * TB + kc, g, :], pr[d % 3][:, j],
                              start=(kc == 0), stop=(kc == TB - 1), skip_group_check=True)
                last.then_inc(av_done, 1)

            for what in FIRST:
                turn(what)
            pe.wait_ge(qkv_ready, NT)
            for c in range(END):
                d = c - LAG
                if c < STEPS:
                    scores1(c, 0)
                if 0 <= d < STEPS:
                    scores2(d, 0)
                for what in turns_at(c):
                    turn(what)
                if 0 <= d - 1 < STEPS and (d - 1) % TB:
                    weigh(d - 1)
                if c < STEPS:
                    scores1(c, 1)
                if 0 <= d < STEPS:
                    scores2(d, 1)
                if 0 <= d - 1 < STEPS and (d - 1) % TB == 0:
                    weigh(d - 1)
            for t in range(NT + 1):
                if t < NT:
                    pe.wait_ge(att_ready, NG)
                    if t >= 4:
                        pe.wait_ge(attT_ready, t - 3)
                    for c in range(KC):
                        last = nc.tensor.transpose(ps[t % 4][:, c * P:(c + 1) * P], xn[:, t, c * P:(c + 1) * P], ident[:])
                    last.then_inc(attT_made, 1)
                if t:
                    u = t - 1
                    pe.wait_ge(attT_ready, u + 1)
                    if u >= 4:
                        pe.wait_ge(y_ready, 2 * NT + u - 3)
                    for c in range(KC):
                        last = mm(ps[4 + u % 4][:, 0:D], xT[:, c, u * P:(u + 1) * P], wo1[:, c],
                                  start=(c == 0), stop=(c == KC - 1))
                    last.then_inc(proj_made, 1)

        def dve_l1(dve, link, mark, settle):
            v = nc.vector
            dve.wait_ge(l1_loaded, 48)

            def take(t):
                dve.wait_ge(qkv_made, t + 1)
                v.tensor_tensor(qkv[:, t, :], ps[4 + t % 3][:, 0:QKV], bqkv[:], ALU.add).then_inc(qkv_ready, 1)

            for t in range(TB):
                take(t)
            dve.wait_ge(qkv_ready, TB)
            dve.wait_ge(l1_consts, 7)
            dve.wait_ge(ks0_consts, 3)
            src = qkv[:, 0:TB, 0:KEND]
            for i in range(3):
                v.tensor_copy(part[0][i][:], src).then_inc(part_ready, 1)
                dve.wait_ge(part_ready, i + 1)
                if i < 2:
                    link(v.tensor_tensor(rest[0][i][:], src, part[0][i][:], ALU.subtract))
                    src = rest[0][i][:]
                take(TB + i)
            take(NT - 1)
            for ver in range(2):
                for at_, i in enumerate(KEY_PARTS):
                    stack_keys(v, 0, ver, at_, i).then_inc(k_stacked[0], 1)
            dve.wait_ge(qkv_ready, NT)
            mark(v.tensor_copy(vals[:, :, :, 0:HD], qkv[:, :, KEND:QKV].rearrange("p t (g d) -> p t g d", d=HD)))
            settle()

            def maximum(c, i):
                n, t = c // TB, c % TB
                dve.wait_ge(s1_made, 2 * c + i + 1)
                if t == 0 and n >= 2:
                    dve.wait_ge(max_ready, n - 1)
                v.tensor_reduce(mx[n % 2][:, t, 2 * i:2 * i + 2], psum[:, i * 1024:(i + 1) * 1024].rearrange(
                    "p (h n) -> p h n", h=2), AX.X, ALU.max, negate=True).then_inc(max_read, 1)

            def outputs(n):
                b, g = n // NKV, n % NKV
                dve.wait_ge(turned, turn_no(("o", 0, n)))
                o = ps[7].rearrange("p (t h w) -> p t h w", t=TB, h=GH)
                link(v.reciprocal(dn[:], o[:, :, :, HD]))
                for t in range(TB):
                    ins = v.tensor_tensor(
                        xn[:, b * TB + t, g * GH * HD:(g + 1) * GH * HD].rearrange("p (h d) -> p h d", d=HD),
                        o[:, t, :, 0:HD], dn[:, t, :].unsqueeze(2).to_broadcast([P, GH, HD]), ALU.mult)
                    if t < TB - 1:
                        mark(ins)
                    else:
                        ins.then_inc(att_ready, 1)

            for c in range(END):
                if c % TB == 0 and c >= 12 and (c - 12) // TB < NG:
                    n = (c - 12) // TB
                    dve.wait_ge(av_done, (n + 1) * TB)
                    v.tensor_copy(oT[:], ps[6]).then_inc(oT_ready, 1)
                if c < STEPS:
                    maximum(c, 0)
                if c % TB == 3 and 0 <= (c - 15) // TB < NG:
                    outputs((c - 15) // TB)
                if c < STEPS:
                    maximum(c, 1)

            def l1_y(half):
                for t in range(half * TB, (half + 1) * TB):
                    dve.wait_ge(proj_made, t + 1)
                    v.tensor_tensor(y[:, t, :], ps[4 + t % 4][:, 0:D], bo1[:], ALU.add).then_inc(y_ready, 1)

            return l1_y

        @block.sync
        def _(eng):
            sync_program(eng)


        @block.gpsimd
        def _(eng):
            gpsimd_program(eng)


        @block.vector
        def _(eng):
            vector_program(eng)


        @block.scalar
        def _(eng):
            scalar_program(eng)


        @block.tensor
        def _(eng):
            tensor_program(eng)


_INS = ['L0_attn_hidden_states', 'L0_attn_Wq', 'L0_attn_Wk', 'L0_attn_Wv', 'L0_attn_Wo', 'L0_attn_bo',
        'L0_ffn_router_w', 'L0_ffn_gate_w', 'L0_ffn_up_w', 'L0_ffn_down_w', 'L0_ffn_shared_gate_w',
        'L0_ffn_shared_up_w', 'L0_ffn_shared_down_w', 'L1_attn_Wqkv', 'L1_attn_bqkv', 'L1_attn_Wo', 'L1_attn_bo',
        'L1_ffn_router_w', 'L1_ffn_gate_w', 'L1_ffn_up_w', 'L1_ffn_down_w', 'L1_ffn_shared_gate_w',
        'L1_ffn_shared_up_w', 'L1_ffn_shared_down_w']


def kernel(**inputs):
    import numpy as np
    import concourse.bacc as bacc
    from concourse.bass_utils import run_bass_kernel_spmd

    nc = bacc.Bacc("TRN2", target_bir_lowering=False, num_devices=1)
    arrays, args = {}, {}
    for name in _INS:
        arr = np.ascontiguousarray(inputs[name])
        arrays[f"in_{name}"] = arr
        args[name] = nc.dram_tensor(f"in_{name}", arr.shape, mybir.dt.from_np(arr.dtype), kind="ExternalInput").ap()
    out = nc.dram_tensor("out_x", (B, S, D), F32, kind="ExternalOutput").ap()
    build(nc, args, out)
    r = run_bass_kernel_spmd(nc, [arrays], core_ids=[0])
    return r.results[0]["out_x"]
```

```python
from contextlib import ExitStack

import concourse.bass as bass
from concourse import mybir

F32 = mybir.dt.float32
F32R = mybir.dt.float32r
BF16 = mybir.dt.bfloat16
I32 = mybir.dt.int32
U32 = mybir.dt.uint32
ALU = mybir.AluOpType
ACT = mybir.ActivationFunctionType
AX = mybir.AxisListType

P = 128
B, S, D = 2, 512, 256
NT = B * S // P
TB = S // P
KC = D // P
EPS = 1e-5

BLOCKS = 4

INNER = 2048
SL = 512
NS = INNER // SL
CH = SL // P
HC = 64

E, F = 8, 256
FC = F // P
NR = NT + E - 1
NSF = 7
NXG = 8
NU = NT + NR


def routed(u):
    return u - NSF if NSF <= u < NSF + NR else None


def shared_tile(u):
    return u if u < NSF else u - NR


NQ, NKV, HD = 32, 8, 8
GH = NQ // NKV
QKV = HD * (NQ + 2 * NKV)
KEND = HD * (NQ + NKV)
HW = 64
MAXAT = 6 * HD
VW = 32
NG = B * NKV
SCALE = float(1.0 / HD ** 0.5)


def build(nc, a, out):
    ctx = ExitStack()
    with ctx:
        def sem(name):
            return ctx.enter_context(nc.semaphore(name))

        def at(name, shape, dt, where):
            n = 1
            for d in shape[1:]:
                n *= d
            size = n * (2 if dt == BF16 else 4)
            t = nc.alloc_sbuf_tensor_at(name, shape, dt, offset=where[0])
            where[0] += (size + 31) // 32 * 32
            assert where[0] <= LIMIT, (name, where[0], LIMIT, here[0])
            return t

        base = nc.sbuf_base
        LIMIT = nc.sbuf_usable_end
        ctx.enter_context(nc.sbuf_tensor("arena", [P, (LIMIT - base - 256) // 4], F32))
        here = [(base + 31) // 32 * 32]

        x = at("x", [P, NT, D], F32, here)
        in_xn = [here[0]]
        xn_id = at("xn_id", [P, NT, D + 1], F32, here)
        xn = xn_id[:, :, 0:D]
        in_xT = [here[0]]
        xT = at("xT", [P, KC, B * S], F32, here)
        in_y, l1_in_y = [here[0]], [here[0]]
        y = at("y", [P, NT, D], F32, here)
        ident = at("ident", [P, P], F32, here)
        identb = at("identb", [P, P], BF16, here)
        ones = at("ones", [P, P], F32, here)
        onesb = at("onesb", [P, P], BF16, here)
        below = at("below", [P, P], BF16, here)
        same_head = at("same_head", [P, P], F32, here)
        pick_r = at("pick_r", [P, CH, P], F32R, here)
        up_to = at("up_to", [P, E, E], F32, here)
        rows_at = at("rows_at", [P, NT], F32, here)
        tile_no = at("tile_no", [P, 16], F32, here)
        pad_no = at("pad_no", [P, NR], U32, here)
        rank_key = at("rank_key", [P, E], F32, here)
        mhalf = at("mhalf", [P, NT], F32, here)
        stat = at("stat", [P, NT, 6], F32, here)
        mv = at("mv", [P, NT, 2], F32, here)
        var = [at(f"var{i}", [P, NT], F32, here) for i in range(2)]
        nmean = [at(f"nmean{i}", [P, NT], F32, here) for i in range(2)]
        rstd = [at(f"rstd{i}", [P, NT], F32, here) for i in range(2)]
        shift = [at(f"shift{i}", [P, NT], F32, here) for i in range(2)]
        bo0 = at("bo0", [P, D], F32, here)
        bo1 = at("bo1", [P, D], F32, here)
        zeros = at("zeros", [P, D], F32, here)
        router = [at(f"router{l}", [P, KC, 32], F32, here) for l in range(2)]
        shared_gu = at("shared_gu", [P, KC, 2 * F], F32, here)
        shared_d = at("shared_d", [P, FC, D], F32, here)

        l0 = [here[0]]
        xT_hi = at("xT_hi", [P, KC, B * S], F32R, in_xT)
        xT_lo = at("xT_lo", [P, KC, B * S], F32R, in_y)
        xn_hi = at("xn_hi", [P, NT, D], F32R, l0)
        xn_lo = at("xn_lo", [P, NT, D], F32R, l0)
        wk_f, wq_f, wv_f = (at(n, [P, KC, SL], F32, l0) for n in ("wk_f", "wq_f", "wv_f"))
        wo_f = at("wo_f", [P, CH, D], F32, l0)
        wk_hi, wk_lo, wq_hi, wq_lo = (at(n, [P, KC, SL], F32R, l0) for n in ("wk_hi", "wk_lo", "wq_hi", "wq_lo"))
        k_hi = [at(f"k_hi{b}", [P, TB, SL], F32R, l0) for b in range(B)]
        k_lo = [at(f"k_lo{b}", [P, TB, SL], F32R, l0) for b in range(B)]
        kx = at("kx", [P, KC, SL], F32, l0)
        q = [at(f"q{b}", [P, CH, SL], F32, l0) for b in range(B)]
        q_hi = [at(f"q_hi{b}", [P, CH, SL], F32R, l0) for b in range(B)]
        q_lo = [at(f"q_lo{b}", [P, CH, SL], F32R, l0) for b in range(B)]
        in_kv = [l0[0]]
        kv = [at(f"kv{b}", [P, CH, P], F32, l0) for b in range(B)]
        pick = at("pick", [P, CH, P], F32, in_kv)
        kvo_hi = [at(f"kvo_hi{b}", [P, CH, D], F32R, l0) for b in range(B)]
        kvo_lo = [at(f"kvo_lo{b}", [P, CH, D], F32R, l0) for b in range(B)]
        ksum = at("ksum", [P, SL], F32, in_xn)
        ksum_t = at("ksum_t", [P, 2, SL], F32, l0)
        nk = [at(f"nk{b}", [P, CH * 34], F32, in_xn) for b in range(B)]
        rec = at("rec", [P, P], F32, in_xn)
        rec_hi = [at(f"rec_hi{b}", [P, SL], F32R, w) for b, w in enumerate((in_xn, l0))]
        rec_lo = [at(f"rec_lo{b}", [P, SL], F32R, w) for b, w in enumerate((in_xn, l0))]

        me = [here[0]]
        w_gu = at("w_gu", [P, E, KC, 2 * F], F32, me)
        in_wd = me[0]
        w_d = at("w_d", [P, E, FC, D], F32, me)
        y_shared = at("y_shared", [P, NT, D], F32, me)
        xg = [at(f"xg{i}", [P, D + 1], F32, me) for i in range(NXG)]
        xgT = [at(f"xgT{i}", [P, KC, P], F32, me) for i in range(2)]
        sg = [at(f"sg{i}", [P, F], F32, me) for i in range(2)]
        h = [at(f"h{i}", [P, F], F32, me) for i in range(2)]
        hT = [at(f"hT{i}", [P, FC, P], F32, me) for i in range(2)]
        yr = [at(f"yr{i}", [P, D], F32, me) for i in range(4)]
        lgT = at("lgT", [P, 2 * P], F32, me)
        lg = at("lg", [P, NT, E], F32, me)
        best = at("best", [P, NT], F32, me)
        score = at("score", [P, NT], F32, me)
        hot_f = at("hot_f", [P, NT, E], F32, me)
        hot = at("hot", [P, NT, E], BF16, me)
        last_max = at("last_max", [P, NT], F32, me)
        cnt = at("cnt", [P, E], F32, me)
        cmp = at("cmp", [P, E, E], F32, me)
        tiles_of = at("tiles_of", [P, E], F32, me)
        tiles_end = at("tiles_end", [P, E], F32, me)
        row0 = at("row0", [P, E], F32, me)
        place = at("place", [P, NT, E], F32, me)
        slot_f = at("slot_f", [P, NT], F32, me)
        slot = at("slot", [P, NT], U32, me)
        past = at("past", [P, 16, E], F32, me)
        expert_f = at("expert_f", [P, 16], F32, me)
        expert = at("expert", [P, 16], I32, me)

        l1 = [here[0]]
        l1_first = [l1[0]]
        rest0 = [at(f"rest0_{i}", [P, TB, KEND], F32, l1) for i in range(2)]
        ks0 = at("ks0", [P, TB, NKV, 2, P], BF16, l1)
        assert l1[0] <= in_wd
        pr = [at(f"pr{i}", [P, GH, S], F32, l1_first) for i in range(3)]
        l1[0] = max(l1[0], l1_first[0])
        qkv = at("qkv", [P, NT, QKV], F32, l1)
        part = [[at(f"part{b}_{i}", [P, TB, KEND], BF16, l1) for i in range(3)] for b in range(B)]
        oT = at("oT", [P, S], F32, l1)
        kT = [at(f"kT{b}", [P, NKV, 2, S], BF16, l1) for b in range(B)]
        assert l1[0] >= me[0]
        qs = [at(f"qs{b}", [P, TB, NQ, HW], BF16, l1) for b in range(B)]
        ks1 = at("ks1", [P, TB, NKV, 2, P], BF16, l1)
        vals = at("vals", [P, NT, NKV, VW], F32, l1)
        bqkv = at("bqkv", [P, QKV], F32, l1)
        wqkv = at("wqkv", [P, KC, QKV], F32, l1)
        wo1 = at("wo1", [P, KC, D], F32, l1)
        rest1 = [at(f"rest1_{i}", [P, TB, KEND], F32, l1) for i in range(2)]
        mx = [at(f"mx{i}", [P, TB, GH], F32, l1) for i in range(2)]
        mr = [at(f"mr{i}", [P, TB, GH], F32, l1) for i in range(2)]
        dn = at("dn", [P, TB, GH], F32, l1)
        rest, ks = [rest0, rest1], [ks0, ks1]
        qT1 = [at(f"qT1_{i}", [P, 2, S], BF16, l1_in_y) for i in range(2)]
        qT2 = [at(f"qT2_{i}", [P, 2, S], BF16, l1_in_y) for i in range(2)]

        psum = ctx.enter_context(nc.psum_tensor("psum", [P, 8 * 512], F32))
        ps = [psum[:, i * 512:(i + 1) * 512] for i in range(8)]

        sorted_x = [nc.dram_tensor(f"sorted_x{l}", [NR * P, D + 1], F32).ap() for l in range(2)]
        routed_y = [nc.dram_tensor(f"routed_y{l}", [NR + B * S, D], F32).ap() for l in range(2)]

        x_loaded = sem("x_loaded")
        small_loaded = sem("small_loaded")
        consts = sem("consts")
        const_casts = sem("const_casts")
        zeroed = sem("zeroed")
        var_ready, rstd_ready = ([sem(f"{n}_{of}") for of in "xy"] for n in ("var_ready", "rstd_ready"))
        dve_chain = sem("dve_chain")
        xn_ready, xT_made, xT_ready = sem("xn_ready"), sem("xT_made"), sem("xT_ready")
        numbered = sem("numbered")
        x_summed = sem("x_summed")
        last_summed = sem("last_summed")
        stored = sem("stored")

        w_loaded = {n: sem(f"w_loaded_{n}") for n in ("k", "q", "v", "o")}
        w_hi_ready, w_lo_ready = ({n: sem(f"w_{p}_{n}") for n in "kq"} for p in ("hi", "lo"))
        split_hi, split_lo, xT_lo_ready = sem("split_hi"), sem("split_lo"), sem("xT_lo_ready")
        product = sem("product")
        act_done, dve_done = sem("act_done"), sem("dve_done")
        ksum_ready = sem("ksum_ready")
        rec_zeroed = sem("rec_zeroed")
        rec_ready = sem("rec_ready")
        q_hi_ready, q_lo_ready = sem("q_hi_ready"), sem("q_lo_ready")
        out_done = sem("out_done")
        y_ready = sem("y_ready")
        pool_chain = sem("pool_chain")


        def per_layer(name):
            return [sem(f"{name}{l}") for l in range(2)]

        moe_w, shared_w = per_layer("moe_w"), per_layer("shared_w")
        lgT_ready, logits_made = per_layer("lgT_ready"), per_layer("logits_made")
        hot_ready, rank_made = per_layer("hot_ready"), per_layer("rank_made")
        rank_read, logits_read = per_layer("rank_read"), per_layer("logits_read")
        slot_ready, expert_ready = per_layer("slot_ready"), per_layer("expert_ready")
        best_ready, score_ready, scaled = per_layer("best_ready"), per_layer("score_ready"), per_layer("scaled")
        scattered = per_layer("scattered")
        xg_loaded = [[sem(f"xg_loaded{l}_{i}") for i in range(NXG)] for l in range(2)]
        xgT_made, xgT_ready = per_layer("xgT_made"), per_layer("xgT_ready")
        gu_made, silu_ready, h_ready = per_layer("gu_made"), per_layer("silu_ready"), per_layer("h_ready")
        hT_made, hT_ready = per_layer("hT_made"), per_layer("hT_ready")
        d_made, yr_ready = per_layer("d_made"), per_layer("yr_ready")
        yr_stored = [[sem(f"yr_stored{l}_{i}") for i in range(4)] for l in range(2)]
        gathered = [[sem(f"gathered{l}_{t}") for t in range(0, NT, 2)] for l in range(2)]

        qkv_made, qkv_ready, turn_copied = (sem(n) for n in ("qkv_made", "qkv_ready", "turn_copied"))
        q_stacked, k_stacked = per_layer("q_stacked"), per_layer("k_stacked")
        ks0_consts, l1_consts = sem("ks0_consts"), sem("l1_consts")
        l1_loaded = sem("l1_loaded")
        part_ready = [sem(f"part_ready{hh}") for hh in range(2)]
        turned = sem("turned")
        s1_made, max_read, max_ready = sem("s1_made"), sem("max_read"), sem("max_ready")
        s2_made, exp_ready = sem("s2_made"), sem("exp_ready")
        av_done, oT_ready, att_ready = sem("av_done"), sem("oT_ready"), sem("att_ready")
        attT_made, proj_made = sem("attT_made"), sem("proj_made")
        att0_copied, att1_copied = sem("att0_copied"), sem("att1_copied")

        block = ctx.enter_context(nc.Block())

        def split_mm(o, lhs, rhs, start, stop, **kw):
            nc.tensor.matmul(o, lhs[0], rhs[0], start=start, stop=False, **kw)
            nc.tensor.matmul(o, lhs[0], rhs[1], start=False, stop=False, **kw)
            return nc.tensor.matmul(o, lhs[1], rhs[0], start=False, stop=stop, **kw)

        HEAD = [("Q", 0, j) for j in range(2, CH)] + [("G", 0, c) for c in range(KC)] + [("S", 0, 0)]
        HEAD += [("KV", 0, 0)] + [("G", 1, c) for c in range(KC)] + [("N", 0, 0)]
        HEAD += [("Q", 1, 0), ("Q", 1, 1), ("S", 1, 0), ("Q", 1, 2), ("Q", 1, 3), ("KV", 1, 0), ("N", 1, 0)]
        TAIL = [("BC", 0, 0), ("KVO", 0, 0), ("K+", 0, 0), ("BC", 0, 1), ("KVO", 0, 1), ("K+", 0, 1), ("BC", 0, 2),
                ("KVO", 1, 0), ("OUT", 0, 0), ("K+", 0, 2), ("BC", 0, 3), ("KVO", 1, 1), ("OUT", 0, 1), ("K+", 0, 3),
                ("BC", 1, 0), ("OUT", 0, 2), ("K+", 1, 0), ("BC", 1, 1), ("OUT", 0, 3), ("K+", 1, 1),
                ("BC", 1, 2), ("K+", 1, 2), ("BC", 1, 3), ("K+", 1, 3)]
        TAIL += [("Q+", 0, 0), ("OUT", 1, 0), ("OUT", 1, 1), ("Q+", 0, 1), ("OUT", 1, 2), ("OUT", 1, 3)]
        STREAM = [(0, ("K", b, t)) for b in range(B) for t in range(TB)] + [(0, ("Q", 0, j)) for j in range(2)]
        for s in range(NS):
            STREAM += [(s, n) for n in HEAD]
            STREAM += [(s + 1, (n[0][0],) + n[1:]) if n[0][-1] == "+" else (s, n) for n in TAIL
                       if n[0][-1] != "+" or s + 1 < NS]
        PRODUCTS = [x_ for x_ in STREAM if x_[1][0] != "OUT"]
        BY_ACT = [x_ for x_ in PRODUCTS if x_[1][0] in ("K", "G", "Q", "KVO")]
        BY_DVE = [x_ for x_ in PRODUCTS if x_[1][0] in ("K", "S", "KV", "N", "KVO", "BC")]
        BANKS = 4

        def made(s, n):
            return PRODUCTS.index((s, n)) + 1

        def act_through(s, n):
            return BY_ACT.index((s, n)) + 1

        def dve_through(s, n):
            return BY_DVE.index((s, n)) + 1

        def bank(s, n):
            return ps[PRODUCTS.index((s, n)) % BANKS]

        acc = [[ps[4 + 2 * b + i] for i in range(2)] for b in range(B)]

        def load(eng, dst, src, s):
            return eng.dma_start(dst, src).then_inc(s, 16)

        def sync_program(sp):
            xv = a["L0_attn_hidden_states"].rearrange("b (t p) d -> p (b t) d", p=P)
            for half in range(2):
                load(sp, x[:, half * TB:(half + 1) * TB, :], xv[:, half * TB:(half + 1) * TB, :], x_loaded)
            cols = {n: a[f"L0_attn_W{n}"].rearrange("(c p) n -> p c n", p=P) for n in "kqv"}
            rows = a["L0_attn_Wo"].rearrange("(j p) n -> p j n", p=P)
            stage = {"k": wk_f, "q": wq_f, "v": wv_f, "o": wo_f}
            for s in range(NS):
                if s:
                    sp.wait_ge(w_hi_ready["k"], s)
                    sp.wait_ge(w_lo_ready["k"], s)
                load(sp, stage["k"][:], cols["k"][:, :, s * SL:(s + 1) * SL], w_loaded["k"])
                if s:
                    sp.wait_ge(w_hi_ready["q"], s)
                    sp.wait_ge(w_lo_ready["q"], s)
                load(sp, stage["q"][:], cols["q"][:, :, s * SL:(s + 1) * SL], w_loaded["q"])
                if s:
                    sp.wait_ge(product, made(s - 1, ("KV", 1, 0)))
                load(sp, stage["v"][:], cols["v"][:, :, s * SL:(s + 1) * SL], w_loaded["v"])
                if s:
                    sp.wait_ge(product, made(s - 1, ("KVO", 1, 1)))
                load(sp, stage["o"][:], rows[:, s * CH:(s + 1) * CH, :], w_loaded["o"])
                if s == 1:
                    small_loads(sp)
            for p in range(1, BLOCKS):
                if p != 2:
                    sp_moe(sp, p // 2)
            for t in range(NT):
                sp.wait_ge(x_summed, (BLOCKS - 1) * NT + t + 1)
                sp.dma_start(out.rearrange("b (t p) d -> p (b t) d", p=P)[:, t, :], x[:, t, :]).then_inc(stored, 16)
            sp.wait_ge(stored, 16 * NT)

        def small_loads(sp):
            for dst, name in ((bo0, "L0_attn_bo"), (bo1, "L1_attn_bo")):
                load(sp, dst[:], a[name].partition_broadcast(P), small_loaded)
            sp.wait_ge(consts, N_CONSTS)
            for l in range(2):
                load(sp, router[l][:, :, 0:E], a[f"L{l}_ffn_router_w"].rearrange("(c p) n -> p c n", p=P), small_loaded)
            for l in range(2):
                for i in range(NR):
                    load(sp, sorted_x[l][i * P:(i + 1) * P, 0:D], zeros[:], zeroed)
                sp.dma_start(sorted_x[l].rearrange("(r p) d -> p r d", p=P)[:, :, D:D + 1],
                             pad_no[:].bitcast(F32).unsqueeze(2), allow_slow_non_contiguous=True).then_inc(zeroed, 16)

        SMALL = 16 * 4

        def shared_loads(sp, l):
            pre = f"L{l}_ffn_"
            if l:
                sp.wait_ge(gu_made[0], NU)
                sp.wait_ge(d_made[0], NU)
            for i, n in enumerate(("gate", "up")):
                load(sp, shared_gu[:, :, i * F:(i + 1) * F], a[f"{pre}shared_{n}_w"].rearrange("(c p) f -> p c f", p=P),
                     shared_w[l])
            load(sp, shared_d[:], a[f"{pre}shared_down_w"].rearrange("(c p) f -> p c f", p=P), shared_w[l])

        def sp_moe(sp, l):
            pre = f"L{l}_ffn_"
            shared_loads(sp, l)
            sp.wait_ge(y_ready, (2 * l + 1) * NT)
            for e in range(E):
                for i, n in enumerate(("gate", "up")):
                    load(sp, w_gu[:, e, :, i * F:(i + 1) * F], a[f"{pre}{n}_w"][e].rearrange("(c p) f -> p c f", p=P),
                         moe_w[l])
                load(sp, w_d[:, e], a[f"{pre}down_w"][e].rearrange("(c p) f -> p c f", p=P), moe_w[l])
            sp.wait_ge(scattered[l], 16 * NT)

            def fetch(r):
                if r >= NXG:
                    sp.wait_ge(yr_stored[l][(r - NXG) % 4], 16 * ((r - NXG) // 4 + 1))
                load(sp, xg[r % NXG][:], sorted_x[l][r * P:(r + 1) * P, :], xg_loaded[l][r % NXG])

            for r in range(NR):
                fetch(r)
            if l == 0:
                load(sp, wqkv[:], a["L1_attn_Wqkv"].rearrange("(c p) n -> p c n", p=P), l1_loaded)
                load(sp, bqkv[:], a["L1_attn_bqkv"].partition_broadcast(P), l1_loaded)
                load(sp, wo1[:], a["L1_attn_Wo"].rearrange("(c p) n -> p c n", p=P), l1_loaded)
            for i in range(4):
                sp.wait_ge(yr_stored[l][i], 16 * len([r for r in range(NR) if r % 4 == i]))
            rows = routed_y[l][NR:, :].rearrange("(t p) d -> p t d", p=P)
            for t in range(0, NT, 2):
                load(sp, y[:, t:t + 2, :], rows[:, t:t + 2, :], gathered[l][t // 2])

        N_CONSTS = 14

        def gpsimd_program(pool):
            g = nc.gpsimd
            count = [0]

            def link(ins):
                count[0] += 1
                ins.then_inc(pool_chain, 1)
                pool.wait_ge(pool_chain, count[0])

            def weight_lo(n, s):
                full, hi, lo = {"k": (wk_f, wk_hi, wk_lo), "q": (wq_f, wq_hi, wq_lo)}[n]
                if s:
                    pool.wait_ge(product, made(s - 1, (n.upper(), 1, TB - 1)))
                pool.wait_ge(w_hi_ready[n], s + 1)
                g.tensor_tensor(lo[:], full[:], hi[:].bitcast(F32), ALU.subtract).then_inc(w_lo_ready[n], 1)

            g.memset(zeros[:], 0.0).then_inc(consts, 1)
            g.memset(ones[:], 1.0).then_inc(consts, 1)
            g.memset(mhalf[:], -0.5).then_inc(consts, 1)
            link(g.memset(ident[:], 0.0))
            g.affine_select(out=ident[:], in_=ident[:], compare_op=ALU.not_equal, fill=1.0, base=0,
                            pattern=[[-1, P]], channel_multiplier=1).then_inc(consts, 1)
            for half in range(2):
                pool_rstd(pool, 0, 0, half)
            weight_lo("k", 0)
            weight_lo("q", 0)
            link(g.memset(below[:], 1.0))
            g.affine_select(out=below[:], in_=below[:], compare_op=ALU.is_gt, fill=0.0, base=0,
                            pattern=[[1, P]], channel_multiplier=-1).then_inc(consts, 1)
            link(g.memset(pick[:], 0.0))
            for t in range(TB):
                ins = g.affine_select(out=pick[:], in_=pick[:], compare_op=ALU.not_equal, fill=1.0, base=-32 * t,
                                      pattern=[[-2, CH], [-1, 2], [0, P // 2]], channel_multiplier=1)
                if t < TB - 1:
                    link(ins)
            ins.then_inc(consts, 1)
            link(g.memset(up_to[:], 1.0))
            g.affine_select(out=up_to[:], in_=up_to[:], compare_op=ALU.is_ge, fill=0.0, base=0,
                            pattern=[[1, E], [-1, E]], channel_multiplier=0).then_inc(consts, 1)
            kw = dict(channel_multiplier=0, allow_small_or_imprecise_dtypes=True)
            g.iota(rows_at[:], pattern=[[P, NT]], base=0, **kw).then_inc(consts, 1)
            g.iota(tile_no[:], pattern=[[1, 16]], base=0, **kw).then_inc(consts, 1)
            g.iota(pad_no[:], pattern=[[1, NR]], base=0, channel_multiplier=0).then_inc(consts, 1)
            g.iota(rank_key[:], pattern=[[-1, E]], base=E, **kw).then_inc(consts, 1)
            g.memset(onesb[:], 1.0).then_inc(consts, 1)
            for l in range(2):
                g.memset(router[l][:], 0.0).then_inc(consts, 1)
            pool_l0(pool, link, weight_lo)
            for p in range(1, BLOCKS):
                norms = [(1, p - 1, 0), (1, p - 1, 1), (0, p, 0), (0, p, 1)]
                for of, block_, half in norms if p != 3 else [norms[i] for i in (0, 2, 1, 3)]:
                    pool_rstd(pool, of, block_, half)
                if p == 2:
                    pool_l1_loop(pool, link)
                if p != 2:
                    pool_moe(pool, p // 2)
            for half in range(2):
                pool_rstd(pool, 1, BLOCKS - 1, half)

        def pool_rstd(pool, of, p, half):
            sl = slice(half * TB, (half + 1) * TB)
            n = 2 * p + half
            pool.wait_ge(consts, 3)
            pool.wait_ge(var_ready[of], 2 * (n + 1))
            nc.gpsimd.tensor_tensor(rstd[of][:, sl], var[of][:, sl], mhalf[:, sl], ALU.pow).then_inc(rstd_ready[of], 1)
            pool.wait_ge(rstd_ready[of], 2 * n + 1)
            nc.gpsimd.tensor_tensor(shift[of][:, sl], nmean[of][:, sl], rstd[of][:, sl],
                                    ALU.mult).then_inc(rstd_ready[of], 1)

        def pool_l1(pool):
            g = nc.gpsimd
            g.memset(vals[:], 0.0).then_inc(l1_consts, 1)
            g.memset(ks[1][:].bitcast(F32), 0.0).then_inc(l1_consts, 1)
            for b in range(B):
                g.memset(qs[b][:, :, :, MAXAT:HW].bitcast(F32), 0.0).then_inc(l1_consts, 1)
            pool.wait_ge(l1_consts, 4)
            for ver in range(2):
                at_ = ver * HW + MAXAT
                g.memset(ks[1][:, :, :, ver, at_:at_ + 3], 1.0).then_inc(l1_consts, 1)
            g.memset(vals[:, :, :, HD:HD + 1], 1.0).then_inc(l1_consts, 1)

        def pool_l0(pool, link, weight_lo):
            g = nc.gpsimd
            for half in range(2):
                sl = slice(half * TB, (half + 1) * TB)
                pool.wait_ge(split_hi, half + 1)
                g.tensor_tensor(xn_lo[:, sl], xn[:, sl], xn_hi[:, sl].bitcast(F32), ALU.subtract).then_inc(split_lo, 1)
            pool.wait_ge(split_lo, 2)
            for b in range(B):
                for zero in (nk[b], rec_hi[b], rec_lo[b]):
                    g.memset(zero[:].bitcast(F32), 0.0).then_inc(rec_zeroed, 1)
            for s in range(NS):
                for b in range(B):
                    pool.wait_ge(dve_done, dve_through(s, ("K", b, TB - 1)))
                    hi, lo = k_hi[b][:].bitcast(F32), k_lo[b][:].bitcast(F32)
                    if s or b:
                        pool.wait_ge(product, made(s, ("S", 0, 0)) if b else made(s - 1, ("S", 1, 0)))
                    link(g.tensor_tensor(ksum_t[:], hi[:, 0:2], hi[:, 2:4], ALU.add))
                    link(g.tensor_tensor(rest_of(lo)[0], lo[:, 0], lo[:, 1], ALU.add))
                    link(g.tensor_tensor(ksum_t[:, 1], ksum_t[:, 0], ksum_t[:, 1], ALU.add))
                    link(g.tensor_tensor(ksum_t[:, 0], lo[:, 2], lo[:, 3], ALU.add))
                    link(g.tensor_tensor(ksum_t[:, 0], ksum_t[:, 0], ksum[:], ALU.add))
                    g.tensor_tensor(ksum[:], ksum_t[:, 0], ksum_t[:, 1], ALU.add).then_inc(ksum_ready, 1)
                if s + 1 < NS:
                    weight_lo("k", s + 1)
                    weight_lo("q", s + 1)

        def rest_of(_):
            return [ksum[:]]

        def pool_moe(pool, l):
            g = nc.gpsimd
            g.iota(xn_id[:, :, D:D + 1].bitcast(U32), pattern=[[P, NT], [0, 1]], base=NR,
                   channel_multiplier=1).then_inc(numbered, 1)
            pool.wait_ge(numbered, l + 1)
            pool.wait_ge(zeroed, 16 * 2 * (NR + 1))
            pool.wait_ge(slot_ready[l], 1)
            for t in range(NT):
                pool.wait_ge(scaled[l], t + 1)
                g.indirect_dma_start(sorted_x[l][:, :], bass.IndirectOffsetOnAxis(ap=slot[:, t:t + 1], axis=0),
                                     xn_id[:, t, :], None).then_inc(scattered[l], 16)
            if l == 0:
                pool_l1(pool)
            for r in range(NR):
                pool.wait_ge(yr_ready[l], NSF + r + 1)
                g.indirect_dma_start(routed_y[l][:, :], bass.IndirectOffsetOnAxis(
                    ap=xg[r % NXG][:, D:D + 1].bitcast(U32), axis=0), yr[r % 4][:], None).then_inc(yr_stored[l][r % 4], 16)

        def vector_program(dve):
            v = nc.vector
            count = [0]

            def link(ins):
                count[0] += 1
                ins.then_inc(dve_chain, 1)
                dve.wait_ge(dve_chain, count[0])

            def mark(ins):
                count[0] += 1
                ins.then_inc(dve_chain, 1)

            def settle():
                dve.wait_ge(dve_chain, count[0])

            dve.wait_ge(consts, 4)
            v.tensor_copy(identb[:], ident[:]).then_inc(const_casts, 1)
            for i in range(2):
                for j in range(2):
                    v.memset(same_head[i * HC:(i + 1) * HC, j * HC:(j + 1) * HC], float(i == j)).then_inc(const_casts, 1)

            def stats(src, half, make=None, y_before=0):
                of = int(src is y)
                tiles = range(half * TB, (half + 1) * TB)
                for t in tiles:
                    if make:
                        for n in ((t, t + 1) if t == tiles[0] else (t + 1,) if t < tiles[-1] else ()):
                            make(n)
                        dve.wait_ge(y_ready, y_before + t + 1)
                    mark(v.bn_stats(stat[:, t, :], src[:, t, :]))
                settle()
                for t in tiles:
                    mark(v.bn_aggr(mv[:, t, :], stat[:, t, :]))
                settle()
                sl = slice(half * TB, (half + 1) * TB)
                v.tensor_scalar(var[of][:, sl], mv[:, sl, 1], EPS, None, ALU.add).then_inc(var_ready[of], 1)
                v.tensor_scalar(nmean[of][:, sl], mv[:, sl, 0], -1.0, None, ALU.mult).then_inc(var_ready[of], 1)

            def close_y(p, half, make_y):
                stats(y, half, make_y, p * NT)

            def close_x(p, half):
                dve.wait_ge(rstd_ready[1], 2 * (2 * p + half) + 1)
                if p:
                    dve.wait_ge(x_summed, (p - 1) * NT + (half + 1) * TB)
                for t in range(half * TB, (half + 1) * TB):
                    ins = v.scalar_tensor_tensor(x[:, t, :], y[:, t, :], rstd[1][:, t:t + 1], x[:, t, :],
                                                 ALU.mult, ALU.add)
                    if p == BLOCKS - 1:
                        ins.then_inc(last_summed, 1)
                    else:
                        mark(ins)
                if p < BLOCKS - 1:
                    settle()
                    stats(x, half)

            def residual(p, make_y):
                if p == 2:
                    close_y(p, 1, make_y)
                    close_x(p, 1)
                else:
                    for half in range(2):
                        close_y(p, half, make_y)
                    for half in range(2):
                        close_x(p, half)

            def turn_lo(i):
                dve.wait_ge(xT_ready, i + 1)
                cols = slice(i * 256, (i + 1) * 256)
                v.tensor_tensor(xT_lo[:, :, cols], ps[4 + i][:].rearrange("p (c n) -> p c n", c=KC),
                                xT_hi[:, :, cols].bitcast(F32), ALU.subtract).then_inc(xT_lo_ready, 1)

            for half in range(2):
                dve.wait_ge(x_loaded, 32)
                stats(x, half)
            for i in range(4):
                turn_lo(i)
            for half in range(2):
                dve.wait_ge(xn_ready, (half + 1) * TB)
                sl = slice(half * TB, (half + 1) * TB)
                v.tensor_copy(xn_hi[:, sl], xn[:, sl]).then_inc(split_hi, 1)
            dve_l0(dve, link, mark, settle)
            dve.wait_ge(small_loaded, SMALL)

            def l0_y(t):
                dve.wait_ge(out_done, t // TB + 1)
                v.tensor_tensor(y[:, t, :], acc[t // TB][t % TB // 2][:, t % 2 * D:(t % 2 + 1) * D], bo0[:],
                                ALU.add).then_inc(y_ready, 1)

            residual(0, l0_y)
            for p in range(1, BLOCKS):
                make_y = dve_l1(dve, link, mark, settle, close_y, close_x) if p == 2 else dve_moe(dve, link, p // 2)
                residual(p, make_y)

        def dve_l0(dve, link, mark, settle):
            v = nc.vector

            def q_low(s, b, j):
                dve.wait_ge(q_hi_ready, (s * B + b) * CH + j + 1)
                v.tensor_tensor(q_lo[b][:, j], q[b][:, j], q_hi[b][:, j].bitcast(F32), ALU.subtract).then_inc(q_lo_ready, 1)

            for s, n in BY_DVE:
                kind, b, i = n
                pt = bank(s, n)
                if kind in ("K", "KVO"):
                    dve.wait_ge(act_done, act_through(s, n))
                else:
                    dve.wait_ge(product, made(s, n))
                if (s, kind, b) == (0, "S", 0):
                    dve.wait_ge(rec_zeroed, 6)
                    dve.wait_ge(consts, N_CONSTS)
                    v.tensor_copy(pick_r[:], pick[:]).then_inc(const_casts, 1)
                    dve.wait_ge(const_casts, 6)
                if kind == "K":
                    if s:
                        dve.wait_ge(ksum_ready, (s - 1) * B + b + 1)
                    ins = v.scalar_tensor_tensor(k_lo[b][:, i], pt[:], 0.0, k_hi[b][:, i].bitcast(F32),
                                                 ALU.max, ALU.subtract)
                elif kind == "S":
                    ins = v.tensor_tensor(nk[b][:].rearrange("p (j m) -> p j m", j=CH)[:, :, 0:2], pt[:].rearrange("p (j m) -> p j m", j=CH)[:, :, 0:2],
                                          same_head[:, 0:P:HC].unsqueeze(1).to_broadcast([P, CH, 2]), ALU.mult)
                elif kind == "KV":
                    ins = v.tensor_tensor(kv[b][:], pt[:].rearrange("p (j m) -> p j m", j=CH),
                                          same_head[:].unsqueeze(1).to_broadcast([P, CH, P]), ALU.mult)
                elif kind == "N":
                    v.tensor_scalar(rec[:], pt[:, 0:P], 1e-6, None, ALU.max).then_inc(dve_done, 1)
                    dve.wait_ge(dve_done, dve_through(s, n))
                    link(v.reciprocal(rec[:], rec[:]))
                    for t in range(TB):
                        rows, cols = slice(t * 32, (t + 1) * 32), slice(t * P, (t + 1) * P)
                        mark(v.tensor_copy(rec_hi[b][rows, cols], rec[rows, :]))
                    settle()
                    for t in range(TB):
                        rows, cols = slice(t * 32, (t + 1) * 32), slice(t * P, (t + 1) * P)
                        v.tensor_tensor(rec_lo[b][rows, cols], rec[rows, :], rec_hi[b][rows, cols].bitcast(F32),
                                        ALU.subtract).then_inc(rec_ready, 1)
                    continue
                elif kind == "KVO":
                    ins = v.tensor_tensor(kvo_lo[b][:, 2 * i:2 * i + 2], pt[:].rearrange("p (j m) -> p j m", j=2),
                                          kvo_hi[b][:, 2 * i:2 * i + 2].bitcast(F32), ALU.subtract)
                else:
                    ins = v.tensor_tensor(q[b][:, i], q[b][:, i], pt[:], ALU.mult)
                ins.then_inc(dve_done, 1)
                if kind == "BC":
                    if i:
                        q_low(s, b, i - 1)
                    if i == CH - 1:
                        q_low(s, b, i)

        def dve_moe(dve, link, l):
            v = nc.vector
            dve.wait_ge(logits_made[l], 1)
            v.tensor_copy(lgT[:], ps[6][:, 0:2 * P]).then_inc(lgT_ready[l], 1)
            dve.wait_ge(logits_made[l], 2)
            v.tensor_copy(lg[:].rearrange("p (j i) e -> p i j e", i=2),
                          ps[6][:, 2 * P:4 * P].rearrange("p (i j m) -> p i j m", i=2, j=4)[:, :, :, 0:E]
                          ).then_inc(logits_read[l], 1)
            dve.wait_ge(logits_read[l], 1)
            v.tensor_reduce(best[:], lg[:], AX.X, ALU.max).then_inc(best_ready[l], 1)
            dve.wait_ge(best_ready[l], 1)
            link(v.tensor_tensor(hot_f[:], lg[:], best[:].unsqueeze(2).to_broadcast([P, NT, E]), ALU.is_ge))
            link(v.tensor_tensor(hot_f[:], hot_f[:], rank_key[:].unsqueeze(1).to_broadcast([P, NT, E]), ALU.mult))
            link(v.tensor_reduce(last_max[:], hot_f[:], AX.X, ALU.max))
            link(v.tensor_tensor(hot_f[:], hot_f[:], last_max[:].unsqueeze(2).to_broadcast([P, NT, E]), ALU.is_equal))
            v.tensor_copy(hot[:], hot_f[:]).then_inc(hot_ready[l], 1)
            dve.wait_ge(rank_made[l], 1)
            counts = ps[7][:, NT * E:(NT + 1) * E]
            link(v.tensor_copy(place[:], ps[7][:, 0:NT * E].rearrange("p (t e) -> p t e", e=E)))
            v.tensor_copy(cnt[:], counts).then_inc(rank_read[l], 1)
            dve.wait_ge(rank_read[l], 1)
            link(v.tensor_tensor(cmp[:], cnt[:].unsqueeze(2).to_broadcast([P, E, NT]),
                                 rows_at[:].unsqueeze(1).to_broadcast([P, E, NT]), ALU.is_gt))
            link(v.tensor_reduce(tiles_of[:], cmp[:], AX.X, ALU.add))
            link(v.tensor_tensor(cmp[:], up_to[:], tiles_of[:].unsqueeze(1).to_broadcast([P, E, E]), ALU.mult))
            link(v.tensor_reduce(tiles_end[:], cmp[:], AX.X, ALU.add))
            link(v.tensor_tensor(row0[:], tiles_end[:], tiles_of[:], ALU.subtract))
            link(v.tensor_scalar(row0[:], row0[:], float(P), None, ALU.mult))
            link(v.tensor_tensor(place[:], place[:], row0[:].unsqueeze(1).to_broadcast([P, NT, E]), ALU.add))
            link(v.tensor_tensor(place[:], place[:], hot_f[:], ALU.mult))
            link(v.tensor_reduce(slot_f[:], place[:], AX.X, ALU.add))
            v.tensor_copy(slot[:], slot_f[:]).then_inc(slot_ready[l], 1)
            dve.wait_ge(score_ready[l], 1)
            for t in range(NT):
                v.tensor_scalar(xn[:, t, :], xn[:, t, :], score[:, t:t + 1], None, ALU.mult).then_inc(scaled[l], 1)
            link(v.tensor_tensor(past[:], tile_no[:].unsqueeze(2).to_broadcast([P, 16, E]),
                                 tiles_end[:].unsqueeze(1).to_broadcast([P, 16, E]), ALU.is_ge))
            link(v.tensor_reduce(expert_f[:], past[:], AX.X, ALU.add))
            link(v.tensor_scalar(expert_f[:], expert_f[:], float(E - 1), None, ALU.min))
            v.tensor_copy(expert[:], expert_f[:]).then_inc(expert_ready[l], 1)
            for i in range(NU + 2):
                if i < NU:
                    dve.wait_ge(silu_ready[l], i + 1)
                    if i >= 2:
                        dve.wait_ge(hT_made[l], i - 1)
                    v.tensor_tensor(h[i % 2][:], sg[i % 2][:], ps[2 + i % 2][:, F:2 * F], ALU.mult).then_inc(h_ready[l], 1)
                if i >= 2:
                    u = i - 2
                    dve.wait_ge(d_made[l], u + 1)
                    r = routed(u)
                    if r is not None and r >= 4:
                        dve.wait_ge(yr_stored[l][r % 4], 16 * (r // 4))
                    dst = y_shared[:, shared_tile(u), :] if r is None else yr[r % 4][:]
                    v.tensor_copy(dst, ps[6 + u % 2][:, 0:D]).then_inc(yr_ready[l], 1)
            dve.wait_ge(yr_ready[l], NU)

            def moe_y(t):
                if t % 2 == 0:
                    dve.wait_ge(gathered[l][t // 2], 16)
                v.tensor_tensor(y[:, t, :], y[:, t, :], y_shared[:, t, :], ALU.add).then_inc(y_ready, 1)

            return moe_y

        def scalar_program(act):
            def turn(p, i):
                act.wait_ge(xT_made, 4 * p + i + 1)
                cols = slice(i * 256, (i + 1) * 256)
                dst = xT_hi if p == 0 else xT
                nc.scalar.activation(dst[:, :, cols], ps[i if p else 4 + i][:].rearrange("p (c n) -> p c n", c=KC),
                                     ACT.Copy).then_inc(xT_ready, 1)

            def weight_hi(n, s):
                full, hi = {"k": (wk_f, wk_hi), "q": (wq_f, wq_hi)}[n]
                if s:
                    act.wait_ge(product, made(s - 1, (n.upper(), 1, TB - 1)))
                    act.wait_ge(w_lo_ready[n], s)
                act.wait_ge(w_loaded[n], 16 * (s + 1))
                nc.scalar.activation(hi[:], full[:], ACT.Copy).then_inc(w_hi_ready[n], 1)

            def normalise(p):
                for half in range(2):
                    if p == 0 and half == 1:
                        weight_hi("k", 0)
                    act.wait_ge(rstd_ready[0], 2 * (2 * p + half + 1))
                    for t in range(half * TB, (half + 1) * TB):
                        nc.scalar.activation(xn[:, t, :], x[:, t, :], ACT.Identity, bias=shift[0][:, t:t + 1],
                                             scale=rstd[0][:, t:t + 1]).then_inc(xn_ready, 1)
                    turn(p, 2 * half)
                    turn(p, 2 * half + 1)

            def complete(p):
                for t in range(NT):
                    if p == BLOCKS - 1:
                        act.wait_ge(last_summed, t + 1)
                        act.wait_ge(rstd_ready[1], 2 * (2 * p + t // TB + 1))
                    nc.scalar.activation(x[:, t, :], x[:, t, :], ACT.Identity,
                                         bias=shift[1][:, t:t + 1]).then_inc(x_summed, 1)

            normalise(0)
            weight_hi("q", 0)
            for s, n in PRODUCTS:
                kind, b, i = n
                pt = bank(s, n)
                if (s, n) in BY_ACT:
                    act.wait_ge(product, made(s, n))
                    if kind == "K":
                        if s:
                            act.wait_ge(ksum_ready, (s - 1) * B + b + 1)
                        nc.scalar.activation(k_hi[b][:, i], pt[:], ACT.Relu).then_inc(act_done, 1)
                    elif kind == "G":
                        nc.scalar.activation(kx[:, i], pt[:], ACT.Copy).then_inc(act_done, 1)
                    elif kind == "Q":
                        if s:
                            act.wait_ge(q_lo_ready, ((s - 1) * B + b) * CH + i + 1)
                        nc.scalar.activation(q[b][:, i], pt[:], ACT.Relu).then_inc(act_done, 1)
                    else:
                        nc.scalar.activation(kvo_hi[b][:, 2 * i:2 * i + 2],
                                             pt[:].rearrange("p (j m) -> p j m", j=2), ACT.Copy).then_inc(act_done, 1)
                elif kind == "BC":
                    act.wait_ge(dve_done, dve_through(s, n))
                    nc.scalar.activation(q_hi[b][:, i], q[b][:, i], ACT.Copy).then_inc(q_hi_ready, 1)
                if s + 1 < NS and n == ("K", 1, TB - 1):
                    weight_hi("k", s + 1)
                if s + 1 < NS and n == ("Q", 1, CH - 1):
                    weight_hi("q", s + 1)
            for p in range(1, BLOCKS):
                normalise(p)
                complete(p - 1)
                if p == 2:
                    act_l1(act)
                else:
                    act_moe(act, p // 2)
                if p == 1:
                    act.wait_ge(gu_made[0], NU)
                    nc.scalar.activation(ks0[:].bitcast(F32).rearrange("p t g v n -> p (t g v n)").rearrange(
                        "p (r d) -> p r d", d=D), zeros[:].unsqueeze(1).to_broadcast([P, TB * NKV * P // D, D]),
                        ACT.Copy).then_inc(ks0_consts, 1)
                    act.wait_ge(ks0_consts, 1)
                    for ver in range(2):
                        at_ = ver * HW + MAXAT
                        nc.scalar.activation(ks0[:, :, :, ver, at_:at_ + 3], ones[:, 0:TB * NKV * 3].rearrange(
                            "p (t g i) -> p t g i", t=TB, g=NKV), ACT.Copy).then_inc(ks0_consts, 1)
            complete(BLOCKS - 1)

        def act_moe(act, l):
            act.wait_ge(best_ready[l], 1)
            nc.scalar.activation(score[:], best[:], ACT.Sigmoid).then_inc(score_ready[l], 1)
            for i in range(-2, NU + 1):
                if 0 <= i < NU:
                    act.wait_ge(gu_made[l], i + 1)
                    if i >= 2:
                        act.wait_ge(h_ready[l], i - 1)
                    nc.scalar.activation(sg[i % 2][:], ps[2 + i % 2][:, 0:F], ACT.Silu).then_inc(silu_ready[l], 1)
                if 1 <= i:
                    u = i - 1
                    act.wait_ge(hT_made[l], u + 1)
                    if u >= 2:
                        act.wait_ge(d_made[l], u - 1)
                    nc.scalar.activation(hT[u % 2][:], ps[4 + u % 2][:, 0:F].rearrange("p (c n) -> p c n", c=FC),
                                         ACT.Copy).then_inc(hT_ready[l], 1)
                r = i + 2 - NSF
                if 0 <= r < NR:
                    act.wait_ge(xgT_made[l], r + 1)
                    if r >= 2:
                        act.wait_ge(gu_made[l], i + 1)
                    nc.scalar.activation(xgT[r % 2][:], ps[r % 2][:, 0:D].rearrange("p (c n) -> p c n", c=KC),
                                         ACT.Copy).then_inc(xgT_ready[l], 1)

        def tensor_program(pe):
            mm = nc.tensor.matmul

            def turn_x(p):
                if p == 0:
                    pe.wait_ge(consts, 4)
                for i in range(4):
                    for t in (2 * i, 2 * i + 1):
                        pe.wait_ge(xn_ready, NT * p + t + 1)
                        for c in range(KC):
                            last = nc.tensor.transpose(ps[i if p else 4 + i][:, c * 256 + t % 2 * P:c * 256 + (t % 2 + 1) * P],
                                                       xn[:, t, c * P:(c + 1) * P], ident[:])
                    last.then_inc(xT_made, 1)

            turn_x(0)
            pe_l0(pe)
            for p in range(1, BLOCKS):
                turn_x(p)
                if p == 2:
                    pe_l1(pe)
                else:
                    pe_moe(pe, p // 2)

        def pe_l0(pe):
            mm = nc.tensor.matmul

            def out_mm(s, b, t, j):
                o = acc[b][t // 2][:, t % 2 * D:(t % 2 + 1) * D]
                tok = slice(t * P, (t + 1) * P)
                return split_mm(o, (q_hi[b][:, j, tok], q_lo[b][:, j, tok]), (kvo_hi[b][:, j], kvo_lo[b][:, j]),
                                start=(s == 0 and j == 0 and t % 2 == 0), stop=(s == NS - 1 and j == CH - 1),
                                skip_group_check=True)

            for s, n in STREAM:
                kind, b, i = n
                if kind == "OUT":
                    if i % 2 == 0:
                        pe.wait_ge(dve_done, dve_through(s, ("KVO", b, i // 2)))
                    pe.wait_ge(q_lo_ready, (s * B + b) * CH + i + 1)
                    for t in range(TB):
                        last = out_mm(s, b, t, i)
                    if s == NS - 1 and i == TB - 1:
                        last.then_inc(out_done, 1)
                    continue
                pos = PRODUCTS.index((s, n))
                if pos >= BANKS:
                    before = PRODUCTS[pos - BANKS]
                    if before in BY_DVE:
                        pe.wait_ge(dve_done, dve_through(*before))
                    else:
                        pe.wait_ge(act_done, act_through(*before))
                pt = bank(s, n)
                if kind == "K":
                    if (b, i) == (0, 0):
                        pe.wait_ge(w_lo_ready["k"], s + 1)
                    if s == 0:
                        pe.wait_ge(xT_lo_ready, (b * TB + i) // 2 + 1)
                    tok = slice((b * TB + i) * P, (b * TB + i + 1) * P)
                    for c in range(KC):
                        last = split_mm(pt[:], (xT_hi[:, c, tok], xT_lo[:, c, tok]), (wk_hi[:, c], wk_lo[:, c]),
                                        c == 0, c == KC - 1)
                elif kind == "Q":
                    if (b, i) == (0, 0):
                        pe.wait_ge(w_lo_ready["q"], s + 1)
                    ch, tok = slice(i * P, (i + 1) * P), slice(b * S, (b + 1) * S)
                    for c in range(KC):
                        last = split_mm(pt[:], (wq_hi[:, c, ch], wq_lo[:, c, ch]), (xT_hi[:, c, tok], xT_lo[:, c, tok]),
                                        c == 0, c == KC - 1)
                elif kind == "G":
                    if s == 0:
                        pe.wait_ge(split_lo, b + 1)
                    ch = slice(i * P, (i + 1) * P)
                    for t in range(TB):
                        pe.wait_ge(dve_done, dve_through(s, ("K", b, t)))
                        last = split_mm(pt[:], (xn_hi[:, b * TB + t, ch], xn_lo[:, b * TB + t, ch]),
                                        (k_hi[b][:, t], k_lo[b][:, t]), t == 0, t == TB - 1)
                elif kind == "S":
                    pe.wait_ge(ksum_ready, s * B + b + 1)
                    for j in range(CH):
                        last = mm(pt[:, j * P:(j + 1) * P], ksum[:, j * P:(j + 1) * P], ones[:], start=True, stop=True)
                elif kind == "KV":
                    pe.wait_ge(w_loaded["v"], 16 * (s + 1))
                    pe.wait_ge(act_done, act_through(s, ("G", b, KC - 1)))
                    for j in range(CH):
                        ch = slice(j * P, (j + 1) * P)
                        for c in range(KC):
                            last = mm(pt[:, ch], wv_f[:, c, ch], kx[:, c, ch], start=(c == 0), stop=(c == KC - 1))
                elif kind == "N":
                    pe.wait_ge(dve_done, dve_through(s, ("S", b, 0)))
                    pe.wait_ge(act_done, act_through(s, ("Q", b, CH - 1)))
                    for j in range(CH):
                        for t in range(TB):
                            last = mm(pt[t * 32:(t + 1) * 32, 0:P], nk[b][:, j * 32:(j + 1) * 32],
                                      q[b][:, j, t * P:(t + 1) * P], start=(j == 0), stop=(j == CH - 1),
                                      skip_group_check=True)
                elif kind == "KVO":
                    pe.wait_ge(w_loaded["o"], 16 * (s + 1))
                    pe.wait_ge(dve_done, dve_through(s, ("KV", b, 0)))
                    for j in (2 * i, 2 * i + 1):
                        last = mm(pt[:, j % 2 * D:(j % 2 + 1) * D], kv[b][:, j], wo_f[:, j], start=True, stop=True)
                else:
                    pe.wait_ge(rec_ready, (s * B + b + 1) * TB)
                    mm(pt[:], pick_r[:, i], rec_hi[b][:], start=True, stop=False)
                    last = mm(pt[:], pick_r[:, i], rec_lo[b][:], start=False, stop=True)
                last.then_inc(product, 1)

        def pe_moe(pe, l):
            mm = nc.tensor.matmul
            if l == 0:
                pe.wait_ge(small_loaded, SMALL)
            pe.wait_ge(y_ready, (2 * l + 1) * NT)
            for c in range(KC):
                for j in range(4):
                    pe.wait_ge(xT_ready, 4 * (2 * l + 1) + j + 1)
                    last = mm(ps[6][j * 32:(j + 1) * 32, 0:2 * P], router[l][:, c], xT[:, c, j * 2 * P:(j + 1) * 2 * P],
                              start=(c == 0), stop=(c == KC - 1), skip_group_check=True)
            last.then_inc(logits_made[l], 1)
            pe.wait_ge(lgT_ready[l], 1)
            for i in range(2):
                last = nc.tensor.transpose(ps[6][:, (2 + i) * P:(3 + i) * P], lgT[:, i * P:(i + 1) * P], ident[:])
            last.then_inc(logits_made[l], 1)

            def ranks():
                pe.wait_ge(hot_ready[l], 1)
                for t in range(NT):
                    o = ps[7][:, t * E:(t + 1) * E]
                    for j in range(t):
                        mm(o, onesb[:], hot[:, j], start=(j == 0), stop=False)
                    mm(o, below[:], hot[:, t], start=(t == 0), stop=True)
                for j in range(NT):
                    last = mm(ps[7][:, NT * E:(NT + 1) * E], onesb[:], hot[:, j], start=(j == 0), stop=(j == NT - 1))
                last.then_inc(rank_made[l], 1)

            def gate_up(u):
                r = routed(u)
                if u >= 2:
                    pe.wait_ge(h_ready[l], u - 1)
                if r is None:
                    if u == 0:
                        pe.wait_ge(shared_w[l], 48)
                    t = shared_tile(u)
                    for c in range(KC):
                        last = mm(ps[2 + u % 2][:], xT[:, c, t * P:(t + 1) * P], shared_gu[:, c],
                                  start=(c == 0), stop=(c == KC - 1))
                else:
                    if r == 0:
                        pe.wait_ge(moe_w[l], 16 * 3 * E)
                    pe.wait_ge(xgT_ready[l], r + 1)
                    for c in range(KC):
                        last = mm(ps[2 + u % 2][:], xgT[r % 2][:, c], w_gu[:, bass.ds(experts[r], 1), c, :],
                                  start=(c == 0), stop=(c == KC - 1))
                last.then_inc(gu_made[l], 1)

            def turn_h(u):
                pe.wait_ge(h_ready[l], u + 1)
                if u >= 2:
                    pe.wait_ge(hT_ready[l], u - 1)
                for c in range(FC):
                    last = nc.tensor.transpose(ps[4 + u % 2][:, c * P:(c + 1) * P], h[u % 2][:, c * P:(c + 1) * P], ident[:])
                last.then_inc(hT_made[l], 1)

            def turn_rows(r):
                pe.wait_ge(xg_loaded[l][r % NXG], 16 * (r // NXG + 1))
                if r >= 2:
                    pe.wait_ge(xgT_ready[l], r - 1)
                for c in range(KC):
                    last = nc.tensor.transpose(ps[r % 2][:, c * P:(c + 1) * P], xg[r % NXG][:, c * P:(c + 1) * P], ident[:])
                last.then_inc(xgT_made[l], 1)

            def down(u):
                r = routed(u)
                pe.wait_ge(hT_ready[l], u + 1)
                if u == 0:
                    pe.wait_ge(logits_read[l], 1)
                elif u == 1:
                    pe.wait_ge(rank_read[l], 1)
                else:
                    pe.wait_ge(yr_ready[l], u - 1)
                for c in range(FC):
                    w = shared_d[:, c] if r is None else w_d[:, bass.ds(experts[r], 1), c, :]
                    last = mm(ps[6 + u % 2][:, 0:D], hT[u % 2][:, c], w, start=(c == 0), stop=(c == FC - 1))
                last.then_inc(d_made[l], 1)

            experts = {}
            for i in range(NU + 2):
                if i == 0:
                    ranks()
                if i < NU:
                    gate_up(i)
                if 1 <= i <= NU:
                    turn_h(i - 1)
                r = i + 2 - NSF
                if 0 <= r < NR:
                    if r == 0:
                        pe.wait_ge(expert_ready[l], 1)
                    experts[r] = pe.value_load(expert[0:1, r:r + 1], min_val=0, max_val=E - 1)
                    turn_rows(r)
                if i >= 2:
                    down(i - 2)

        STEPS = NG * TB
        LAG = 7
        PROJ_AT = STEPS + 1
        PROJ_BANK = [ps[2 + t % 2] for t in range(TB)] + ps[TB:NT]
        QKV_BANK = (4, 5, 6, 0, 1, 2, 3, 4)
        K1_AT = (11, 15, 19, 23, 27, 31, 35, 39)

        def turns_at(c):
            items = []
            if c < TB:
                items.append(("k", 0, TB + c))
            if c in K1_AT:
                items.append(("k", 1, K1_AT.index(c)))
            if c % TB == 0 and c // TB + 1 < NG:
                items.append(("q1", 0, c // TB + 1))
            if c % TB == 1 and 0 <= (c - 5) // TB < NG:
                items.append(("q2", 0, (c - 5) // TB))
            if c % TB == 2 and 0 <= (c - 14) // TB < NG:
                items.append(("o", 0, (c - 14) // TB))
            return items

        END = STEPS + 12
        FIRST = [("k", 0, t) for t in range(TB)] + [("q1", 0, 0)]
        TURNS = FIRST + [x_ for c_ in range(END) for x_ in turns_at(c_)]
        BY_READER = {"act": [x_ for x_ in TURNS if x_[0] != "o"], "dve": [x_ for x_ in TURNS if x_[0] == "o"]}

        def turn_no(what):
            return TURNS.index(what) + 1

        def turn_bank(n):
            return ps[(7, 5, 6, 7, 5)[n] if n < len(FIRST) else 7]

        LAST_IN_BANK = {3: 0, 4: 1, 5: 3}

        def wait_read(eng, what):
            if what[0] == "o":
                eng.wait_ge(att_ready, BY_READER["dve"].index(what) + 1)
            else:
                eng.wait_ge(turn_copied, BY_READER["act"].index(what) + 1)

        def act_l1(act):
            def copy_turn(what):
                kind, b, i = what
                act.wait_ge(turned, turn_no(what))
                turned_ = turn_bank(TURNS.index(what)).bitcast(BF16)
                if kind == "k":
                    half, t = i // TB, i % TB
                    dst, src = kT[b][:, half * 4:half * 4 + 4, :, t * P:(t + 1) * P], turned_.rearrange(
                        "p (g w n) -> p g w n", g=4, w=2)
                else:
                    dst, src = (qT1 if kind == "q1" else qT2)[i % 2][:], turned_.rearrange("p (i n) -> p i n", i=2)
                nc.scalar.activation(dst, src, ACT.Copy).then_inc(turn_copied, 1)

            def query_stack(hh, i):
                act.wait_ge(part_ready[hh], i + 1)
                for t in range(TB):
                    stack_queries(nc.scalar, 0, t, i, HALVES[hh]).then_inc(q_stacked[0], 1)

            for i in range(3):
                query_stack(0, i)
                copy_turn(FIRST[i])
            for what in FIRST[3:]:
                copy_turn(what)
            for c in range(END):
                d = c - LAG
                if c < 6 and c % 2 == 1:
                    query_stack(1, c // 2)
                if 0 <= d < STEPS:
                    if d >= 3:
                        act.wait_ge(av_done, d - 2)
                for j in range(GH):
                    if j == 2:
                        for what in turns_at(c):
                            if what[0] != "o":
                                copy_turn(what)
                    if 0 <= d < STEPS:
                        act.wait_ge(s2_made, d * GH + j + 1)
                        nc.scalar.activation(pr[d % 3][:, j], ps[4 + j % 2], ACT.Exp, scale=SCALE).then_inc(exp_ready, 1)
            for t in range(TB, NT):
                act.wait_ge(attT_made, t + 1)
                nc.scalar.activation(xT[:, :, t * P:(t + 1) * P],
                                     ps[t][:, 0:D].rearrange("p (c n) -> p c n", c=KC), ACT.Copy).then_inc(att1_copied, 1)

        HALVES = (slice(0, NQ // 2), slice(NQ // 2, NQ))
        QUERY_AT = ((0, 3), (3, 2), (5, 1))

        def stack_queries(eng, b, t, i, heads=slice(0, NQ)):
            at_, n = QUERY_AT[i]
            nh = heads.stop - heads.start
            dst = qs[b][:, t, heads, at_ * HD:(at_ + n) * HD].rearrange("p h (n d) -> p h n d", d=HD)
            src = part[b][i][:, t, heads.start * HD:heads.stop * HD].rearrange(
                "p (h d) -> p h d", d=HD).unsqueeze(2).to_broadcast([P, nh, n, HD])
            if eng is nc.scalar:
                return eng.activation(dst, src, ACT.Copy)
            return eng.tensor_copy(dst, src)

        def stack_keys(eng, b, ver, at_, i):
            return eng.tensor_copy(ks[b][:, :, :, ver, ver * HW + at_ * HD:ver * HW + (at_ + 1) * HD],
                                   part[b][i][:, :, NQ * HD:].rearrange("p t (g d) -> p t g d", d=HD))

        KEY_PARTS = (0, 1, 2, 0, 1, 0)

        def pool_l1_loop(pool, link):
            g = nc.gpsimd
            b = 1

            def split(k, tiles, cols):
                i = k // 2
                src = qkv[:, b * TB + tiles.start:b * TB + tiles.stop, cols] if i == 0 else rest[b][i - 1][:, tiles, cols]
                if k % 2 == 0:
                    link(g.tensor_copy(part[b][i][:, tiles, cols], src))
                else:
                    link(g.tensor_tensor(rest[b][i][:, tiles, cols], src, part[b][i][:, tiles, cols], ALU.subtract))

            SPLIT, STACK = 5, 2 * len(KEY_PARTS)
            STEPS_OF = (SPLIT, STACK, SPLIT * TB, 3 * TB)

            def prepare(k):
                if k < SPLIT:
                    return split(k, slice(0, TB), slice(NQ * HD, KEND))
                k -= SPLIT
                if k < STACK:
                    ver, at_ = divmod(k, len(KEY_PARTS))
                    return stack_keys(g, b, ver, at_, KEY_PARTS[at_]).then_inc(k_stacked[b], 1)
                k -= STACK
                if k < SPLIT * TB:
                    t, k = divmod(k, SPLIT)
                    return split(k, slice(t, t + 1), slice(0, NQ * HD))
                t, i = divmod(k - SPLIT * TB, 3)
                return stack_queries(g, b, t, i).then_inc(q_stacked[b], 1)

            shares = (6, 9, 9, 9, 7, 5, 4)
            assert sum(shares) == sum(STEPS_OF)
            pool.wait_ge(qkv_ready, NT)
            cols = slice(NQ // 2 * HD, NQ * HD)
            for i in range(3):
                src = qkv[:, 0:TB, cols] if i == 0 else rest[0][i - 1][:, :, cols]
                g.tensor_copy(part[0][i][:, :, cols], src).then_inc(part_ready[1], 1)
                pool.wait_ge(part_ready[1], i + 1)
                if i < 2:
                    link(g.tensor_tensor(rest[0][i][:, :, cols], src, part[0][i][:, :, cols], ALU.subtract))
            for n in range(NG):
                for k in range(sum(shares[:n]), sum(shares[:n + 1])):
                    prepare(k)
                bb, gg = n // NKV, n % NKV
                pool.wait_ge(max_read, (n + 1) * TB * 2)
                to = [qs[bb][:, :, gg * GH:(gg + 1) * GH, MAXAT + i] for i in range(3)]
                m = mx[n % 2]
                link(g.tensor_copy(to[0], m[:]))
                link(g.tensor_tensor(mr[0][:], m[:], to[0], ALU.subtract))
                link(g.tensor_copy(to[1], mr[0][:]))
                link(g.tensor_tensor(mr[1][:], mr[0][:], to[1], ALU.subtract))
                g.tensor_copy(to[2], mr[1][:]).then_inc(max_ready, 1)

        def pe_l1(pe):
            mm = nc.tensor.matmul
            pe.wait_ge(l1_loaded, 48)
            for t in range(NT):
                pe.wait_ge(xT_ready, 4 * 2 + (t // 2 + 1 if t < 3 else max(t // 2 + 1, t % 7 - 2 if t < 7 else 4)))
                if t >= 7:
                    pe.wait_ge(qkv_ready, t - 6)
                for c in range(KC):
                    last = mm(ps[QKV_BANK[t]][:, 0:QKV], xT[:, c, t * P:(t + 1) * P], wqkv[:, c],
                              start=(c == 0), stop=(c == KC - 1))
                last.then_inc(qkv_made, 1)

            def turn(what):
                n = TURNS.index(what)
                if n >= 3:
                    wait_read(pe, TURNS[LAST_IN_BANK.get(n, n - 1)])
                into = turn_bank(n)
                kind, b, i = what
                if kind == "o":
                    pe.wait_ge(oT_ready, i + 1)
                    for t in range(TB):
                        last = nc.tensor.transpose(into[:, t * P:(t + 1) * P], oT[:, t * P:(t + 1) * P], ident[:])
                elif kind == "k":
                    pe.wait_ge(k_stacked[b], 2 * len(KEY_PARTS))
                    half, t = i // TB, i % TB
                    for k in range(8):
                        last = nc.tensor.transpose(into.bitcast(BF16)[:, k * P:(k + 1) * P],
                                                   ks[b][:, t, half * 4 + k // 2, k % 2, :], identb[:])
                else:
                    b, g = i // NKV, i % NKV
                    pe.wait_ge(q_stacked[b], 3 * TB * (2 if b == 0 and g >= NKV // 2 else 1))
                    if kind == "q2":
                        pe.wait_ge(max_ready, i + 1)
                    for k in range(2):
                        for t in range(TB):
                            last = nc.tensor.transpose(
                                into.bitcast(BF16)[:, (k * TB + t) * P:(k * TB + t + 1) * P],
                                qs[b][:, t, GH * g + 2 * k:GH * g + 2 * k + 2, :].rearrange("p h w -> p (h w)"), identb[:])
                last.then_inc(turned, 1)

            def scores1(c, i):
                n, t = c // TB, c % TB
                b, g = n // NKV, n % NKV
                if 2 * c + i >= 2:
                    pe.wait_ge(max_read, 2 * c + i - 1)
                if t == 0 and i == 0:
                    wait_read(pe, ("q1", 0, n))
                    if g in (0, NKV // 2):
                        wait_read(pe, ("k", b, TB - 1 if g == 0 else 2 * TB - 1))
                for ver in range(2):
                    last = mm(ps[2 * i + ver], qT1[n % 2][:, i, t * P:(t + 1) * P], kT[b][:, g, ver, :],
                              start=True, stop=True)
                last.then_inc(s1_made, 1)

            def scores2(d, i):
                n, kc = d // TB, d % TB
                b, g = n // NKV, n % NKV
                if kc == 0 and i == 0:
                    wait_read(pe, ("q2", 0, n))
                for ver in range(2):
                    k = d * GH + 2 * i + ver
                    if k >= 2:
                        pe.wait_ge(exp_ready, k - 1)
                    mm(ps[4 + ver], kT[b][:, g, ver, kc * P:(kc + 1) * P], qT2[n % 2][:, i, :], start=True,
                       stop=True).then_inc(s2_made, 1)

            def weigh(d):
                n, kc = d // TB, d % TB
                b, g = n // NKV, n % NKV
                pe.wait_ge(exp_ready, (d + 1) * GH)
                if kc == 0 and n:
                    pe.wait_ge(oT_ready, n)
                for j in range(GH):
                    last = mm(ps[6][j * VW:(j + 1) * VW, :], vals[:, b * TB + kc, g, :], pr[d % 3][:, j],
                              start=(kc == 0), stop=(kc == TB - 1), skip_group_check=True)
                last.then_inc(av_done, 1)

            def turn_att(t):
                if t < TB:
                    pe.wait_ge(att_ready, NKV)
                    pe.wait_ge(max_read, 2 * STEPS)
                    if t >= 2:
                        pe.wait_ge(att0_copied, t - 1)
                    into = ps[t % 2]
                else:
                    pe.wait_ge(att_ready, NG)
                    into = ps[t]
                for c in range(KC):
                    last = nc.tensor.transpose(into[:, c * P:(c + 1) * P], xn[:, t, c * P:(c + 1) * P], ident[:])
                last.then_inc(attT_made, 1)

            def project(t):
                if t < TB:
                    pe.wait_ge(att0_copied, t + 1)
                    if t >= 2:
                        pe.wait_ge(y_ready, 2 * NT + t - 1)
                else:
                    pe.wait_ge(att1_copied, t - TB + 1)
                for c in range(KC):
                    last = mm(PROJ_BANK[t][:, 0:D], xT[:, c, t * P:(t + 1) * P], wo1[:, c],
                              start=(c == 0), stop=(c == KC - 1))
                last.then_inc(proj_made, 1)

            for what in FIRST:
                turn(what)
            pe.wait_ge(qkv_ready, NT)
            for c in range(END):
                d = c - LAG
                if c < STEPS:
                    scores1(c, 0)
                if 0 <= d - 2 < STEPS:
                    weigh(d - 2)
                if 0 <= d < STEPS:
                    scores2(d, 0)
                for what in turns_at(c):
                    turn(what)
                if c < STEPS:
                    scores1(c, 1)
                if 0 <= d < STEPS:
                    scores2(d, 1)
                if 0 <= c - PROJ_AT < TB:
                    turn_att(c - PROJ_AT)
                if 1 <= c - PROJ_AT <= TB:
                    project(c - PROJ_AT - 1)
            for t in range(TB, NT):
                turn_att(t)
            for t in range(TB, NT):
                project(t)

        def dve_l1(dve, link, mark, settle, close_y, close_x):
            v = nc.vector
            dve.wait_ge(l1_loaded, 48)

            def take(t):
                dve.wait_ge(qkv_made, t + 1)
                v.tensor_tensor(qkv[:, t, :], ps[QKV_BANK[t]][:, 0:QKV], bqkv[:], ALU.add).then_inc(qkv_ready, 1)

            for t in range(TB):
                take(t)
            dve.wait_ge(qkv_ready, TB)
            keys = slice(NQ * HD, KEND)
            src = qkv[:, 0:TB, keys]
            for i in range(3):
                link(v.tensor_copy(part[0][i][:, :, keys], src))
                if i < 2:
                    link(v.tensor_tensor(rest[0][i][:, :, keys], src, part[0][i][:, :, keys], ALU.subtract))
                    src = rest[0][i][:, :, keys]
            dve.wait_ge(l1_consts, 7)
            dve.wait_ge(ks0_consts, 3)
            for ver in range(2):
                for at_, i in enumerate(KEY_PARTS):
                    stack_keys(v, 0, ver, at_, i).then_inc(k_stacked[0], 1)

            def query_step(k):
                i, cols = k // 2, slice(0, NQ // 2 * HD)
                src = qkv[:, 0:TB, cols] if i == 0 else rest[0][i - 1][:, :, cols]
                if k % 2 == 0:
                    v.tensor_copy(part[0][i][:, :, cols], src).then_inc(part_ready[0], 1)
                    dve.wait_ge(part_ready[0], i + 1)
                else:
                    link(v.tensor_tensor(rest[0][i][:, :, cols], src, part[0][i][:, :, cols], ALU.subtract))

            for k in range(5):
                query_step(k)
                if k < NT - TB:
                    take(TB + k)
            dve.wait_ge(qkv_ready, NT)
            mark(v.tensor_copy(vals[:, :, :, 0:HD], qkv[:, :, KEND:QKV].rearrange("p t (g d) -> p t g d", d=HD)))
            settle()

            def maximum(c, i):
                n, t = c // TB, c % TB
                dve.wait_ge(s1_made, 2 * c + i + 1)
                if t == 0 and n >= 2:
                    dve.wait_ge(max_ready, n - 1)
                v.tensor_reduce(mx[n % 2][:, t, 2 * i:2 * i + 2], psum[:, i * 1024:(i + 1) * 1024].rearrange(
                    "p (h n) -> p h n", h=2), AX.X, ALU.max, negate=True).then_inc(max_read, 1)

            def outputs(n):
                b, g = n // NKV, n % NKV
                dve.wait_ge(turned, turn_no(("o", 0, n)))
                o = ps[7].rearrange("p (t h w) -> p t h w", t=TB, h=GH)
                link(v.reciprocal(dn[:], o[:, :, :, HD]))
                for t in range(TB):
                    ins = v.tensor_tensor(
                        xn[:, b * TB + t, g * GH * HD:(g + 1) * GH * HD].rearrange("p (h d) -> p h d", d=HD),
                        o[:, t, :, 0:HD], dn[:, t, :].unsqueeze(2).to_broadcast([P, GH, HD]), ALU.mult)
                    if t < TB - 1:
                        mark(ins)
                    else:
                        ins.then_inc(att_ready, 1)

            def l1_y(t):
                dve.wait_ge(proj_made, t + 1)
                v.tensor_tensor(y[:, t, :], PROJ_BANK[t][:, 0:D], bo1[:], ALU.add).then_inc(y_ready, 1)

            def copy_att(t):
                dve.wait_ge(attT_made, t + 1)
                v.tensor_copy(xT[:, :, t * P:(t + 1) * P],
                              ps[t % 2][:, 0:D].rearrange("p (c n) -> p c n", c=KC)).then_inc(att0_copied, 1)

            for c in range(END):
                if c < STEPS:
                    maximum(c, 0)
                if c % TB == 0 and c >= 12 and (c - 12) // TB < NG:
                    n = (c - 12) // TB
                    dve.wait_ge(av_done, (n + 1) * TB)
                    v.tensor_copy(oT[:], ps[6]).then_inc(oT_ready, 1)
                if c < STEPS:
                    maximum(c, 1)
                if c % TB == 2 and 0 <= (c - 14) // TB < NG:
                    outputs((c - 14) // TB)
                if 0 <= c - PROJ_AT < TB:
                    copy_att(c - PROJ_AT)
                if 1 <= c - PROJ_AT <= TB:
                    l1_y(c - PROJ_AT - 1)
                if c == PROJ_AT + TB:
                    close_y(2, 0, lambda t: None)
            close_x(2, 0)
            return l1_y

        @block.sync
        def _(eng):
            sync_program(eng)

        @block.gpsimd
        def _(eng):
            gpsimd_program(eng)

        @block.vector
        def _(eng):
            vector_program(eng)

        @block.scalar
        def _(eng):
            scalar_program(eng)

        @block.tensor
        def _(eng):
            tensor_program(eng)


_INS = ['L0_attn_hidden_states', 'L0_attn_Wq', 'L0_attn_Wk', 'L0_attn_Wv', 'L0_attn_Wo', 'L0_attn_bo',
        'L0_ffn_router_w', 'L0_ffn_gate_w', 'L0_ffn_up_w', 'L0_ffn_down_w', 'L0_ffn_shared_gate_w',
        'L0_ffn_shared_up_w', 'L0_ffn_shared_down_w', 'L1_attn_Wqkv', 'L1_attn_bqkv', 'L1_attn_Wo', 'L1_attn_bo',
        'L1_ffn_router_w', 'L1_ffn_gate_w', 'L1_ffn_up_w', 'L1_ffn_down_w', 'L1_ffn_shared_gate_w',
        'L1_ffn_shared_up_w', 'L1_ffn_shared_down_w']


def kernel(**inputs):
    import numpy as np
    import concourse.bacc as bacc
    from concourse.bass_utils import run_bass_kernel_spmd

    nc = bacc.Bacc("TRN2", target_bir_lowering=False, num_devices=1)
    arrays, args = {}, {}
    for name in _INS:
        arr = np.ascontiguousarray(inputs[name])
        arrays[f"in_{name}"] = arr
        args[name] = nc.dram_tensor(f"in_{name}", arr.shape, mybir.dt.from_np(arr.dtype), kind="ExternalInput").ap()
    out = nc.dram_tensor("out_x", (B, S, D), F32, kind="ExternalOutput").ap()
    build(nc, args, out)
    r = run_bass_kernel_spmd(nc, [arrays], core_ids=[0])
    return r.results[0]["out_x"]
```
